# Optimizing a Trainium2 kernel written in Bass

```python
import numpy as np
import jax
import jax.numpy as jnp

def _softmax(x, axis=-1):
    return jax.nn.softmax(x, axis=axis)

def _gelu(x):
    return jax.nn.gelu(x, approximate=True)

def _silu(x):
    return jax.nn.silu(x)

def _sigmoid(x):
    return jax.nn.sigmoid(x)

def _layernorm(x, axis=-1, eps=1e-05):
    m = jnp.mean(x, axis=axis, keepdims=True)
    v = jnp.var(x, axis=axis, keepdims=True)
    return (x - m) / jnp.sqrt(v + eps)

def _scatter_add(tgt, idx, src, axis=0):
    return tgt.at[idx].add(src)

def _segment_sum(src, seg, n):
    return jax.ops.segment_sum(src, seg, n)
kernel_name = 'mk_early_fusion_embed_d1_tok_img512_r4_fb93b4'

def setup_inputs(seed: int=0):
    np.random.seed(seed)
    _w = jnp.asarray

    def _rec_inputs():
        import jax
        import jax.numpy as jnp
        _rk = jax.random.key(seed)
        x = -0.000392918 + 0.999932 * jax.random.normal(jax.random.fold_in(_rk, 1), (16, 1, 128, 128), jnp.float32)
        x_txt = jax.random.randint(jax.random.fold_in(_rk, 51), (16, 77), 0, 24997, jnp.int32)
        mask_BS_f1_0 = jnp.where(jnp.ones((16, 77), dtype=bool), 1.0, 0.0).astype(jnp.float32)
        return (x, x_txt, mask_BS_f1_0)
    x, x_txt, mask_BS_f1_0 = _rec_inputs()

    def _L0_tok_setup():
        import math
        import jax, jax.numpy as jnp
        import numpy as np
        PW = PH = 16
        EMB = 128
        HID = 128
        B, H, W = (64, 128, 128)
        L = H // PW * (W // PH)
        SIGMA_ZERO = 0.1

        def _f_noise(x):
            return jnp.sign(x) * jnp.sqrt(jnp.abs(x))

        def _noisy_linear(x, w, b, sw, sb, eps_in, eps_out):
            ei = _f_noise(eps_in)
            eo = _f_noise(eps_out)
            w_n = w + sw * (eo[:, None] * ei[None, :])
            b_n = b + sb * eo
            return x @ w_n.T + b_n

        def _unfold_patches(x):
            b = x.shape[0]
            p = x.reshape(b, H // PW, PW, W // PH, PH)
            p = p.transpose(0, 1, 3, 2, 4)
            return p.reshape(b, L, PW * PH)

        def _pos_encoding(x):
            pos = jnp.arange(L, dtype=jnp.float32)[:, None]
            div = jnp.exp(jnp.arange(0, EMB, 2, dtype=jnp.float32) * (-math.log(10000.0) / EMB))
            ang = pos * div
            pe = jnp.stack([jnp.sin(ang), jnp.cos(ang)], axis=-1).reshape(L, EMB)
            return x + pe[None, :, :]
        key = jax.random.key(seed)
        ks = jax.random.split(key, 12)
        in_f = PW * PH
        sig = SIGMA_ZERO / math.sqrt(in_f)
        bnd1 = 1.0 / math.sqrt(in_f)
        bnd3 = 1.0 / math.sqrt(HID)
        u = lambda k, shape, bnd: jax.random.uniform(k, shape, jnp.float32, -bnd, bnd)
        return {'inputs': jax.random.normal(ks[0], (B, 1, H, W), jnp.float32), 'W1_w': u(ks[1], (HID, in_f), bnd1), 'W1_b': u(ks[2], (HID,), bnd1), 'W1_sw': jnp.full((HID, in_f), sig, jnp.float32), 'W1_sb': jnp.full((HID,), sig, jnp.float32), 'W2_w': u(ks[3], (HID, in_f), bnd1), 'W2_b': u(ks[4], (HID,), bnd1), 'W2_sw': jnp.full((HID, in_f), sig, jnp.float32), 'W2_sb': jnp.full((HID,), sig, jnp.float32), 'W3_w': u(ks[5], (EMB, HID), bnd3), 'W3_b': u(ks[6], (EMB,), bnd3), 'eps_in1': jax.random.normal(ks[7], (in_f,), jnp.float32), 'eps_out1': jax.random.normal(ks[8], (HID,), jnp.float32), 'eps_in2': jax.random.normal(ks[9], (in_f,), jnp.float32), 'eps_out2': jax.random.normal(ks[10], (HID,), jnp.float32)}
    _L0_tok_all = _L0_tok_setup()
    _L0_tok_in = {k: v for k, v in _L0_tok_all.items() if k in ('W1_w', 'W1_b', 'W1_sw', 'W1_sb', 'W2_w', 'W2_b', 'W2_sw', 'W2_sb', 'W3_w', 'W3_b', 'eps_in1', 'eps_out1', 'eps_in2', 'eps_out2')}
    del _L0_tok_all

    def _L0_txt_setup():
        import jax, jax.numpy as jnp
        import numpy as np
        B, S, D, H, L, F, V = (128, 200, 128, 8, 4, 512, 100001)
        HD = D // H

        def layer_norm(x, g, b, eps=1e-05):
            mu = jnp.mean(x, axis=-1, keepdims=True)
            var = jnp.mean((x - mu) ** 2, axis=-1, keepdims=True)
            return (x - mu) / jnp.sqrt(var + eps) * g + b
        key = jax.random.key(seed)
        ks = jax.random.split(key, 12)
        r = lambda k, shape: jax.random.normal(k, shape, jnp.float32) * 0.02
        item_seq = jax.random.randint(ks[0], (B, S), 1, V)
        attention_mask = jnp.ones((B, S), jnp.float32)
        item_emb = r(ks[1], (V, D)).at[0].set(0.0)
        pos_emb = r(ks[2], (S, D))
        return {'item_seq': item_seq, 'attention_mask': attention_mask, 'item_emb': item_emb, 'pos_emb': pos_emb, 'Wq': r(ks[3], (L, D, D)), 'bq': jnp.zeros((L, D)), 'Wk': r(ks[4], (L, D, D)), 'bk': jnp.zeros((L, D)), 'Wv': r(ks[5], (L, D, D)), 'bv': jnp.zeros((L, D)), 'Wo': r(ks[6], (L, D, D)), 'bo': jnp.zeros((L, D)), 'ln1_g': jnp.ones((L, D)), 'ln1_b': jnp.zeros((L, D)), 'ln2_g': jnp.ones((L, D)), 'ln2_b': jnp.zeros((L, D)), 'W1': r(ks[7], (L, D, F)), 'b1': jnp.zeros((L, F)), 'W2': r(ks[8], (L, F, D)), 'b2': jnp.zeros((L, D)), 'lnf_g': jnp.ones((D,)), 'lnf_b': jnp.zeros((D,))}
    _L0_txt_all = _L0_txt_setup()
    _L0_txt_in = {k: v for k, v in _L0_txt_all.items() if k in ('item_emb', 'pos_emb', 'Wq', 'bq', 'Wk', 'bk', 'Wv', 'bv', 'Wo', 'bo', 'ln1_g', 'ln1_b', 'ln2_g', 'ln2_b', 'W1', 'b1', 'W2', 'b2', 'lnf_g', 'lnf_b')}
    del _L0_txt_all

    def _L0_attn_setup():
        import jax, jax.numpy as jnp
        import numpy as np
        import math
        B, L, D = (4, 512, 128)
        H = 8
        HD = D // H
        K1 = 64
        K2 = 64

        def semi_local_mask(seq_len):
            i = jnp.arange(seq_len)[:, None]
            j = jnp.arange(seq_len)[None, :]
            band = (i + j >= seq_len - K1) & (i + j <= seq_len)
            glob = (j <= K2) & (j <= seq_len - i)
            causal = j <= i
            return (band | glob) & causal
        key = jax.random.key(seed)
        ks = jax.random.split(key, 8)

        def xavier(k, shape):
            fan_in, fan_out = (shape[1], shape[0])
            lim = math.sqrt(6.0 / (fan_in + fan_out))
            return jax.random.uniform(k, shape, jnp.float32, -lim, lim)
        x = jax.random.normal(ks[0], (B, L, D), jnp.float32)
        w_qkv = xavier(ks[1], (3 * D, D))
        b_qkv = jnp.zeros((3 * D,), jnp.float32)
        w_u = xavier(ks[2], (D, D))
        b_u = jnp.zeros((D,), jnp.float32)
        w_out = xavier(ks[3], (D, D))
        b_out = jnp.zeros((D,), jnp.float32)
        return {'x': x, 'w_qkv': w_qkv, 'b_qkv': b_qkv, 'w_u': w_u, 'b_u': b_u, 'w_out': w_out, 'b_out': b_out}
    _L0_attn_all = _L0_attn_setup()
    _L0_attn_in = {k: v for k, v in _L0_attn_all.items() if k in ('w_qkv', 'b_qkv', 'w_u', 'b_u', 'w_out', 'b_out')}
    del _L0_attn_all

    def _L0_ffn_setup():
        import jax, jax.numpy as jnp
        import numpy as np
        D_MODEL = 128
        D_FF = 128
        N_EXPERTS = 16
        TOP_K = 3
        BATCH, SEQ = (1, 512)

        def _swiglu(combined):
            gate, up = jnp.split(combined, 2, axis=-1)
            return jax.nn.silu(gate) * up
        key = jax.random.key(seed)
        ks = jax.random.split(key, 6)
        x = jax.random.normal(ks[0], (BATCH, SEQ, D_MODEL), dtype=jnp.float32)
        gate_w = 0.01 * jax.random.normal(ks[1], (N_EXPERTS, D_MODEL), dtype=jnp.float32)
        expert_bias = jnp.zeros((N_EXPERTS,), dtype=jnp.float32)
        shared_gate_up = 0.02 * jax.random.normal(ks[2], (2 * D_FF, D_MODEL), dtype=jnp.float32)
        shared_down = 0.02 * jax.random.normal(ks[3], (D_MODEL, D_FF), dtype=jnp.float32)
        expert_gate_up = 0.02 * jax.random.normal(ks[4], (N_EXPERTS, 2 * D_FF, D_MODEL), dtype=jnp.float32)
        expert_down = 0.02 * jax.random.normal(ks[5], (N_EXPERTS, D_MODEL, D_FF), dtype=jnp.float32)
        return {'x': x, 'gate_w': gate_w, 'expert_bias': expert_bias, 'shared_gate_up': shared_gate_up, 'shared_down': shared_down, 'expert_gate_up': expert_gate_up, 'expert_down': expert_down}
    _L0_ffn_all = _L0_ffn_setup()
    _L0_ffn_in = {k: v for k, v in _L0_ffn_all.items() if k in ('gate_w', 'expert_bias', 'shared_gate_up', 'shared_down', 'expert_gate_up', 'expert_down')}
    del _L0_ffn_all
    return {'x': x, 'x_txt': x_txt, 'mask_BS_f1_0': mask_BS_f1_0, 'L0_tok_W1_w': _L0_tok_in['W1_w'], 'L0_tok_W1_b': _L0_tok_in['W1_b'], 'L0_tok_W1_sw': _L0_tok_in['W1_sw'], 'L0_tok_W1_sb': _L0_tok_in['W1_sb'], 'L0_tok_W2_w': _L0_tok_in['W2_w'], 'L0_tok_W2_b': _L0_tok_in['W2_b'], 'L0_tok_W2_sw': _L0_tok_in['W2_sw'], 'L0_tok_W2_sb': _L0_tok_in['W2_sb'], 'L0_tok_W3_w': _L0_tok_in['W3_w'], 'L0_tok_W3_b': _L0_tok_in['W3_b'], 'L0_tok_eps_in1': _L0_tok_in['eps_in1'], 'L0_tok_eps_out1': _L0_tok_in['eps_out1'], 'L0_tok_eps_in2': _L0_tok_in['eps_in2'], 'L0_tok_eps_out2': _L0_tok_in['eps_out2'], 'L0_txt_item_emb': _L0_txt_in['item_emb'], 'L0_txt_pos_emb': _L0_txt_in['pos_emb'], 'L0_txt_Wq': _L0_txt_in['Wq'], 'L0_txt_bq': _L0_txt_in['bq'], 'L0_txt_Wk': _L0_txt_in['Wk'], 'L0_txt_bk': _L0_txt_in['bk'], 'L0_txt_Wv': _L0_txt_in['Wv'], 'L0_txt_bv': _L0_txt_in['bv'], 'L0_txt_Wo': _L0_txt_in['Wo'], 'L0_txt_bo': _L0_txt_in['bo'], 'L0_txt_ln1_g': _L0_txt_in['ln1_g'], 'L0_txt_ln1_b': _L0_txt_in['ln1_b'], 'L0_txt_ln2_g': _L0_txt_in['ln2_g'], 'L0_txt_ln2_b': _L0_txt_in['ln2_b'], 'L0_txt_W1': _L0_txt_in['W1'], 'L0_txt_b1': _L0_txt_in['b1'], 'L0_txt_W2': _L0_txt_in['W2'], 'L0_txt_b2': _L0_txt_in['b2'], 'L0_txt_lnf_g': _L0_txt_in['lnf_g'], 'L0_txt_lnf_b': _L0_txt_in['lnf_b'], 'L0_attn_w_qkv': _L0_attn_in['w_qkv'], 'L0_attn_b_qkv': _L0_attn_in['b_qkv'], 'L0_attn_w_u': _L0_attn_in['w_u'], 'L0_attn_b_u': _L0_attn_in['b_u'], 'L0_attn_w_out': _L0_attn_in['w_out'], 'L0_attn_b_out': _L0_attn_in['b_out'], 'L0_ffn_gate_w': _L0_ffn_in['gate_w'], 'L0_ffn_expert_bias': _L0_ffn_in['expert_bias'], 'L0_ffn_shared_gate_up': _L0_ffn_in['shared_gate_up'], 'L0_ffn_shared_down': _L0_ffn_in['shared_down'], 'L0_ffn_expert_gate_up': _L0_ffn_in['expert_gate_up'], 'L0_ffn_expert_down': _L0_ffn_in['expert_down']}

def reference(x, x_txt, mask_BS_f1_0, L0_tok_W1_w, L0_tok_W1_b, L0_tok_W1_sw, L0_tok_W1_sb, L0_tok_W2_w, L0_tok_W2_b, L0_tok_W2_sw, L0_tok_W2_sb, L0_tok_W3_w, L0_tok_W3_b, L0_tok_eps_in1, L0_tok_eps_out1, L0_tok_eps_in2, L0_tok_eps_out2, L0_txt_item_emb, L0_txt_pos_emb, L0_txt_Wq, L0_txt_bq, L0_txt_Wk, L0_txt_bk, L0_txt_Wv, L0_txt_bv, L0_txt_Wo, L0_txt_bo, L0_txt_ln1_g, L0_txt_ln1_b, L0_txt_ln2_g, L0_txt_ln2_b, L0_txt_W1, L0_txt_b1, L0_txt_W2, L0_txt_b2, L0_txt_lnf_g, L0_txt_lnf_b, L0_attn_w_qkv, L0_attn_b_qkv, L0_attn_w_u, L0_attn_b_u, L0_attn_w_out, L0_attn_b_out, L0_ffn_gate_w, L0_ffn_expert_bias, L0_ffn_shared_gate_up, L0_ffn_shared_down, L0_ffn_expert_gate_up, L0_ffn_expert_down):
    import jax
    import jax.numpy as jnp

    def _L0_tok_ref(inputs, W1_w, W1_b, W1_sw, W1_sb, W2_w, W2_b, W2_sw, W2_sb, W3_w, W3_b, eps_in1, eps_out1, eps_in2, eps_out2):
        import math
        import jax, jax.numpy as jnp
        import numpy as np
        PW = PH = 16
        EMB = 128
        HID = 128
        B, H, W = (64, 128, 128)
        L = H // PW * (W // PH)
        SIGMA_ZERO = 0.1

        def _f_noise(x):
            return jnp.sign(x) * jnp.sqrt(jnp.abs(x))

        def _noisy_linear(x, w, b, sw, sb, eps_in, eps_out):
            ei = _f_noise(eps_in)
            eo = _f_noise(eps_out)
            w_n = w + sw * (eo[:, None] * ei[None, :])
            b_n = b + sb * eo
            return x @ w_n.T + b_n

        def _unfold_patches(x):
            b = x.shape[0]
            p = x.reshape(b, H // PW, PW, W // PH, PH)
            p = p.transpose(0, 1, 3, 2, 4)
            return p.reshape(b, L, PW * PH)

        def _pos_encoding(x):
            pos = jnp.arange(L, dtype=jnp.float32)[:, None]
            div = jnp.exp(jnp.arange(0, EMB, 2, dtype=jnp.float32) * (-math.log(10000.0) / EMB))
            ang = pos * div
            pe = jnp.stack([jnp.sin(ang), jnp.cos(ang)], axis=-1).reshape(L, EMB)
            return x + pe[None, :, :]
        x = _unfold_patches(inputs)
        g = _noisy_linear(x, W1_w, W1_b, W1_sw, W1_sb, eps_in1, eps_out1)
        x_gate = g * jnp.tanh(jax.nn.softplus(g))
        x_inner = _noisy_linear(x, W2_w, W2_b, W2_sw, W2_sb, eps_in2, eps_out2)
        x = x_gate * x_inner
        x = x @ W3_w.T + W3_b
        return _pos_encoding(x)

    def _L0_txt_ref(item_seq, attention_mask, item_emb, pos_emb, Wq, bq, Wk, bk, Wv, bv, Wo, bo, ln1_g, ln1_b, ln2_g, ln2_b, W1, b1, W2, b2, lnf_g, lnf_b):
        import jax, jax.numpy as jnp
        import numpy as np
        B, S, D, H, L, F, V = (128, 200, 128, 8, 4, 512, 100001)
        HD = D // H

        def layer_norm(x, g, b, eps=1e-05):
            mu = jnp.mean(x, axis=-1, keepdims=True)
            var = jnp.mean((x - mu) ** 2, axis=-1, keepdims=True)
            return (x - mu) / jnp.sqrt(var + eps) * g + b
        b, s = item_seq.shape
        x = item_emb[item_seq] + pos_emb[None, :s, :]
        causal = jnp.triu(jnp.ones((s, s), bool), 1)
        pad = attention_mask[:, None, None, :] == 0
        mask = causal[None, None, :, :] | pad
        scale = 1.0 / np.sqrt(HD)
        for l in range(L):
            h = layer_norm(x, ln1_g[l], ln1_b[l])
            q = (h @ Wq[l] + bq[l]).reshape(b, s, H, HD)
            k = (h @ Wk[l] + bk[l]).reshape(b, s, H, HD)
            v = (h @ Wv[l] + bv[l]).reshape(b, s, H, HD)
            scores = jnp.einsum('bqhd,bkhd->bhqk', q, k) * scale
            scores = jnp.where(mask, -jnp.inf, scores)
            attn = jax.nn.softmax(scores, axis=-1)
            ctx = jnp.einsum('bhqk,bkhd->bqhd', attn, v).reshape(b, s, D)
            x = x + ctx @ Wo[l] + bo[l]
            h2 = layer_norm(x, ln2_g[l], ln2_b[l])
            x = x + jax.nn.gelu(h2 @ W1[l] + b1[l], approximate=False) @ W2[l] + b2[l]
        return layer_norm(x, lnf_g, lnf_b)

    def _L0_attn_ref(x, w_qkv, b_qkv, w_u, b_u, w_out, b_out):
        import jax, jax.numpy as jnp
        import numpy as np
        import math
        B, L, D = (4, 512, 128)
        H = 8
        HD = D // H
        K1 = 64
        K2 = 64

        def semi_local_mask(seq_len):
            i = jnp.arange(seq_len)[:, None]
            j = jnp.arange(seq_len)[None, :]
            band = (i + j >= seq_len - K1) & (i + j <= seq_len)
            glob = (j <= K2) & (j <= seq_len - i)
            causal = j <= i
            return (band | glob) & causal
        Bsz, Lq, Dm = x.shape
        qkv = (x @ w_qkv.T + b_qkv).reshape(Bsz, Lq, 3, H, HD)
        q, k, v = jnp.moveaxis(qkv, 2, 0)
        q = jnp.transpose(q, (0, 2, 1, 3))
        k = jnp.transpose(k, (0, 2, 1, 3))
        v = jnp.transpose(v, (0, 2, 1, 3))
        u = x @ w_u.T + b_u
        scale = 1.0 / math.sqrt(HD)
        scores = jnp.einsum('bhqd,bhkd->bhqk', q * scale, k)
        mask = semi_local_mask(Lq)
        scores = jnp.where(mask[None, None], scores, -jnp.inf)
        attn = jax.nn.softmax(scores, axis=-1)
        out = jnp.einsum('bhqk,bhkd->bhqd', attn, v)
        out = jnp.transpose(out, (0, 2, 1, 3)).reshape(Bsz, Lq, Dm)
        out = jax.nn.silu(out) * u
        return out @ w_out.T + b_out

    def _L0_ffn_ref(x, gate_w, expert_bias, shared_gate_up, shared_down, expert_gate_up, expert_down):
        import jax, jax.numpy as jnp
        import numpy as np
        D_MODEL = 128
        D_FF = 128
        N_EXPERTS = 16
        TOP_K = 3
        BATCH, SEQ = (1, 512)

        def _swiglu(combined):
            gate, up = jnp.split(combined, 2, axis=-1)
            return jax.nn.silu(gate) * up
        B, S, D = x.shape
        xf = x.reshape(-1, D)
        shared_out = _swiglu(xf @ shared_gate_up.T) @ shared_down.T
        logits = xf @ gate_w.T
        affinity = jax.nn.sigmoid(logits)
        routing_scores = affinity + expert_bias
        _, sel = jax.lax.top_k(routing_scores, TOP_K)
        sel_aff = jnp.take_along_axis(affinity, sel, axis=1)
        gating = sel_aff / (sel_aff.sum(axis=-1, keepdims=True) + 1e-09)
        combined = jnp.einsum('td,efd->tef', xf, expert_gate_up)
        hidden = _swiglu(combined)
        expert_out = jnp.einsum('tef,edf->ted', hidden, expert_down)
        sel_out = jnp.take_along_axis(expert_out, sel[:, :, None], axis=1)
        routed_out = jnp.einsum('tk,tkd->td', gating, sel_out)
        out = shared_out + routed_out
        return out.reshape(B, S, D)
    h = _L0_tok_ref(x, L0_tok_W1_w, L0_tok_W1_b, L0_tok_W1_sw, L0_tok_W1_sb, L0_tok_W2_w, L0_tok_W2_b, L0_tok_W2_sw, L0_tok_W2_sb, L0_tok_W3_w, L0_tok_W3_b, L0_tok_eps_in1, L0_tok_eps_out1, L0_tok_eps_in2, L0_tok_eps_out2)
    h = jnp.concatenate([h, _L0_txt_ref(x_txt, mask_BS_f1_0, L0_txt_item_emb, L0_txt_pos_emb, L0_txt_Wq, L0_txt_bq, L0_txt_Wk, L0_txt_bk, L0_txt_Wv, L0_txt_bv, L0_txt_Wo, L0_txt_bo, L0_txt_ln1_g, L0_txt_ln1_b, L0_txt_ln2_g, L0_txt_ln2_b, L0_txt_W1, L0_txt_b1, L0_txt_W2, L0_txt_b2, L0_txt_lnf_g, L0_txt_lnf_b)], axis=1)
    h = h + _L0_attn_ref(_layernorm(h, axis=-1), L0_attn_w_qkv, L0_attn_b_qkv, L0_attn_w_u, L0_attn_b_u, L0_attn_w_out, L0_attn_b_out)
    h = h + _L0_ffn_ref(_layernorm(h, axis=-1), L0_ffn_gate_w, L0_ffn_expert_bias, L0_ffn_shared_gate_up, L0_ffn_shared_down, L0_ffn_expert_gate_up, L0_ffn_expert_down)
    return h

_drawn_inputs = setup_inputs


def setup_inputs(seed=0):
    import zlib

    import numpy as np

    out = dict(_drawn_inputs(seed))
    spreads = {'L0_tok_W1_sw': (0.0062500000931322575, 0.6),
     'L0_tok_W1_sb': (0.0062500000931322575, 0.6),
     'L0_tok_W2_sw': (0.0062500000931322575, 0.6),
     'L0_tok_W2_sb': (0.0062500000931322575, 0.6),
     'L0_txt_bq': (0.0, 0.8),
     'L0_txt_bk': (0.0, 0.8),
     'L0_txt_bv': (0.0, 0.1),
     'L0_txt_bo': (0.0, 0.1),
     'L0_txt_ln1_g': (1.0, 0.2),
     'L0_txt_ln1_b': (0.0, 0.295),
     'L0_txt_ln2_g': (1.0, 0.2),
     'L0_txt_ln2_b': (0.0, 0.275),
     'L0_txt_b1': (0.0, 0.1),
     'L0_txt_b2': (0.0, 0.1),
     'L0_txt_lnf_g': (1.0, 0.2),
     'L0_txt_lnf_b': (0.0, 0.1),
     'L0_attn_b_qkv': (0.0, 0.1),
     'L0_attn_b_u': (0.0, 0.1),
     'L0_attn_b_out': (0.0, 0.1),
     'L0_ffn_expert_bias': (0.0, 0.8)}
    factors = {'L0_tok_W1_b': 8.0,
     'L0_tok_W2_b': 8.0,
     'L0_tok_eps_in1': 3.54,
     'L0_tok_eps_out1': 3.384,
     'L0_tok_eps_in2': 3.387,
     'L0_tok_eps_out2': 3.229,
     'L0_txt_Wq': 8.0,
     'L0_txt_Wk': 8.0,
     'L0_ffn_gate_w': 8.0,
     'L0_ffn_shared_gate_up': 8.0,
     'L0_ffn_shared_down': 8.0,
     'L0_ffn_expert_gate_up': 8.0,
     'L0_ffn_expert_down': 8.0}
    for name, (base, spread) in spreads.items():
        noise = np.random.default_rng([zlib.crc32(name.encode()), seed]).standard_normal(out[name].shape)
        drawn = base * np.exp(spread * noise) if base else spread * noise
        out[name] = jnp.asarray(drawn.astype(out[name].dtype))
    for name, factor in factors.items():
        out[name] = (out[name] * factor).astype(out[name].dtype)
    return out
```

```python
from contextlib import ExitStack

import numpy as np

import concourse.bass as bass
from concourse import mybir

F32 = mybir.dt.float32
BF16 = mybir.dt.bfloat16
I32 = mybir.dt.int32
U32 = mybir.dt.uint32
ALU = mybir.AluOpType
ACT = mybir.ActivationFunctionType
AX = mybir.AxisListType

P = 128
D = 128
B = 16
NH, HD = 8, 16
VW = HD + 1
LAYERS = 4
S_IMG, S_TXT = 64, 77
S_ALL = S_IMG + S_TXT
K_JOINT = S_ALL // 2 + 1
IMG_TILES = B * S_IMG // P
TXT_TOKENS = B * S_TXT
TXT_TILES = -(-TXT_TOKENS // P)
TILES = IMG_TILES + TXT_TILES
LAST_ROWS = TXT_TOKENS - (TXT_TILES - 1) * P
COLS = TILES * P
T0 = IMG_TILES * P
FF = 4
E = 16
CHUNK_TILES = 3
CHUNK = CHUNK_TILES * P
CHUNKS = TILES // CHUNK_TILES
EPS = 1e-5
FAR = -1e30
Q_SCALE = 1.0 / np.sqrt(HD)
EXP_CAP = 30.0


def groups_of(first, count):
    return [(t, min(4, first + count - t)) for t in range(first, first + count, 4)]


TXT_GROUPS = groups_of(IMG_TILES, TXT_TILES)
ALL_GROUPS = groups_of(0, TILES)
NG = len(TXT_GROUPS)
NA = len(ALL_GROUPS)

C_ID, C_CAUSAL, C_JOINT, C_MASKL, C_HEAD, C_POS = 0, 128, 205, 276, 353, 361
C_IOTA = 489
C_ALL = 505
PAD_ROW = 96
V_G1, V_B1, V_BQ, V_BK, V_G2, V_B2, V_BF = 0, 1, 2, 3, 4, 5, 6
V_ALL = 10
R_BV, R_BO, R_B2 = 0, 128, 256
JV_BQ, JV_BK, JV_BU = 0, 1, 2
JR_BV, JR_BO, JR_W3B, JR_FG, JR_FB, JR_EB = 0, 128, 256, 384, 512, 640
JR_ALL = 656


class Unit:

    def __init__(self, nq, nk, qcol, kslot, vals, mask_l, mask_r, c_off, kexp_no):
        self.nq, self.nk, self.qcol, self.kslot, self.vals = nq, nk, qcol, kslot, vals
        self.mask_l, self.mask_r, self.c_off, self.kexp_no = mask_l, mask_r, c_off, kexp_no


class Passed:

    def __init__(self, l):
        self.l = l

    def __call__(self, k):
        return self.l * B + k

    def group(self, g):
        return self.l * (B // 4) + g


class Norms:

    def __init__(self, groups, norms):
        self.groups, self.norms = groups, norms

    def __call__(self, k):
        return self.groups + k

    def norm(self):
        return self.norms + 1


def build(nc, a, out):
    ctx = ExitStack()
    with ctx:
        def sb(name, shape, dt=F32):
            return ctx.enter_context(nc.sbuf_tensor(name, shape, dt))

        def sem(name):
            return ctx.enter_context(nc.semaphore(name))

        const = sb("const", [P, C_ALL])
        ident = const[:, C_ID:C_ID + P]
        ident_bf = sb("ident_bf", [P, P], BF16)
        mask_l_bf = sb("mask_l_bf", [P, S_TXT], BF16)
        txt_mask = sb("txt_mask", [P, B, S_TXT], BF16)
        joint_mask = sb("joint_mask", [P, K_JOINT], BF16)
        pad_col = sb("pad_col", [P, B])
        pad_col1 = sb("pad_col1", [P, B])
        head_mask = const[:, C_HEAD:C_HEAD + NH]
        eps_t = sb("eps_t", [P, TILES])
        half_t = sb("half_t", [P, TILES])
        x_tok = sb("x_tok", [P, TILES, D])
        x_norm = sb("x_norm", [P, TILES, D])
        hT = sb("hT", [P, COLS])
        qT = sb("qT", [P, COLS])
        kT = sb("kT", [P, COLS])
        uT = sb("uT", [P, COLS])
        ctxT = sb("ctxT", [P, COLS])
        stats = sb("stats", [P, TILES, 6])
        mv = sb("mv", [P, TILES, 2])
        wait_carrier = sb("wait_carrier", [1, 1])
        veps = sb("veps", [P, TILES])
        rstd = sb("rstd", [P, TILES])
        k_exp = sb("k_exp", [P, 2, NH * S_TXT])
        v_txt = sb("v_txt", [P, B, NH, VW])
        v_joint = sb("v_joint", [P, B, NH, VW])
        probs = sb("probs", [P, 2, 2, 4 * S_TXT])
        probsT = sb("probsT", [P, 2, 2, 4 * S_TXT])
        pad_in = probsT[:].rearrange("p a b k -> p (a b k)")
        neg_max = sb("neg_max", [P, 2, NH], BF16)
        r_den = sb("r_den", [P, NH])
        ctx_sb_t = sb("ctx_sb_t", [P, 2, D])
        gelu_t = sb("gelu_t", [P, 2, FF, 512])
        w_qkv_t = sb("w_qkv_t", [P, 3 * D])
        w_o_t = sb("w_o_t", [P, D])
        w_1_t = sb("w_1_t", [P, FF * D])
        w_2_t = sb("w_2_t", [P, FF, D])
        vec = sb("vec", [P, V_ALL])
        row = sb("row", [P, 3 * D])
        jw = sb("jw", [P, 5 * D])
        jvec = sb("jvec", [P, 3])
        jrow = sb("jrow", [P, JR_ALL])
        idx = sb("idx", [P, TXT_TILES], I32)
        patches = sb("patches", [P, 2, T0])
        tok_w = sb("tok_w", [P, 2, 2, D])
        tok_sw = sb("tok_sw", [P, 2, 2, D])
        tok_w3 = sb("tok_w3", [P, D])
        tok_b = sb("tok_b", [P, 4])
        noise = sb("noise", [P, 6 + 2 * D])
        noise_abs = sb("noise_abs", [P, 6 + 2 * D])
        noise_root = sb("noise_root", [P, 6 + 2 * D])
        noise_sign = sb("noise_sign", [P, 6 + 2 * D])
        tok_bn = sb("tok_bn", [P, 2])
        pos_b = sb("pos_b", [P, D])
        w_gu = sb("w_gu", [P, E + 1, 2 * D])
        w_dn = sb("w_dn", [P, E + 1, D])
        w_gate = sb("w_gate", [P, E])
        select = sb("select", [P, E, P])
        aff = sb("aff", [P, TILES, E])
        route = sb("route", [P, TILES, E])
        route2 = sb("route2", [P, TILES, E])
        route3 = sb("route3", [P, TILES, E])
        top8 = sb("top8", [P, TILES, 8])
        place = sb("place", [P, TILES, 8], U32)
        gsum = sb("gsum", [P, TILES])
        gateT = sb("gateT", [P, COLS])
        slots = qT[:].rearrange("p (k s t) -> p k s t", k=3, s=2)
        silu_t, su_t, hg_t = slots[:, 0], slots[:, 1], slots[:, 2]
        oT_t = sb("oT_t", [P, CHUNK])

        ps = ctx.enter_context(nc.psum_tensor("ps", [P, 8, 512], F32))

        s_const = sem("s_const")
        s_tokin = sem("s_tokin")
        s_txtin = sem("s_txtin")
        s_pos = sem("s_pos")
        s_gather = sem("s_gather")
        s_joint = sem("s_joint")
        s_moe = sem("s_moe")
        s_wqkv, s_wo, s_w1, s_w2 = sem("s_wqkv"), sem("s_wo"), sem("s_w1"), sem("s_w2")
        s_vec, s_row = sem("s_vec"), sem("s_row")
        s_zero = sem("s_zero")
        s_masks = sem("s_masks")
        s_dve = sem("s_dve")
        s_act = sem("s_act")
        noise_ready = sem("noise_ready")
        tokw_ready = sem("tokw_ready")
        tok_psum = sem("tok_psum")
        tok_min = sem("tok_min")
        tok_exp = sem("tok_exp")
        tok_mid = sem("tok_mid")
        tok_out = sem("tok_out")
        img_ready = sem("img_ready")
        x_upd = sem("x_upd")
        ln_stats = sem("ln_stats")
        ln_mv = sem("ln_mv")
        ln_eps = sem("ln_eps")
        ln_rstd = sem("ln_rstd")
        xn_ready = sem("xn_ready")
        xT_psum = sem("xT_psum")
        hT_sb = sem("hT_sb")
        q_psum, k_psum, v_psum, u_psum = sem("q_psum"), sem("k_psum"), sem("v_psum"), sem("u_psum")
        q_sb, k_sb, v_sb, u_sb = sem("q_sb"), sem("k_sb"), sem("v_sb"), sem("u_sb")
        kexp_sb = sem("kexp_sb")
        bias_added = sem("bias_added")
        scores_psum = sem("scores_psum")
        max_sb = sem("max_sb")
        shifted_psum = sem("shifted_psum")
        probs_sb = sem("probs_sb")
        pTa_psum, pTb_psum = sem("pTa_psum"), sem("pTb_psum")
        pTa_sb, pTb_sb = sem("pTa_sb"), sem("pTb_sb")
        o_psum = sem("o_psum")
        rden_sb = sem("rden_sb")
        ctx_sb = sem("ctx_sb")
        c_psum = sem("c_psum")
        ctxT_sb = sem("ctxT_sb")
        wo_psum = sem("wo_psum")
        w1_psum = sem("w1_psum")
        gelu_sb = sem("gelu_sb")
        w2_psum = sem("w2_psum")
        silu_ctx = sem("silu_ctx")
        gated_sb = sem("gated_sb")
        x_joint = sem("x_joint")
        lg_psum = sem("lg_psum")
        aff_sb = sem("aff_sb")
        gates_sb = sem("gates_sb")
        gT_psum = sem("gT_psum")
        gT_sb = sem("gT_sb")
        g_psum, up_psum, gb_psum = sem("g_psum"), sem("up_psum"), sem("gb_psum")
        silu_sb = sem("silu_sb")
        su_sb = sem("su_sb")
        hg_sb = sem("hg_sb")
        d_psum = sem("d_psum")
        oT_sb = sem("oT_sb")
        oT_psum = sem("oT_psum")
        final_sb = sem("final_sb")
        s_out = sem("s_out")

        def kview(slot, nk):
            return k_exp[:, slot, 0:NH * nk].rearrange("p (h k) -> p h k", h=NH)

        def text_units():
            return [Unit(S_TXT, S_TXT, T0 + b * S_TXT, kview(b % 2, S_TXT), v_txt[:, b],
                         mask_l_bf[0:PAD_ROW + 1, :], txt_mask[0:PAD_ROW + 1, b, :],
                         (b % 4) * S_TXT, b) for b in range(B)]

        def joint_units():
            units = []
            for b in range(B):
                keys = kview(b % 2, K_JOINT)
                units.append(Unit(S_IMG, S_IMG, b * S_IMG, keys, v_joint[:, b], ident_bf[0:S_IMG, :],
                                  txt_mask[0:S_IMG, 0, 0:S_IMG], (b % 2) * S_IMG, b))
                units.append(Unit(S_TXT, K_JOINT, T0 + b * S_TXT, keys, v_joint[:, b], ident_bf[0:S_TXT, :],
                                  joint_mask[0:S_TXT, :], 2 * S_IMG + (b % 2) * S_TXT, b))
            return units

        def scores_at(i, u):
            s = 2 * (i % 2)
            return ps[0:u.nq, s:s + 2, 0:4 * u.nk]


        def attend_pe(pe, units, at, kexp_at):
            n = len(units)
            for i in range(n + 3):
                if i < n:
                    u = units[i]
                    pe.wait_ge(kexp_sb, kexp_at(u.kexp_no + 1))
                    if i >= 2:
                        pe.wait_ge(probs_sb, at(i - 1))
                    for half in range(2):
                        s = 2 * (i % 2) + half
                        dst = ps[0:u.nq, s, 0:4 * u.nk]
                        nc.tensor.matmul(dst, qT[:, u.qcol:u.qcol + u.nq],
                                         u.kslot[:, 4 * half:4 * half + 4, 0:u.nk],
                                         start=True, stop=False, skip_group_check=True)
                        last = nc.tensor.matmul(dst, u.mask_l[:, 0:u.nq],
                                                u.mask_r.unsqueeze(1).broadcast_to([u.mask_r.shape[0], 4, u.nk]),
                                                start=False, stop=False, skip_group_check=True)
                    last.then_inc(scores_psum, 1)
                if 0 <= i - 1 < n:
                    u, j = units[i - 1], i - 1
                    pe.wait_ge(probs_sb, at(j + 1))
                    if j >= 1:
                        pe.wait_ge(pTa_sb, at(j))
                    for h in range(NH):
                        if h == 4 and j >= 1:
                            pe.wait_ge(pTb_sb, at(j))
                        last = nc.tensor.transpose(
                            ps[0:u.nk, 4 + h // 4, (h % 4) * u.nq:(h % 4 + 1) * u.nq],
                            probs[0:u.nq, j % 2, h // 4, (h % 4) * u.nk:(h % 4 + 1) * u.nk],
                            ident[0:u.nq, 0:u.nq])
                        if h % 4 == 3:
                            last.then_inc((pTa_psum, pTb_psum)[h // 4], 1)
                if 0 <= i - 2 < n:
                    u, j = units[i - 2], i - 2
                    pe.wait_ge(pTa_sb, at(j + 1))
                    if j >= 1:
                        pe.wait_ge(ctx_sb, at(j))
                    for h in range(NH):
                        if h == 4:
                            pe.wait_ge(pTb_sb, at(j + 1))
                        last = nc.tensor.matmul(
                            ps[0:u.nq, 6, h * VW:(h + 1) * VW],
                            probsT[0:u.nk, j % 2, h // 4, (h % 4) * u.nq:(h % 4 + 1) * u.nq],
                            u.vals[0:u.nk, h, :], start=True, stop=True)
                    last.then_inc(o_psum, 1)
                if i < n:
                    u = units[i]
                    pe.wait_ge(max_sb, at(i + 1))
                    for half in range(2):
                        s = 2 * (i % 2) + half
                        last = nc.tensor.matmul(
                            ps[0:u.nq, s, 0:4 * u.nk], ident_bf[0:u.nq, 0:u.nq],
                            neg_max[0:u.nq, i % 2, 4 * half:4 * half + 4].unsqueeze(2)
                            .broadcast_to([u.nq, 4, u.nk]),
                            start=False, stop=True, skip_group_check=True)
                    last.then_inc(shifted_psum, 1)
                if 0 <= i - 3 < n:
                    u, j = units[i - 3], i - 3
                    pe.wait_ge(ctx_sb, at(j + 1))
                    if j % 4 == 0 and j >= 4:
                        pe.wait_ge(ctxT_sb, at.group(j // 4))
                    nc.tensor.transpose(ps[:, 7, u.c_off:u.c_off + u.nq], ctx_sb_t[0:u.nq, j % 2, :],
                                        ident[0:u.nq, 0:u.nq]).then_inc(c_psum, 1)

        def attend_act(act, units, at, evict_ctx):
            n = len(units)
            for i in range(n + 3):
                if 0 <= i - 1 < n:
                    u, j = units[i - 1], i - 1
                    act.wait_ge(pTb_psum, at(j + 1))
                    if j >= 2:
                        act.wait_ge(o_psum, at(j - 1))
                    nc.scalar.activation(probsT[0:u.nk, j % 2, 1, 0:4 * u.nq], ps[0:u.nk, 5, 0:4 * u.nq],
                                         ACT.Copy).then_inc(pTb_sb, 1)
                if i < n:
                    u = units[i]
                    act.wait_ge(shifted_psum, at(i + 1))
                    if i >= 2:
                        act.wait_ge(pTb_psum, at(i - 1))
                    nc.scalar.activation(probs[0:u.nq, i % 2, :, 0:4 * u.nk], scores_at(i, u),
                                         ACT.Exp).then_inc(probs_sb, 1)
                if 0 <= i - 3 < n and (i - 3) % 4 == 3:
                    act.wait_ge(c_psum, at(i - 2))
                    evict_ctx((i - 3) // 4)

        def attend_dve(dve, units, at):
            n = len(units)
            for i in range(n + 2):
                if i < n:
                    u = units[i]
                    dve.wait_ge(scores_psum, at(i + 1))
                    nc.vector.tensor_reduce(
                        neg_max[0:u.nq, i % 2, :].rearrange("p (a h) -> p a h", a=2),
                        scores_at(i, u).rearrange("p a (h k) -> p a h k", h=4),
                        AX.X, ALU.max, negate=True).then_inc(max_sb, 1)
                if 0 <= i - 1 < n:
                    u, j = units[i - 1], i - 1
                    dve.wait_ge(pTa_psum, at(j + 1))
                    if j >= 2:
                        dve.wait_ge(o_psum, at(j - 1))
                    nc.vector.tensor_copy(probsT[0:u.nk, j % 2, 0, 0:4 * u.nq],
                                          ps[0:u.nk, 4, 0:4 * u.nq]).then_inc(pTa_sb, 1)
                if 0 <= i - 2 < n:
                    u, j = units[i - 2], i - 2
                    dve.wait_ge(o_psum, at(j + 1))
                    o = ps[0:u.nq, 6, 0:NH * VW].rearrange("p (h w) -> p h w", h=NH)
                    nc.vector.reciprocal(r_den[0:u.nq, :], o[:, :, HD]).then_inc(rden_sb, 1)
                    dve.wait_ge(rden_sb, at(j + 1))
                    if j >= 2:
                        dve.wait_ge(c_psum, at(j - 1))
                    nc.vector.tensor_tensor(
                        ctx_sb_t[0:u.nq, j % 2, :].rearrange("p (h w) -> p h w", h=NH), o[:, :, 0:HD],
                        r_den[0:u.nq, :].unsqueeze(2).broadcast_to([u.nq, NH, HD]),
                        ALU.mult).then_inc(ctx_sb, 1)

        def spread_keys(slot, nk, parts):
            at, dst = 0, kview(slot, nk)
            for col, n in parts:
                last = nc.gpsimd.tensor_tensor(
                    dst[:, :, at:at + n], kT[:, col:col + n].unsqueeze(1).broadcast_to([P, NH, n]),
                    head_mask.unsqueeze(2).broadcast_to([P, NH, n]), ALU.mult)
                at += n
            last.then_inc(kexp_sb, 1)


        def norm_dve(dve, groups, at):
            for t0, nt in groups:
                for t in range(t0, t0 + nt):
                    last = nc.vector.bn_stats(stats[:, t, :], x_tok[:, t, :])
            last.then_inc(ln_stats, 1)
            dve.wait_ge(ln_stats, at.norm())
            nc.vector.memset(wait_carrier[:], 0.0)
            for t0, nt in groups:
                for t in range(t0, t0 + nt):
                    last = nc.vector.bn_aggr(mv[:, t, :], stats[:, t, :])
                last.then_inc(ln_mv, 1)
            for k, (t0, nt) in enumerate(groups):
                dve.wait_ge(ln_rstd, at(k + 1))
                for t in range(t0, t0 + nt):
                    last = nc.vector.tensor_scalar(x_norm[:, t, :], x_tok[:, t, :], mv[:, t, 0:1],
                                                   rstd[:, t:t + 1], ALU.subtract, ALU.mult)
                last.then_inc(xn_ready, 1)

        def norm_pool(pool, groups, at):
            for k, (t0, nt) in enumerate(groups):
                s = slice(t0, t0 + nt)
                pool.wait_ge(ln_mv, at(k + 1))
                nc.gpsimd.tensor_tensor(veps[:, s], mv[:, s, 1], eps_t[:, s], ALU.add).then_inc(ln_eps, 1)
                pool.wait_ge(ln_eps, at(k + 1))
                nc.gpsimd.tensor_tensor(rstd[:, s], veps[:, s], half_t[:, s], ALU.pow).then_inc(ln_rstd, 1)

        def norm_pe(pe, groups, xn_at, banks):
            for k, (t0, nt) in enumerate(groups):
                pe.wait_ge(xn_ready, xn_at(k + 1))
                for t in range(t0, t0 + nt):
                    last = nc.tensor.transpose(ps[:, banks[k], (t - t0) * P:(t - t0 + 1) * P],
                                               x_norm[:, t, :], ident)
                last.then_inc(xT_psum, 1)

        def project_tokens(weights, src, t0, nt, b):
            for t in range(t0, t0 + nt):
                last = nc.tensor.matmul(ps[:, b, (t - t0) * P:(t - t0 + 1) * P], src[:, t * P:(t + 1) * P],
                                        weights, start=True, stop=True)
            return last

        def row_of(r, n, rows=P):
            return r[0:rows].unsqueeze(1).broadcast_to([rows, n, r.shape[1]])

        block = ctx.enter_context(nc.Block())

        @block.sync
        def _(sp):
            sp.dma_start(const[:], a["const"]).then_inc(s_const, 16)
            sp.dma_start(idx[:, 0:TXT_TILES - 1],
                         a["tokens"]).then_inc(s_txtin, 16)
            sp.dma_start(idx[0:LAST_ROWS, TXT_TILES - 1:TXT_TILES],
                         a["tokens_end"]).then_inc(s_txtin, 16)
            sp.dma_start(noise[:, 0:6], a["noise_cols"]).then_inc(s_tokin, 16)
            sp.dma_start(noise[:, 6:6 + 2 * D], a["noise_rows"].broadcast_to([P, 2 * D])).then_inc(s_tokin, 16)
            sp.dma_start(tok_w[:].rearrange("p m c o -> p (m c o)"), a["tok_w"]).then_inc(s_tokin, 16)
            sp.dma_start(tok_sw[:].rearrange("p m c o -> p (m c o)"), a["tok_sw"]).then_inc(s_tokin, 16)
            sp.dma_start(tok_w3[:], a["tok_w3"]).then_inc(s_tokin, 16)
            sp.dma_start(tok_b[:], a["tok_b"]).then_inc(s_tokin, 16)
            sp.dma_start(patches[:].rearrange("p c t -> p (c t)"), a["patches"]).then_inc(s_tokin, 16)
            sp.dma_start(jrow[:], a["jrow"].broadcast_to([P, JR_ALL])).then_inc(s_joint, 16)
            sp.dma_start(pad_in[PAD_ROW:PAD_ROW + 1, :], a["pad_row"]).then_inc(s_txtin, 16)
            sp.dma_start(pad_col[0:S_TXT, :], a["pad_col"]).then_inc(s_txtin, 16)
            n9 = (TXT_TILES - 1) * P
            sp.dma_start(x_norm[:, IMG_TILES:TILES - 1, :],
                         a["pos"][0:n9, :].rearrange("(t p) d -> p t d", p=P)).then_inc(s_pos, 16)
            sp.dma_start(x_norm[0:LAST_ROWS, TILES - 1, :], a["pos"][n9:TXT_TOKENS, :]).then_inc(s_pos, 16)
            sp.dma_start(w_qkv_t[:], a["w_qkv"][0:P, :]).then_inc(s_wqkv, 16)
            sp.dma_start(vec[:], a["vec"][0:P, :]).then_inc(s_vec, 16)
            sp.dma_start(row[:], a["row"][0:1, :].broadcast_to([P, 3 * D])).then_inc(s_row, 16)
            sp.dma_start(w_o_t[:], a["w_o"][0:P, :]).then_inc(s_wo, 16)
            sp.dma_start(w_1_t[:], a["w_1"][0:P, :]).then_inc(s_w1, 16)
            sp.dma_start(w_2_t[:].rearrange("p f d -> p (f d)"), a["w_2"][0:P, :]).then_inc(s_w2, 16)
            with sp.Fori(1, LAYERS) as l:
                lo = l * P
                sp.wait_ge(v_psum, l * 4)
                sp.dma_start(w_qkv_t[:], a["w_qkv"][bass.ds(lo, P), :]).then_inc(s_wqkv, 16)
                sp.wait_ge(wo_psum, l * NG)
                sp.dma_start(w_o_t[:], a["w_o"][bass.ds(lo, P), :]).then_inc(s_wo, 16)
                sp.wait_ge(w1_psum, l * (NG * FF))
                sp.dma_start(w_1_t[:], a["w_1"][bass.ds(lo, P), :]).then_inc(s_w1, 16)
                sp.wait_ge(gelu_sb, l * (NG * FF))
                sp.dma_start(vec[:], a["vec"][bass.ds(lo, P), :]).then_inc(s_vec, 16)
                sp.wait_ge(bias_added, l * 2)
                sp.dma_start(row[:], a["row"][bass.ds(l, 1), :].broadcast_to([P, 3 * D])).then_inc(s_row, 16)
                sp.wait_ge(w2_psum, l * NG)
                sp.dma_start(w_2_t[:].rearrange("p f d -> p (f d)"), a["w_2"][bass.ds(lo, P), :]
                             ).then_inc(s_w2, 16)
            with sp.Fori(0, CHUNKS) as c:
                sp.wait_ge(final_sb, c + 2)
                sp.dma_start(out[bass.ds(c * CHUNK, CHUNK), :].rearrange("(t p) d -> p t d", p=P),
                             x_tok[:, bass.ds(c * CHUNK_TILES, CHUNK_TILES), :]).then_inc(s_out, 16)
            sp.wait_ge(s_out, 16 * CHUNKS)

        @block.gpsimd
        def _(pool):
            nc.gpsimd.memset(x_tok[:, TILES - 1, :], 0.0).then_inc(s_zero, 1)
            nc.gpsimd.memset(ctxT[:, T0 + TXT_TOKENS:COLS], 0.0).then_inc(s_zero, 1)
            nc.gpsimd.memset(eps_t[:], EPS).then_inc(s_zero, 1)
            nc.gpsimd.memset(half_t[:], -0.5).then_inc(s_zero, 1)
            nc.gpsimd.memset(v_joint[:], 1.0).then_inc(s_zero, 1)
            nc.gpsimd.memset(gateT[:], 0.0).then_inc(s_zero, 1)
            pool.wait_ge(s_txtin, 64)
            pool.wait_ge(s_zero, 6)
            for t in range(TXT_TILES):
                rows = P if t < TXT_TILES - 1 else LAST_ROWS
                pool.indirect_dma_start(
                    out=x_tok[0:rows, IMG_TILES + t, :], out_offset=None, in_=a["item_emb"],
                    in_offset=bass.IndirectOffsetOnAxis(ap=idx[0:rows, t:t + 1], axis=0)
                ).then_inc(s_gather, 16)
            pool.wait_ge(s_const, 16)
            with pool.Fori(0, LAYERS) as l:
                norm_pool(pool, TXT_GROUPS, lambda k: l * (2 * NG) + k)
                for b in range(B):
                    if b == 0:
                        pool.wait_ge(k_sb, l * NG + NG)
                    if b >= 2:
                        pool.wait_ge(scores_psum, l * B + (b - 1))
                    spread_keys(b % 2, S_TXT, [(T0 + b * S_TXT, S_TXT)])
                    if b == 3:
                        pool.wait_ge(xn_ready, l * (2 * NG) + NG)
                        pool.wait_ge(s_row, l * 16 + 16)
                        nc.gpsimd.tensor_tensor(x_tok[:, IMG_TILES:, :], x_tok[:, IMG_TILES:, :],
                                                row_of(row[:, R_BO:R_BO + D], TXT_TILES),
                                                ALU.add).then_inc(bias_added, 1)
                norm_pool(pool, TXT_GROUPS, lambda k: l * (2 * NG) + NG + k)
                pool.wait_ge(xn_ready, l * (2 * NG) + 2 * NG)
                nc.gpsimd.tensor_tensor(x_tok[:, IMG_TILES:, :], x_tok[:, IMG_TILES:, :],
                                        row_of(row[:, R_B2:R_B2 + D], TXT_TILES),
                                        ALU.add).then_inc(bias_added, 1)
            base = LAYERS * 2 * NG
            norm_pool(pool, TXT_GROUPS, lambda k: base + k)
            norm_pool(pool, ALL_GROUPS, lambda k: base + NG + k)
            for b in range(B):
                if b == 0:
                    pool.wait_ge(k_sb, LAYERS * NG + NA)
                if b >= 2:
                    pool.wait_ge(scores_psum, LAYERS * B + 2 * (b - 1))
                spread_keys(b % 2, K_JOINT, [(b * S_IMG, S_IMG), (T0 + b * S_TXT, K_JOINT - S_IMG)])
                if b == 3:
                    pool.wait_ge(xn_ready, base + NG + NA)
                    pool.wait_ge(s_joint, 48)
                    nc.gpsimd.tensor_tensor(x_tok[:], x_tok[:], row_of(jrow[:, JR_BO:JR_BO + D], TILES),
                                            ALU.add).then_inc(bias_added, 1)
            norm_pool(pool, ALL_GROUPS, lambda k: base + NG + NA + k)

        @block.scalar
        def _(act):
            act.dma_start(jw[:], a["jw"]).then_inc(s_joint, 16)
            act.dma_start(jvec[:], a["jvec"]).then_inc(s_joint, 16)
            act.dma_start(w_gu[:].rearrange("p e f -> p (e f)"), a["w_gu"]).then_inc(s_moe, 16)
            act.dma_start(w_dn[:].rearrange("p e f -> p (e f)"), a["w_dn"]).then_inc(s_moe, 16)
            act.dma_start(w_gate[:], a["w_gate"]).then_inc(s_moe, 16)
            act.wait_ge(s_tokin, 16 * 7)
            nc.scalar.activation(noise_abs[:], noise[:], ACT.Abs).then_inc(s_act, 1)
            nc.scalar.activation(noise_sign[:], noise[:], ACT.Sign).then_inc(s_act, 1)
            act.wait_ge(s_act, 2)
            nc.scalar.activation(noise_root[:], noise_abs[:], ACT.Sqrt).then_inc(noise_ready, 1)
            for c in range(2):
                act.wait_ge(tok_min, c + 1)
                nc.scalar.activation(gelu_t[:, 0, 2 * c, :], gelu_t[:, 0, 2 * c + 1, :],
                                     ACT.Exp).then_inc(tok_exp, 1)

            def text_ctx(g):
                w = 4 * S_TXT
                nc.scalar.activation(ctxT[:, T0 + g * w:T0 + (g + 1) * w], ps[:, 7, 0:w],
                                     ACT.Copy).then_inc(ctxT_sb, 1)

            def joint_ctx(g):
                wi, wt = 2 * S_IMG, 2 * S_TXT
                nc.scalar.activation(ctxT[:, g * wi:(g + 1) * wi], ps[:, 7, 0:wi], ACT.Copy)
                nc.scalar.activation(ctxT[:, T0 + g * wt:T0 + (g + 1) * wt], ps[:, 7, wi:wi + wt],
                                     ACT.Copy).then_inc(ctxT_sb, 1)

            def norm_out(groups, at, banks, gain, shift):
                for k, (t0, nt) in enumerate(groups):
                    act.wait_ge(xT_psum, at(k + 1))
                    dst, src = hT[:, t0 * P:(t0 + nt) * P], ps[:, banks[k], 0:nt * P]
                    if gain is None:
                        ins = nc.scalar.activation(dst, src, ACT.Copy)
                    else:
                        ins = nc.scalar.activation(dst, src, ACT.Identity, bias=shift, scale=gain)
                    ins.then_inc(hT_sb, 1)

            with act.Fori(0, LAYERS) as l:
                act.wait_ge(s_vec, l * 16 + 16)
                norm_out(TXT_GROUPS, lambda k: l * (2 * NG) + k, (0, 1, 2),
                         vec[:, V_G1:V_G1 + 1], vec[:, V_B1:V_B1 + 1])
                for g, (t0, nt) in enumerate(TXT_GROUPS):
                    act.wait_ge(k_psum, l * NG + (g + 1))
                    nc.scalar.activation(kT[:, t0 * P:(t0 + nt) * P], ps[:, (6, 7, 0)[g], 0:nt * P],
                                         ACT.Identity, bias=vec[:, V_BK:V_BK + 1]).then_inc(k_sb, 1)
                attend_act(act, text_units(), lambda k: l * B + k, text_ctx)
                norm_out(TXT_GROUPS, lambda k: l * (2 * NG) + NG + k, (0, 1, 2),
                         vec[:, V_G2:V_G2 + 1], vec[:, V_B2:V_B2 + 1])
                for g, (t0, nt) in enumerate(TXT_GROUPS):
                    if g == 2:
                        act.wait_ge(w2_psum, l * NG + 1)
                    for f in range(FF):
                        j = g * FF + f
                        act.wait_ge(w1_psum, l * (NG * FF) + (j + 1))
                        nc.scalar.activation(gelu_t[:, g % 2, f, 0:nt * P], ps[:, (6, 7, 0, 1, 2)[j % 5], 0:nt * P],
                                             ACT.Gelu, bias=vec[:, V_BF + f:V_BF + f + 1]).then_inc(gelu_sb, 1)
            base = LAYERS * 2 * NG
            act.wait_ge(s_joint, 48)
            norm_out(ALL_GROUPS, lambda k: base + k, (0, 1, 2, 3, 4), None, None)
            for g, (t0, nt) in enumerate(ALL_GROUPS):
                act.wait_ge(k_psum, LAYERS * NG + g + 1)
                nc.scalar.activation(kT[:, t0 * P:(t0 + nt) * P], ps[:, 6, 0:nt * P], ACT.Identity,
                                     bias=jvec[:, JV_BK:JV_BK + 1]).then_inc(k_sb, 1)
                act.wait_ge(u_psum, g + 1)
                nc.scalar.activation(uT[:, t0 * P:(t0 + nt) * P], ps[:, 7, 0:nt * P], ACT.Identity,
                                     bias=jvec[:, JV_BU:JV_BU + 1]).then_inc(u_sb, 1)
            attend_act(act, joint_units(), lambda k: LAYERS * B + k, joint_ctx)
            act.wait_ge(ctxT_sb, LAYERS * 4 + 8)
            for g, (t0, nt) in enumerate(ALL_GROUPS):
                nc.scalar.activation(hT[:, t0 * P:(t0 + nt) * P], ctxT[:, t0 * P:(t0 + nt) * P],
                                     ACT.Silu).then_inc(silu_ctx, 1)
            norm_out(ALL_GROUPS, lambda k: base + NA + k, (0, 1, 2, 3, 4), None, None)
            act.wait_ge(lg_psum, 1)
            nc.scalar.activation(aff[:].rearrange("p t e -> p (t e)"), ps[:, 5, 0:TILES * E],
                                 ACT.Sigmoid).then_inc(aff_sb, 1)
            for g, (t0, nt) in enumerate(ALL_GROUPS):
                act.wait_ge(gT_psum, g + 1)
                nc.scalar.activation(gateT[0:E, t0 * P:(t0 + nt) * P], ps[0:E, (6, 7, 0, 1, 2)[g], 0:nt * P],
                                     ACT.Copy).then_inc(gT_sb, 1)
            n = E + 1
            with act.Fori(0, CHUNKS) as c:
                for e in range(n):
                    act.wait_ge(g_psum, c * n + (e + 1))
                    if e >= 2:
                        act.wait_ge(su_sb, c * n + (e - 1))
                    nc.scalar.activation(silu_t[:, e % 2, :], ps[:, e % 2, 0:CHUNK],
                                         ACT.Silu).then_inc(silu_sb, 1)
                act.wait_ge(d_psum, c * n + n)
                nc.scalar.activation(oT_t[:], ps[:, 6, 0:CHUNK], ACT.Copy).then_inc(oT_sb, 1)

        @block.tensor
        def _(pe):
            pe.wait_ge(tokw_ready, 1)
            pe.wait_ge(s_const, 16)
            for c in range(2):
                for m in range(2):
                    for h in range(2):
                        last = nc.tensor.matmul(ps[:, 2 * m + c, :], tok_w[:, m, h, :],
                                                patches[:, h, c * 512:(c + 1) * 512],
                                                start=(h == 0), stop=(h == 1))
                last.then_inc(tok_psum, 1)
            for c in range(2):
                pe.wait_ge(tok_mid, c + 1)
                project_tokens(tok_w3[:], gelu_t[:, 1, 0:2, :].rearrange("p a t -> p (a t)"), 4 * c, 4,
                               4 + c).then_inc(tok_out, 1)
            pe.wait_ge(img_ready, 2)
            pe.wait_ge(s_masks, 1)

            with pe.Fori(0, LAYERS) as l:
                norm_pe(pe, TXT_GROUPS, lambda k: l * (2 * NG) + k, (0, 1, 2))
                pe.wait_ge(s_wqkv, l * 16 + 16)
                for g, (t0, nt) in enumerate(TXT_GROUPS):
                    pe.wait_ge(hT_sb, l * (2 * NG) + (g + 1))
                    rhs = hT[:, t0 * P:(t0 + nt) * P]
                    nc.tensor.matmul(ps[:, 3 + g, 0:nt * P], w_qkv_t[:, 0:D], rhs,
                                     start=True, stop=True).then_inc(q_psum, 1)
                    nc.tensor.matmul(ps[:, (6, 7, 0)[g], 0:nt * P], w_qkv_t[:, D:2 * D], rhs,
                                     start=True, stop=True).then_inc(k_psum, 1)
                for j in range(4):
                    if j >= 2:
                        pe.wait_ge(q_sb, l * NG + (j - 1))
                    for b in range(4 * j, 4 * j + 4):
                        col = T0 + b * S_TXT
                        last = nc.tensor.matmul(ps[0:S_TXT, 1 + j, (b % 4) * D:(b % 4 + 1) * D],
                                                hT[:, col:col + S_TXT], w_qkv_t[:, 2 * D:3 * D],
                                                start=True, stop=True)
                    last.then_inc(v_psum, 1)
                pe.wait_ge(q_sb, l * NG + NG)
                pe.wait_ge(k_sb, l * NG + NG)
                pe.wait_ge(v_sb, l * 4 + 4)
                attend_pe(pe, text_units(), Passed(l), lambda k: l * B + k)
                pe.wait_ge(s_wo, l * 16 + 16)
                pe.wait_ge(ctxT_sb, l * 4 + 4)
                for g, (t0, nt) in enumerate(TXT_GROUPS):
                    project_tokens(w_o_t[:], ctxT, t0, nt, 3 + g).then_inc(wo_psum, 1)
                norm_pe(pe, TXT_GROUPS, lambda k: l * (2 * NG) + NG + k, (0, 1, 2))

                def hidden(g):
                    t0, nt = TXT_GROUPS[g]
                    pe.wait_ge(hT_sb, l * (2 * NG) + NG + (g + 1))
                    for f in range(FF):
                        j = g * FF + f
                        if j == 3:
                            pe.wait_ge(hT_sb, l * (2 * NG) + NG + 2)
                        if j == 4:
                            pe.wait_ge(hT_sb, l * (2 * NG) + NG + 3)
                        if j >= 5:
                            pe.wait_ge(gelu_sb, l * (NG * FF) + (j - 4))
                        nc.tensor.matmul(ps[:, (6, 7, 0, 1, 2)[j % 5], 0:nt * P], w_1_t[:, f * D:(f + 1) * D],
                                         hT[:, t0 * P:(t0 + nt) * P], start=True, stop=True
                                         ).then_inc(w1_psum, 1)

                def ffn_out(g):
                    t0, nt = TXT_GROUPS[g]
                    pe.wait_ge(gelu_sb, l * (NG * FF) + FF * (g + 1))
                    for t in range(nt):
                        for f in range(FF):
                            last = nc.tensor.matmul(ps[:, 3 + g, t * P:(t + 1) * P],
                                                    gelu_t[:, g % 2, f, t * P:(t + 1) * P], w_2_t[:, f, :],
                                                    start=(f == 0), stop=(f == FF - 1))
                    last.then_inc(w2_psum, 1)

                pe.wait_ge(s_w1, l * 16 + 16)
                hidden(0)
                hidden(1)
                pe.wait_ge(s_w2, l * 16 + 16)
                ffn_out(0)
                hidden(2)
                ffn_out(1)
                ffn_out(2)
            base = LAYERS * 2 * NG
            norm_pe(pe, ALL_GROUPS, lambda k: base + NG + k, (0, 1, 2, 3, 4))
            pe.wait_ge(s_joint, 48)
            for g, (t0, nt) in enumerate(ALL_GROUPS):
                pe.wait_ge(hT_sb, base + g + 1)
                rhs = hT[:, t0 * P:(t0 + nt) * P]
                for m, b, psum_sem, sb_sem in ((0, 5, q_psum, q_sb), (1, 6, k_psum, k_sb), (3, 7, u_psum, u_sb)):
                    if g >= 1:
                        before = 0 if m == 3 else LAYERS * NG
                        pe.wait_ge(sb_sem, before + g)
                    nc.tensor.matmul(ps[:, b, 0:nt * P], jw[:, m * D:(m + 1) * D], rhs,
                                     start=True, stop=True).then_inc(psum_sem, 1)
            for j in range(4):
                for b in range(4 * j, 4 * j + 4):
                    s = slice((b % 4) * D, (b % 4 + 1) * D)
                    nc.tensor.matmul(ps[0:S_IMG, 1 + j, s], hT[:, b * S_IMG:(b + 1) * S_IMG],
                                     jw[:, 2 * D:3 * D], start=True, stop=True)
                    col = T0 + b * S_TXT
                    last = nc.tensor.matmul(ps[S_IMG:K_JOINT, 1 + j, s], hT[:, col:col + K_JOINT - S_IMG],
                                            jw[:, 2 * D:3 * D], start=True, stop=True)
                last.then_inc(v_psum, 1)
            pe.wait_ge(q_sb, LAYERS * NG + NA)
            pe.wait_ge(k_sb, LAYERS * NG + NA)
            pe.wait_ge(u_sb, NA)
            pe.wait_ge(v_sb, LAYERS * 4 + 4)
            attend_pe(pe, joint_units(), Passed(LAYERS), lambda k: LAYERS * B + k)
            for g, (t0, nt) in enumerate(ALL_GROUPS):
                pe.wait_ge(gated_sb, g + 1)
                project_tokens(jw[:, 4 * D:5 * D], uT, t0, nt, 3 + g).then_inc(wo_psum, 1)
            norm_pe(pe, ALL_GROUPS, lambda k: base + NG + NA + k, (0, 1, 2, 3, 4))
            pe.wait_ge(s_moe, 48)
            pe.wait_ge(hT_sb, base + 2 * NA)
            for t in range(TILES):
                last = nc.tensor.matmul(ps[:, 5, t * E:(t + 1) * E], hT[:, t * P:(t + 1) * P], w_gate[:],
                                        start=True, stop=True)
            last.then_inc(lg_psum, 1)
            pe.wait_ge(gates_sb, 1)
            for g, (t0, nt) in enumerate(ALL_GROUPS):
                for t in range(t0, t0 + nt):
                    last = nc.tensor.transpose(ps[0:E, (6, 7, 0, 1, 2)[g], (t - t0) * P:(t - t0 + 1) * P],
                                               aff[:, t, :], ident)
                last.then_inc(gT_psum, 1)
            pe.wait_ge(gT_sb, NA)
            n = E + 1
            with pe.Fori(0, CHUNKS) as c:
                tok = bass.ds(c * CHUNK, CHUNK)

                def down(e):
                    if e < E:
                        pe.wait_ge(hg_sb, c * E + (e + 1))
                    else:
                        pe.wait_ge(su_sb, c * n + n)
                    nc.tensor.matmul(ps[:, 6, 0:CHUNK], w_dn[:, e, :], hg_t[:, e % 2, :],
                                     start=(e == 0), stop=(e == E)).then_inc(d_psum, 1)

                for e in range(n):
                    if e >= 2:
                        pe.wait_ge(silu_sb, c * n + (e - 1))
                    nc.tensor.matmul(ps[:, e % 2, 0:CHUNK], w_gu[:, e, 0:D], hT[:, tok],
                                     start=True, stop=True).then_inc(g_psum, 1)
                    if e >= 2:
                        pe.wait_ge(su_sb, c * n + (e - 1))
                    nc.tensor.matmul(ps[:, 2 + e % 2, 0:CHUNK], w_gu[:, e, D:2 * D], hT[:, tok],
                                     start=True, stop=True).then_inc(up_psum, 1)
                    if e < E:
                        if e >= 2:
                            pe.wait_ge(hg_sb, c * E + (e - 1))
                        nc.tensor.matmul(ps[:, 4 + e % 2, 0:CHUNK], select[:, e, :], gateT[:, tok],
                                         start=True, stop=True).then_inc(gb_psum, 1)
                    if e >= 1:
                        down(e - 1)
                down(E)
                pe.wait_ge(final_sb, c + 1)
                pe.wait_ge(oT_sb, c + 1)
                for t in range(CHUNK_TILES):
                    last = nc.tensor.transpose(ps[:, 7, t * P:(t + 1) * P], oT_t[:, t * P:(t + 1) * P], ident)
                last.then_inc(oT_psum, 1)

        @block.vector
        def _(dve):
            chain = [0]

            def link(ins):
                chain[0] += 1
                ins.then_inc(s_dve, 1)
                dve.wait_ge(s_dve, chain[0])

            dve.wait_ge(s_const, 16)
            dve.wait_ge(s_txtin, 64)
            nc.vector.tensor_copy(ident_bf[:], ident)
            nc.vector.tensor_copy(mask_l_bf[:], const[:, C_MASKL:C_MASKL + S_TXT])
            nc.vector.tensor_copy(joint_mask[:], const[:, C_JOINT:C_JOINT + K_JOINT])
            nc.vector.tensor_copy(txt_mask[0:PAD_ROW], row_of(const[:, C_CAUSAL:C_CAUSAL + S_TXT], B, PAD_ROW))
            r = slice(PAD_ROW, PAD_ROW + 1)
            nc.vector.tensor_scalar(txt_mask[r].rearrange("p b k -> p (b k)"), pad_in[r, :], 0.0, FAR,
                                    ALU.is_equal, ALU.mult)
            link(nc.vector.tensor_scalar(pad_col1[0:S_TXT, :], pad_col[0:S_TXT, :], 0.0, -1.0,
                                         ALU.is_equal, ALU.mult))
            nc.vector.tensor_scalar(
                v_txt[0:S_TXT, :, :, HD], pad_col1[0:S_TXT, :].unsqueeze(2).broadcast_to([S_TXT, B, NH]),
                1.0, None, ALU.add)
            nc.vector.tensor_copy(select[:], ident[:, 0:E].unsqueeze(2).broadcast_to([P, E, P])
                                  ).then_inc(s_masks, 1)
            dve.wait_ge(noise_ready, 1)
            dve.wait_ge(s_tokin, 16 * 7)
            link(nc.vector.tensor_tensor(noise[:], noise_root[:], noise_sign[:], ALU.mult))
            for m in range(2):
                for h in range(2):
                    nc.vector.scalar_tensor_tensor(
                        tok_sw[:, m, h, :], tok_sw[:, m, h, :], noise[:, 2 * m + h:2 * m + h + 1],
                        noise[:, 6 + m * D:6 + (m + 1) * D], ALU.mult, ALU.mult)
                last = nc.vector.scalar_tensor_tensor(tok_bn[:, m:m + 1], tok_b[:, 2 * m + 1:2 * m + 2],
                                                      noise[:, 4 + m:5 + m], tok_b[:, 2 * m:2 * m + 1],
                                                      ALU.mult, ALU.add)
            link(last)
            dve.wait_ge(s_joint, 48)
            nc.vector.tensor_tensor(tok_w[:], tok_w[:], tok_sw[:], ALU.add).then_inc(tokw_ready, 1)
            nc.vector.tensor_tensor(pos_b[:], const[:, C_POS:C_POS + D], jrow[:, JR_W3B:JR_W3B + D], ALU.add)
            dve.wait_ge(s_gather, 16 * TXT_TILES)
            dve.wait_ge(s_pos, 32)
            m = slice(IMG_TILES, TILES - 1)
            nc.vector.tensor_tensor(x_tok[:, m, :], x_tok[:, m, :], x_norm[:, m, :], ALU.add)
            nc.vector.tensor_tensor(x_tok[0:LAST_ROWS, TILES - 1, :], x_tok[0:LAST_ROWS, TILES - 1, :],
                                    x_norm[0:LAST_ROWS, TILES - 1, :], ALU.add).then_inc(x_upd, 1)
            for c in range(2):
                dve.wait_ge(tok_psum, c + 1)
                nc.vector.tensor_scalar(gelu_t[:, 0, 2 * c + 1, :], ps[:, c, :], tok_bn[:, 0:1], EXP_CAP,
                                        ALU.add, ALU.min).then_inc(tok_min, 1)
            for c in range(2):
                dve.wait_ge(tok_exp, c + 1)
                t = gelu_t[:, 0, 2 * c, :]
                w2 = gelu_t[:, 0, 2 * c + 1, :]
                w = gelu_t[:, 1, 2, :]
                link(nc.vector.scalar_tensor_tensor(w, t, 2.0, t, ALU.add, ALU.mult))
                link(nc.vector.tensor_scalar(w2, w, 2.0, None, ALU.add))
                link(nc.vector.reciprocal(t, w2))
                link(nc.vector.tensor_tensor(w2, w, t, ALU.mult))
                link(nc.vector.scalar_tensor_tensor(t, ps[:, c, :], tok_bn[:, 0:1], w2, ALU.add, ALU.mult))
                nc.vector.scalar_tensor_tensor(gelu_t[:, 1, c, :], ps[:, 2 + c, :], tok_bn[:, 1:2], t,
                                               ALU.add, ALU.mult).then_inc(tok_mid, 1)
            for c in range(2):
                dve.wait_ge(tok_out, c + 1)
                nc.vector.tensor_tensor(x_tok[:, 4 * c:4 * c + 4, :],
                                        ps[:, 4 + c, :].rearrange("p (t d) -> p t d", t=4),
                                        row_of(pos_b[:], 4), ALU.add).then_inc(img_ready, 1)

            def add_back(groups, signal, psum_at, psum_sem):
                for g, (t0, nt) in enumerate(groups):
                    dve.wait_ge(psum_sem, psum_at(g + 1))
                    nc.vector.tensor_tensor(x_tok[:, t0:t0 + nt, :], x_tok[:, t0:t0 + nt, :],
                                            ps[:, 3 + g, 0:nt * P].rearrange("p (t d) -> p t d", t=nt),
                                            ALU.add).then_inc(signal, 1)

            with dve.Fori(0, LAYERS) as l:
                dve.wait_ge(x_upd, l * (2 * NG) + 1)
                norm_dve(dve, TXT_GROUPS, Norms(l * (2 * NG), l * 2))
                dve.wait_ge(s_row, l * 16 + 16)
                dve.wait_ge(s_vec, l * 16 + 16)
                for g, (t0, nt) in enumerate(TXT_GROUPS):
                    dve.wait_ge(q_psum, l * NG + (g + 1))
                    nc.vector.tensor_scalar(qT[:, t0 * P:(t0 + nt) * P], ps[:, 3 + g, 0:nt * P],
                                            vec[:, V_BQ:V_BQ + 1], float(Q_SCALE), ALU.add, ALU.mult
                                            ).then_inc(q_sb, 1)
                for j in range(4):
                    dve.wait_ge(v_psum, l * 4 + (j + 1))
                    nc.vector.tensor_tensor(
                        v_txt[0:S_TXT, 4 * j:4 * j + 4, :, 0:HD],
                        ps[0:S_TXT, 1 + j, :].rearrange("p (b h w) -> p b h w", b=4, w=HD),
                        row[0:S_TXT, R_BV:R_BV + D].rearrange("p (h w) -> p h w", w=HD).unsqueeze(1)
                        .broadcast_to([S_TXT, 4, NH, HD]), ALU.add).then_inc(v_sb, 1)
                attend_dve(dve, text_units(), lambda k: l * B + k)
                dve.wait_ge(bias_added, l * 2 + 1)
                add_back(TXT_GROUPS, x_upd, lambda k: l * NG + k, wo_psum)
                dve.wait_ge(x_upd, l * (2 * NG) + (NG + 1))
                norm_dve(dve, TXT_GROUPS, Norms(l * (2 * NG) + NG, l * 2 + 1))
                dve.wait_ge(bias_added, l * 2 + 2)
                add_back(TXT_GROUPS, x_upd, lambda k: l * NG + k, w2_psum)
            base = LAYERS * 2 * NG
            dve.wait_ge(x_upd, base + 1)
            norm_dve(dve, TXT_GROUPS, Norms(base, 2 * LAYERS))
            dve.wait_ge(xn_ready, base + NG)
            m = slice(IMG_TILES, TILES)
            link(nc.vector.tensor_tensor(x_norm[:, m, :], x_norm[:, m, :],
                                         row_of(jrow[:, JR_FG:JR_FG + D], TXT_TILES), ALU.mult))
            link(nc.vector.tensor_tensor(x_tok[:, m, :], x_norm[:, m, :],
                                         row_of(jrow[:, JR_FB:JR_FB + D], TXT_TILES), ALU.add))
            dve.wait_ge(img_ready, 2)
            norm_dve(dve, ALL_GROUPS, Norms(base + NG, 2 * LAYERS + 1))
            for g, (t0, nt) in enumerate(ALL_GROUPS):
                dve.wait_ge(q_psum, LAYERS * NG + g + 1)
                nc.vector.tensor_scalar(qT[:, t0 * P:(t0 + nt) * P], ps[:, 5, 0:nt * P],
                                        jvec[:, JV_BQ:JV_BQ + 1], float(Q_SCALE), ALU.add, ALU.mult
                                        ).then_inc(q_sb, 1)
            for j in range(4):
                dve.wait_ge(v_psum, LAYERS * 4 + j + 1)
                nc.vector.tensor_tensor(
                    v_joint[0:K_JOINT, 4 * j:4 * j + 4, :, 0:HD],
                    ps[0:K_JOINT, 1 + j, :].rearrange("p (b h w) -> p b h w", b=4, w=HD),
                    jrow[0:K_JOINT, JR_BV:JR_BV + D].rearrange("p (h w) -> p h w", w=HD).unsqueeze(1)
                    .broadcast_to([K_JOINT, 4, NH, HD]), ALU.add).then_inc(v_sb, 1)
            attend_dve(dve, joint_units(), lambda k: LAYERS * B + k)
            for g, (t0, nt) in enumerate(ALL_GROUPS):
                s = slice(t0 * P, (t0 + nt) * P)
                dve.wait_ge(silu_ctx, g + 1)
                dve.wait_ge(u_sb, NA)
                nc.vector.tensor_tensor(uT[:, s], uT[:, s], hT[:, s], ALU.mult).then_inc(gated_sb, 1)
            dve.wait_ge(bias_added, 2 * LAYERS + 1)
            add_back(ALL_GROUPS, x_joint, lambda k: LAYERS * NG + k, wo_psum)
            dve.wait_ge(x_joint, NA)
            norm_dve(dve, ALL_GROUPS, Norms(base + NG + NA, 2 * LAYERS + 2))
            dve.wait_ge(aff_sb, 1)
            link(nc.vector.tensor_tensor(route[:], aff[:], row_of(jrow[:, JR_EB:JR_EB + E], TILES), ALU.add))
            for t in range(TILES):
                last = nc.vector.max(top8[:, t, :], route[:, t, :])
            link(last)
            for t in range(TILES):
                last = nc.vector.max_index(place[:, t, :], top8[:, t, :], route[:, t, :])
            link(last)
            for k in range(3):
                last = nc.vector.tensor_tensor(
                    (route, route2, route3)[k][:], row_of(const[:, C_IOTA:C_IOTA + E], TILES),
                    place[:, :, k:k + 1].broadcast_to([P, TILES, E]), ALU.is_equal)
            link(last)
            link(nc.vector.tensor_tensor(route[:], route[:], route2[:], ALU.add))
            link(nc.vector.tensor_tensor(route[:], route[:], route3[:], ALU.add))
            link(nc.vector.tensor_tensor(aff[:], aff[:], route[:], ALU.mult))
            link(nc.vector.tensor_reduce(gsum[:], aff[:], AX.X, ALU.add))
            link(nc.vector.tensor_scalar(gsum[:], gsum[:], 1e-9, None, ALU.add))
            link(nc.vector.reciprocal(veps[:], gsum[:]))
            nc.vector.tensor_tensor(aff[:], aff[:], veps[:].unsqueeze(2).broadcast_to([P, TILES, E]),
                                    ALU.mult).then_inc(gates_sb, 1)
            nc.vector.memset(wait_carrier[:], 0.0).then_inc(final_sb, 1)
            n = E + 1
            with dve.Fori(0, CHUNKS) as c:
                def silu_up(e):
                    if e == E:
                        dve.wait_ge(d_psum, c * n + (e - 1))
                    dve.wait_ge(up_psum, c * n + (e + 1))
                    dve.wait_ge(silu_sb, c * n + (e + 1))
                    dst = hg_t if e == E else su_t
                    return nc.vector.tensor_tensor(dst[:, e % 2, :], silu_t[:, e % 2, :],
                                                   ps[:, 2 + e % 2, 0:CHUNK], ALU.mult)

                silu_up(0).then_inc(su_sb, 1)
                for e in range(E):
                    if e + 1 < E:
                        silu_up(e + 1).then_inc(su_sb, 1)
                    if e >= 2:
                        dve.wait_ge(d_psum, c * n + (e - 1))
                    dve.wait_ge(gb_psum, c * E + (e + 1))
                    dve.wait_ge(su_sb, c * n + (e + 1))
                    nc.vector.tensor_tensor(hg_t[:, e % 2, :], su_t[:, e % 2, :], ps[:, 4 + e % 2, 0:CHUNK],
                                            ALU.mult).then_inc(hg_sb, 1)
                silu_up(E).then_inc(su_sb, 1)
                dve.wait_ge(oT_psum, c + 1)
                xs = x_tok[:, bass.ds(c * CHUNK_TILES, CHUNK_TILES), :]
                nc.vector.tensor_tensor(xs, xs, ps[:, 7, 0:CHUNK].rearrange("p (t d) -> p t d", t=CHUNK_TILES),
                                        ALU.add).then_inc(final_sb, 1)


_NAMES = ["const", "tokens", "tokens_end", "noise_cols", "noise_rows", "tok_w", "tok_sw", "tok_w3", "tok_b", "patches",
          "pad_row", "pad_col", "pos", "item_emb", "w_qkv", "w_o", "w_1", "w_2", "vec", "row", "jw", "jvec",
          "jrow", "w_gu", "w_dn", "w_gate"]


def constants():
    c = np.zeros((P, C_ALL), np.float32)
    c[:, C_ID:C_ID + P] = np.eye(P)
    i, j = np.arange(S_TXT)[:, None], np.arange(S_TXT)[None, :]
    c[:S_TXT, C_CAUSAL:C_CAUSAL + S_TXT] = np.where(j > i, FAR, 0.0)
    i, j = S_IMG + np.arange(S_TXT)[:, None], np.arange(K_JOINT)[None, :]
    c[:S_TXT, C_JOINT:C_JOINT + K_JOINT] = np.where((j <= i) & (i + j <= S_ALL), 0.0, FAR)
    c[:S_TXT, C_MASKL:C_MASKL + S_TXT] = np.eye(S_TXT)
    c[PAD_ROW, C_MASKL:C_MASKL + S_TXT] = 1.0
    c[np.arange(P), C_HEAD + np.arange(P) // HD] = 1.0
    pos = np.arange(S_IMG, dtype=np.float32)[:, None]
    div = np.exp(np.arange(0, D, 2, dtype=np.float32) * np.float32(-np.log(10000.0) / D))
    ang = (pos * div).astype(np.float32)
    pe = np.stack([np.sin(ang), np.cos(ang)], axis=-1).reshape(S_IMG, D)
    c[:, C_IOTA:C_IOTA + E] = np.arange(E)
    c[:, C_POS:C_POS + D] = np.tile(pe, (P // S_IMG, 1))
    return c


def kernel(**inputs):
    import concourse.bacc as _bacc
    from concourse.bass_utils import run_bass_kernel_spmd as _run

    f = {k: np.asarray(v) for k, v in inputs.items()}

    def t(name):
        return f[name]

    def halves(w):
        return w.T.reshape(2, P, D).transpose(1, 0, 2)

    def col(name, n=1):
        return t(name).reshape(n, P).T

    x = t("x").reshape(B, 8, 16, 8, 16).transpose(2, 4, 0, 1, 3).reshape(2, P, T0).transpose(1, 0, 2)
    tokens = t("x_txt").reshape(TXT_TOKENS)
    layers = range(LAYERS)
    arrays = {
        "const": constants(),
        "tokens": tokens[:TXT_TOKENS - LAST_ROWS].reshape(TXT_TILES - 1, P).T,
        "tokens_end": tokens[TXT_TOKENS - LAST_ROWS:, None],
        "noise_cols": np.concatenate([col("L0_tok_eps_in1", 2), col("L0_tok_eps_in2", 2),
                                      col("L0_tok_eps_out1"), col("L0_tok_eps_out2")], axis=1),
        "noise_rows": np.concatenate([t("L0_tok_eps_out1"), t("L0_tok_eps_out2")])[None, :],
        "tok_w": np.stack([halves(t("L0_tok_W1_w")), halves(t("L0_tok_W2_w"))], axis=1).reshape(P, 4 * D),
        "tok_sw": np.stack([halves(t("L0_tok_W1_sw")), halves(t("L0_tok_W2_sw"))], axis=1).reshape(P, 4 * D),
        "tok_w3": t("L0_tok_W3_w").T,
        "tok_b": np.stack([t("L0_tok_W1_b"), t("L0_tok_W1_sb"), t("L0_tok_W2_b"), t("L0_tok_W2_sb")], axis=1),
        "patches": x.reshape(P, 2 * T0),
        "pad_row": t("mask_BS_f1_0").reshape(1, TXT_TOKENS),
        "pad_col": t("mask_BS_f1_0").T,
        "pos": np.concatenate([t("L0_txt_pos_emb")[:S_TXT]] * B, axis=0),
        "item_emb": t("L0_txt_item_emb"),
        "w_qkv": np.concatenate([t("L0_txt_Wq"), t("L0_txt_Wk"), t("L0_txt_Wv")], axis=2).reshape(LAYERS * P, 3 * D),
        "w_o": t("L0_txt_Wo").reshape(LAYERS * P, D),
        "w_1": t("L0_txt_W1").reshape(LAYERS * P, FF * D),
        "w_2": t("L0_txt_W2").reshape(LAYERS, FF, P, D).transpose(0, 2, 1, 3).reshape(LAYERS * P, FF * D),
        "vec": np.concatenate([
            np.concatenate([np.stack([t("L0_txt_" + n)[l] for n in ("ln1_g", "ln1_b", "bq", "bk", "ln2_g", "ln2_b")],
                                     axis=1), t("L0_txt_b1")[l].reshape(FF, P).T], axis=1) for l in layers], axis=0),
        "row": np.concatenate([t("L0_txt_bv"), t("L0_txt_bo"), t("L0_txt_b2")], axis=1),
        "jw": np.concatenate([t("L0_attn_w_qkv").T, t("L0_attn_w_u").T, t("L0_attn_w_out").T], axis=1),
        "jvec": np.stack([t("L0_attn_b_qkv")[0:D], t("L0_attn_b_qkv")[D:2 * D], t("L0_attn_b_u")], axis=1),
        "jrow": np.concatenate([t("L0_attn_b_qkv")[2 * D:], t("L0_attn_b_out"), t("L0_tok_W3_b"), t("L0_txt_lnf_g"),
                                t("L0_txt_lnf_b"), t("L0_ffn_expert_bias")])[None, :],
        "w_gu": np.concatenate([t("L0_ffn_expert_gate_up").transpose(2, 0, 1),
                                t("L0_ffn_shared_gate_up").T[:, None, :]], axis=1).reshape(P, (E + 1) * 2 * D),
        "w_dn": np.concatenate([t("L0_ffn_expert_down").transpose(2, 0, 1),
                                t("L0_ffn_shared_down").T[:, None, :]], axis=1).reshape(P, (E + 1) * D),
        "w_gate": t("L0_ffn_gate_w").T,
    }
    nc = _bacc.Bacc("TRN2", target_bir_lowering=False, num_devices=1)
    given, aps = {}, {}
    for name in _NAMES:
        v = np.ascontiguousarray(arrays[name])
        given["in_" + name] = v
        aps[name] = nc.dram_tensor("in_" + name, v.shape, mybir.dt.from_np(v.dtype), kind="ExternalInput").ap()
    out = nc.dram_tensor("out_tokens", (COLS, D), F32, kind="ExternalOutput").ap()
    build(nc, aps, out)
    got = _run(nc, [given], core_ids=[0]).results[0]["out_tokens"]
    return np.concatenate([got[:T0].reshape(B, S_IMG, D), got[T0:T0 + TXT_TOKENS].reshape(B, S_TXT, D)], axis=1)
```

```python
from contextlib import ExitStack

import numpy as np

import concourse.bass as bass
from concourse import mybir

F32 = mybir.dt.float32
F32R = mybir.dt.float32r
BF16 = mybir.dt.bfloat16
I32 = mybir.dt.int32
U32 = mybir.dt.uint32
ALU = mybir.AluOpType
ACT = mybir.ActivationFunctionType
AX = mybir.AxisListType

P = 128
D = 128
B = 16
NH, HD = 8, 16
VW = HD + 1
LAYERS = 4
S_IMG, S_TXT = 64, 77
S_ALL = S_IMG + S_TXT
K_JOINT = S_ALL // 2 + 1
IMG_TILES = B * S_IMG // P
TXT_TOKENS = B * S_TXT
TXT_TILES = -(-TXT_TOKENS // P)
TILES = IMG_TILES + TXT_TILES
LAST_ROWS = TXT_TOKENS - (TXT_TILES - 1) * P
COLS = TILES * P
T0 = IMG_TILES * P
FF = 4
E = 16
CHUNK_TILES = 3
CHUNK = CHUNK_TILES * P
CHUNKS = TILES // CHUNK_TILES
EW = 3 * D
STAGE = 4
EPS = 1e-5
FAR = -1e30
Q_SCALE = 1.0 / np.sqrt(HD)
EXP_CAP = 30.0


def groups_of(first, count):
    return [(t, min(4, first + count - t)) for t in range(first, first + count, 4)]


TXT_GROUPS = groups_of(IMG_TILES, TXT_TILES)
ALL_GROUPS = groups_of(0, TILES)
NG = len(TXT_GROUPS)
NA = len(ALL_GROUPS)

C_ID, C_CAUSAL, C_JOINT, C_MASKL, C_HEAD, C_POS = 0, 128, 205, 276, 353, 361
C_IOTA = 489
C_ALL = 505
PAD_ROW = 96
V_G1, V_B1, V_BQ, V_BK, V_G2, V_B2, V_BF = 0, 1, 2, 3, 4, 5, 6
V_ALL = 10
R_BV, R_BO, R_B2 = 0, 128, 256
JV_BQ, JV_BK, JV_BU = 0, 1, 2
JR_BV, JR_BO, JR_W3B, JR_FG, JR_FB, JR_EB = 0, 128, 256, 384, 512, 640
JR_ALL = 656


class Unit:

    def __init__(self, nq, nk, qcol, kslot, vals, mask_l, mask_r, c_off, kexp_no):
        self.nq, self.nk, self.qcol, self.kslot, self.vals = nq, nk, qcol, kslot, vals
        self.mask_l, self.mask_r, self.c_off, self.kexp_no = mask_l, mask_r, c_off, kexp_no


class Passed:

    def __init__(self, l):
        self.l = l

    def __call__(self, k):
        return self.l * B + k

    def group(self, g):
        return self.l * (B // 4) + g


class Norms:

    def __init__(self, groups, norms):
        self.groups, self.norms = groups, norms

    def __call__(self, k):
        return self.groups + k

    def norm(self):
        return self.norms + 1


def build(nc, a, out):
    ctx = ExitStack()
    with ctx:
        def sb(name, shape, dt=F32):
            return ctx.enter_context(nc.sbuf_tensor(name, shape, dt))

        def sem(name):
            return ctx.enter_context(nc.semaphore(name))

        const = sb("const", [P, C_ALL])
        ident = const[:, C_ID:C_ID + P]
        ident_bf = sb("ident_bf", [P, P], BF16)
        mask_l_bf = sb("mask_l_bf", [P, S_TXT], BF16)
        txt_mask = sb("txt_mask", [P, B, S_TXT], BF16)
        joint_mask = sb("joint_mask", [P, K_JOINT], BF16)
        pad_col = sb("pad_col", [P, B])
        pad_col1 = sb("pad_col1", [P, B])
        head_mask = const[:, C_HEAD:C_HEAD + NH]
        eps_t = sb("eps_t", [P, TILES])
        half_t = sb("half_t", [P, TILES])
        x_tok = sb("x_tok", [P, TILES, D])
        x_norm = sb("x_norm", [P, TILES, D])
        hT = sb("hT", [P, COLS])
        qT = sb("qT", [P, COLS])
        kT = sb("kT", [P, COLS])
        uT = sb("uT", [P, COLS])
        ctxT = sb("ctxT", [P, COLS])
        stats = sb("stats", [P, TILES, 6])
        mv = sb("mv", [P, TILES, 2])
        wait_carrier = sb("wait_carrier", [1, 1])
        veps = sb("veps", [P, TILES])
        rstd = sb("rstd", [P, TILES])
        k_exp = sb("k_exp", [P, 2, NH * S_TXT])
        v_joint = sb("v_joint", [P, B, NH, VW])
        probs = sb("probs", [P, 2, 2, 4 * S_TXT])
        probsT = sb("probsT", [P, 2, 2, 4 * S_TXT])
        pad_in = probsT[:].rearrange("p a b k -> p (a b k)")
        neg_max = sb("neg_max", [P, 2, NH], BF16)
        r_den = sb("r_den", [P, NH])
        ctx_sb_t = sb("ctx_sb_t", [P, 2, D])
        jw = sb("jw", [P, 5 * D])
        jvec = sb("jvec", [P, 3])
        jrow = sb("jrow", [P, JR_ALL])
        idx = sb("idx", [P, TXT_TILES], I32)
        w_gate = sb("w_gate", [P, E])
        select = sb("select", [P, E, P], F32R)
        gateT = sb("gateT", [P, COLS], F32R)
        top8 = sb("top8", [P, TILES, 8])
        place = sb("place", [P, TILES, 8], U32)
        gsum = sb("gsum", [P, TILES])
        oT_t = sb("oT_t", [P, CHUNK])
        slots = qT[:].rearrange("p (k s t) -> p k s t", k=3, s=2)
        silu_t, su_t, hg_t = slots[:, 0], slots[:, 1], slots[:, 2]

        def after_keys(k):
            n = TILES * E
            return kT[:, k * n:(k + 1) * n].rearrange("p (t e) -> p t e", t=TILES)

        aff, route, route2, route3 = (after_keys(k) for k in range(4))

        with ExitStack() as early:
            def sbe(name, shape, dt=F32):
                return early.enter_context(nc.sbuf_tensor(name, shape, dt))

            v_txt = sbe("v_txt", [P, B, NH, VW])
            gelu_t = sbe("gelu_t", [P, 2, FF, 512])
            w_qkv_t = sbe("w_qkv_t", [P, 3 * D])
            w_o_t = sbe("w_o_t", [P, D])
            w_1_t = sbe("w_1_t", [P, FF * D])
            w_2_t = sbe("w_2_t", [P, FF, D])
            vec = sbe("vec", [P, V_ALL])
            row = sbe("row", [P, 3 * D])
            patches = sbe("patches", [P, 2, T0])
            tok_w = sbe("tok_w", [P, 2, 2, D])
            tok_sw = sbe("tok_sw", [P, 2, 2, D])
            tok_w3 = sbe("tok_w3", [P, D])
            tok_b = sbe("tok_b", [P, 4])
            noise = sbe("noise", [P, 6 + 2 * D])
            noise_abs = sbe("noise_abs", [P, 6 + 2 * D])
            noise_root = sbe("noise_root", [P, 6 + 2 * D])
            noise_sign = sbe("noise_sign", [P, 6 + 2 * D])
            tok_bn = sbe("tok_bn", [P, 2])
            pos_b = sbe("pos_b", [P, D])
        w_stage = sb("w_stage", [P, STAGE, EW])
        w_hi = sb("w_hi", [P, E + 1, EW], F32R)
        w_lo = sb("w_lo", [P, E + 1, EW], F32R)
        h_hi = sb("h_hi", [P, COLS], F32R)
        h_lo = sb("h_lo", [P, COLS], F32R)
        hg_hi = sb("hg_hi", [P, 2, CHUNK], F32R)
        hg_lo = sb("hg_lo", [P, 2, CHUNK], F32R)
        gates = sb("gates", [P, TILES, 2 * E], F32R)

        ps = ctx.enter_context(nc.psum_tensor("ps", [P, 8, 512], F32))

        s_const = sem("s_const")
        s_tokin = sem("s_tokin")
        s_idx = sem("s_idx")
        s_txtin = sem("s_txtin")
        s_pos = sem("s_pos")
        s_gather = sem("s_gather")
        s_joint = sem("s_joint")
        s_gate = sem("s_gate")
        s_expert = [sem(f"s_expert{k}") for k in range(STAGE)]
        whi_sb = sem("whi_sb")
        wlo_sb = sem("wlo_sb")
        hhi_sb = sem("hhi_sb")
        hlo_sb = sem("hlo_sb")
        hghi_sb = sem("hghi_sb")
        hglo_sb = sem("hglo_sb")
        s_wqkv, s_wo, s_w1, s_w2 = sem("s_wqkv"), sem("s_wo"), sem("s_w1"), sem("s_w2")
        s_vec, s_row = sem("s_vec"), sem("s_row")
        s_zero = sem("s_zero")
        s_masks = sem("s_masks")
        s_dve = sem("s_dve")
        s_act = sem("s_act")
        noise_ready = sem("noise_ready")
        tokw_ready = sem("tokw_ready")
        tok_psum = sem("tok_psum")
        tok_min = sem("tok_min")
        tok_exp = sem("tok_exp")
        tok_mid = sem("tok_mid")
        tok_out = sem("tok_out")
        img_ready = sem("img_ready")
        x_upd = sem("x_upd")
        ln_stats = sem("ln_stats")
        ln_mv = sem("ln_mv")
        ln_eps = sem("ln_eps")
        ln_rstd = sem("ln_rstd")
        xn_ready = sem("xn_ready")
        xT_psum = sem("xT_psum")
        hT_sb = sem("hT_sb")
        q_psum, k_psum, v_psum, u_psum = sem("q_psum"), sem("k_psum"), sem("v_psum"), sem("u_psum")
        q_sb, k_sb, v_sb, u_sb = sem("q_sb"), sem("k_sb"), sem("v_sb"), sem("u_sb")
        kexp_sb = sem("kexp_sb")
        bias_added = sem("bias_added")
        scores_psum = sem("scores_psum")
        max_sb = sem("max_sb")
        shifted_psum = sem("shifted_psum")
        probs_sb = sem("probs_sb")
        pTa_psum, pTb_psum = sem("pTa_psum"), sem("pTb_psum")
        pTa_sb, pTb_sb = sem("pTa_sb"), sem("pTb_sb")
        o_psum = sem("o_psum")
        rden_sb = sem("rden_sb")
        ctx_sb = sem("ctx_sb")
        c_psum = sem("c_psum")
        ctxT_sb = sem("ctxT_sb")
        wo_psum = sem("wo_psum")
        w1_psum = sem("w1_psum")
        gelu_sb = sem("gelu_sb")
        w2_psum = sem("w2_psum")
        silu_ctx = sem("silu_ctx")
        gated_sb = sem("gated_sb")
        x_joint = sem("x_joint")
        lg_psum = sem("lg_psum")
        aff_sb = sem("aff_sb")
        gates_sb = sem("gates_sb")
        gT_psum = sem("gT_psum")
        gT_sb = sem("gT_sb")
        g_psum, up_psum, gb_psum = sem("g_psum"), sem("up_psum"), sem("gb_psum")
        silu_sb = sem("silu_sb")
        su_sb = sem("su_sb")
        hg_sb = sem("hg_sb")
        d_psum = sem("d_psum")
        oT_sb = sem("oT_sb")
        oT_psum = sem("oT_psum")
        final_sb = sem("final_sb")
        s_out = sem("s_out")

        def kview(slot, nk):
            return k_exp[:, slot, 0:NH * nk].rearrange("p (h k) -> p h k", h=NH)

        def text_units():
            return [Unit(S_TXT, S_TXT, T0 + b * S_TXT, kview(b % 2, S_TXT), v_txt[:, b],
                         mask_l_bf[0:PAD_ROW + 1, :], txt_mask[0:PAD_ROW + 1, b, :],
                         (b % 4) * S_TXT, b) for b in range(B)]

        def joint_units():
            units = []
            for b in range(B):
                keys = kview(b % 2, K_JOINT)
                units.append(Unit(S_IMG, S_IMG, b * S_IMG, keys, v_joint[:, b], ident_bf[0:S_IMG, :],
                                  txt_mask[0:S_IMG, 0, 0:S_IMG], (b % 2) * S_IMG, b))
                units.append(Unit(S_TXT, K_JOINT, T0 + b * S_TXT, keys, v_joint[:, b], ident_bf[0:S_TXT, :],
                                  joint_mask[0:S_TXT, :], 2 * S_IMG + (b % 2) * S_TXT, b))
            return units

        def scores_at(i, u):
            s = 2 * (i % 2)
            return ps[0:u.nq, s:s + 2, 0:4 * u.nk]


        def attend_pe(pe, units, at, kexp_at):
            n = len(units)
            for i in range(n + 3):
                if i < n:
                    u = units[i]
                    pe.wait_ge(kexp_sb, kexp_at(u.kexp_no + 1))
                    if i >= 2:
                        pe.wait_ge(probs_sb, at(i - 1))
                    for half in range(2):
                        s = 2 * (i % 2) + half
                        dst = ps[0:u.nq, s, 0:4 * u.nk]
                        nc.tensor.matmul(dst, qT[:, u.qcol:u.qcol + u.nq],
                                         u.kslot[:, 4 * half:4 * half + 4, 0:u.nk],
                                         start=True, stop=False, skip_group_check=True)
                        last = nc.tensor.matmul(dst, u.mask_l[:, 0:u.nq],
                                                u.mask_r.unsqueeze(1).broadcast_to([u.mask_r.shape[0], 4, u.nk]),
                                                start=False, stop=False, skip_group_check=True)
                    last.then_inc(scores_psum, 1)
                if 0 <= i - 1 < n:
                    u, j = units[i - 1], i - 1
                    pe.wait_ge(probs_sb, at(j + 1))
                    if j >= 1:
                        pe.wait_ge(pTa_sb, at(j))
                    for h in range(NH):
                        if h == 4 and j >= 1:
                            pe.wait_ge(pTb_sb, at(j))
                        last = nc.tensor.transpose(
                            ps[0:u.nk, 4 + h // 4, (h % 4) * u.nq:(h % 4 + 1) * u.nq],
                            probs[0:u.nq, j % 2, h // 4, (h % 4) * u.nk:(h % 4 + 1) * u.nk],
                            ident[0:u.nq, 0:u.nq])
                        if h % 4 == 3:
                            last.then_inc((pTa_psum, pTb_psum)[h // 4], 1)
                if 0 <= i - 2 < n:
                    u, j = units[i - 2], i - 2
                    pe.wait_ge(pTa_sb, at(j + 1))
                    if j >= 1:
                        pe.wait_ge(ctx_sb, at(j))
                    for h in range(NH):
                        if h == 4:
                            pe.wait_ge(pTb_sb, at(j + 1))
                        last = nc.tensor.matmul(
                            ps[0:u.nq, 6, h * VW:(h + 1) * VW],
                            probsT[0:u.nk, j % 2, h // 4, (h % 4) * u.nq:(h % 4 + 1) * u.nq],
                            u.vals[0:u.nk, h, :], start=True, stop=True)
                    last.then_inc(o_psum, 1)
                if i < n:
                    u = units[i]
                    pe.wait_ge(max_sb, at(i + 1))
                    for half in range(2):
                        s = 2 * (i % 2) + half
                        last = nc.tensor.matmul(
                            ps[0:u.nq, s, 0:4 * u.nk], ident_bf[0:u.nq, 0:u.nq],
                            neg_max[0:u.nq, i % 2, 4 * half:4 * half + 4].unsqueeze(2)
                            .broadcast_to([u.nq, 4, u.nk]),
                            start=False, stop=True, skip_group_check=True)
                    last.then_inc(shifted_psum, 1)
                if 0 <= i - 3 < n:
                    u, j = units[i - 3], i - 3
                    pe.wait_ge(ctx_sb, at(j + 1))
                    if j % 4 == 0 and j >= 4:
                        pe.wait_ge(ctxT_sb, at.group(j // 4))
                    nc.tensor.transpose(ps[:, 7, u.c_off:u.c_off + u.nq], ctx_sb_t[0:u.nq, j % 2, :],
                                        ident[0:u.nq, 0:u.nq]).then_inc(c_psum, 1)

        def attend_act(act, units, at, evict_ctx, beside=lambda i: None):
            n = len(units)
            for i in range(n + 3):
                if 0 <= i - 1 < n:
                    u, j = units[i - 1], i - 1
                    act.wait_ge(pTb_psum, at(j + 1))
                    if j >= 2:
                        act.wait_ge(o_psum, at(j - 1))
                    nc.scalar.activation(probsT[0:u.nk, j % 2, 1, 0:4 * u.nq], ps[0:u.nk, 5, 0:4 * u.nq],
                                         ACT.Copy).then_inc(pTb_sb, 1)
                if i < n:
                    u = units[i]
                    act.wait_ge(shifted_psum, at(i + 1))
                    if i >= 2:
                        act.wait_ge(pTb_psum, at(i - 1))
                    nc.scalar.activation(probs[0:u.nq, i % 2, :, 0:4 * u.nk], scores_at(i, u),
                                         ACT.Exp).then_inc(probs_sb, 1)
                if 0 <= i - 3 < n and (i - 3) % 4 == 3:
                    act.wait_ge(c_psum, at(i - 2))
                    evict_ctx((i - 3) // 4)
                beside(i)

        def attend_dve(dve, units, at):
            n = len(units)
            for i in range(n + 2):
                if i < n:
                    u = units[i]
                    dve.wait_ge(scores_psum, at(i + 1))
                    nc.vector.tensor_reduce(
                        neg_max[0:u.nq, i % 2, :].rearrange("p (a h) -> p a h", a=2),
                        scores_at(i, u).rearrange("p a (h k) -> p a h k", h=4),
                        AX.X, ALU.max, negate=True).then_inc(max_sb, 1)
                if 0 <= i - 1 < n:
                    u, j = units[i - 1], i - 1
                    dve.wait_ge(pTa_psum, at(j + 1))
                    if j >= 2:
                        dve.wait_ge(o_psum, at(j - 1))
                    nc.vector.tensor_copy(probsT[0:u.nk, j % 2, 0, 0:4 * u.nq],
                                          ps[0:u.nk, 4, 0:4 * u.nq]).then_inc(pTa_sb, 1)
                if 0 <= i - 2 < n:
                    u, j = units[i - 2], i - 2
                    dve.wait_ge(o_psum, at(j + 1))
                    o = ps[0:u.nq, 6, 0:NH * VW].rearrange("p (h w) -> p h w", h=NH)
                    nc.vector.reciprocal(r_den[0:u.nq, :], o[:, :, HD]).then_inc(rden_sb, 1)
                    dve.wait_ge(rden_sb, at(j + 1))
                    if j >= 2:
                        dve.wait_ge(c_psum, at(j - 1))
                    nc.vector.tensor_tensor(
                        ctx_sb_t[0:u.nq, j % 2, :].rearrange("p (h w) -> p h w", h=NH), o[:, :, 0:HD],
                        r_den[0:u.nq, :].unsqueeze(2).broadcast_to([u.nq, NH, HD]),
                        ALU.mult).then_inc(ctx_sb, 1)

        def spread_keys(slot, nk, parts):
            at, dst = 0, kview(slot, nk)
            for col, n in parts:
                last = nc.gpsimd.tensor_tensor(
                    dst[:, :, at:at + n], kT[:, col:col + n].unsqueeze(1).broadcast_to([P, NH, n]),
                    head_mask.unsqueeze(2).broadcast_to([P, NH, n]), ALU.mult)
                at += n
            last.then_inc(kexp_sb, 1)


        def norm_dve(dve, groups, at):
            for t0, nt in groups:
                for t in range(t0, t0 + nt):
                    last = nc.vector.bn_stats(stats[:, t, :], x_tok[:, t, :])
            last.then_inc(ln_stats, 1)
            dve.wait_ge(ln_stats, at.norm())
            nc.vector.memset(wait_carrier[:], 0.0)
            for t0, nt in groups:
                for t in range(t0, t0 + nt):
                    last = nc.vector.bn_aggr(mv[:, t, :], stats[:, t, :])
                last.then_inc(ln_mv, 1)
            for k, (t0, nt) in enumerate(groups):
                dve.wait_ge(ln_rstd, at(k + 1))
                for t in range(t0, t0 + nt):
                    last = nc.vector.tensor_scalar(x_norm[:, t, :], x_tok[:, t, :], mv[:, t, 0:1],
                                                   rstd[:, t:t + 1], ALU.subtract, ALU.mult)
                last.then_inc(xn_ready, 1)

        def norm_pool(pool, groups, at):
            for k, (t0, nt) in enumerate(groups):
                s = slice(t0, t0 + nt)
                pool.wait_ge(ln_mv, at(k + 1))
                nc.gpsimd.tensor_tensor(veps[:, s], mv[:, s, 1], eps_t[:, s], ALU.add).then_inc(ln_eps, 1)
                pool.wait_ge(ln_eps, at(k + 1))
                nc.gpsimd.tensor_tensor(rstd[:, s], veps[:, s], half_t[:, s], ALU.pow).then_inc(ln_rstd, 1)

        def norm_pe(pe, groups, xn_at, banks):
            for k, (t0, nt) in enumerate(groups):
                pe.wait_ge(xn_ready, xn_at(k + 1))
                for t in range(t0, t0 + nt):
                    last = nc.tensor.transpose(ps[:, banks[k], (t - t0) * P:(t - t0 + 1) * P],
                                               x_norm[:, t, :], ident)
                last.then_inc(xT_psum, 1)

        def project_tokens(weights, src, t0, nt, b):
            for t in range(t0, t0 + nt):
                last = nc.tensor.matmul(ps[:, b, (t - t0) * P:(t - t0 + 1) * P], src[:, t * P:(t + 1) * P],
                                        weights, start=True, stop=True)
            return last

        def row_of(r, n, rows=P):
            return r[0:rows].unsqueeze(1).broadcast_to([rows, n, r.shape[1]])

        block = ctx.enter_context(nc.Block())

        @block.sync
        def _(sp):
            sp.dma_start(const[:], a["const"]).then_inc(s_const, 16)
            sp.dma_start(idx[:, 0:TXT_TILES - 1],
                         a["tokens"]).then_inc(s_idx, 16)
            sp.dma_start(idx[0:LAST_ROWS, TXT_TILES - 1:TXT_TILES],
                         a["tokens_end"]).then_inc(s_idx, 16)
            sp.dma_start(noise[:, 0:6], a["noise_cols"]).then_inc(s_tokin, 16)
            sp.dma_start(noise[:, 6:6 + 2 * D], a["noise_rows"].broadcast_to([P, 2 * D])).then_inc(s_tokin, 16)
            sp.dma_start(tok_w[:].rearrange("p m c o -> p (m c o)"), a["tok_w"]).then_inc(s_tokin, 16)
            sp.dma_start(tok_sw[:].rearrange("p m c o -> p (m c o)"), a["tok_sw"]).then_inc(s_tokin, 16)
            sp.dma_start(tok_w3[:], a["tok_w3"]).then_inc(s_tokin, 16)
            sp.dma_start(tok_b[:], a["tok_b"]).then_inc(s_tokin, 16)
            sp.dma_start(patches[:].rearrange("p c t -> p (c t)"), a["patches"]).then_inc(s_tokin, 16)
            sp.dma_start(jrow[:], a["jrow"].broadcast_to([P, JR_ALL])).then_inc(s_joint, 16)
            sp.dma_start(pad_in[PAD_ROW:PAD_ROW + 1, :], a["pad_row"]).then_inc(s_txtin, 16)
            sp.dma_start(pad_col[0:S_TXT, :], a["pad_col"]).then_inc(s_txtin, 16)
            n9 = (TXT_TILES - 1) * P
            sp.dma_start(x_norm[:, IMG_TILES:TILES - 1, :],
                         a["pos"][0:n9, :].rearrange("(t p) d -> p t d", p=P)).then_inc(s_pos, 16)
            sp.dma_start(x_norm[0:LAST_ROWS, TILES - 1, :], a["pos"][n9:TXT_TOKENS, :]).then_inc(s_pos, 16)
            sp.dma_start(w_qkv_t[:], a["w_qkv"][0:P, :]).then_inc(s_wqkv, 16)
            sp.dma_start(vec[:], a["vec"][0:P, :]).then_inc(s_vec, 16)
            sp.dma_start(row[:], a["row"][0:1, :].broadcast_to([P, 3 * D])).then_inc(s_row, 16)
            sp.dma_start(w_o_t[:], a["w_o"][0:P, :]).then_inc(s_wo, 16)
            sp.dma_start(w_1_t[:], a["w_1"][0:P, :]).then_inc(s_w1, 16)
            sp.dma_start(w_2_t[:].rearrange("p f d -> p (f d)"), a["w_2"][0:P, :]).then_inc(s_w2, 16)
            with sp.Fori(1, LAYERS) as l:
                lo = l * P
                sp.wait_ge(v_psum, l * 4)
                sp.dma_start(w_qkv_t[:], a["w_qkv"][bass.ds(lo, P), :]).then_inc(s_wqkv, 16)
                sp.wait_ge(wo_psum, l * NG)
                sp.dma_start(w_o_t[:], a["w_o"][bass.ds(lo, P), :]).then_inc(s_wo, 16)
                sp.wait_ge(w1_psum, l * (NG * FF))
                sp.dma_start(w_1_t[:], a["w_1"][bass.ds(lo, P), :]).then_inc(s_w1, 16)
                sp.wait_ge(gelu_sb, l * (NG * FF))
                sp.dma_start(vec[:], a["vec"][bass.ds(lo, P), :]).then_inc(s_vec, 16)
                sp.wait_ge(bias_added, l * 2)
                sp.dma_start(row[:], a["row"][bass.ds(l, 1), :].broadcast_to([P, 3 * D])).then_inc(s_row, 16)
                sp.wait_ge(w2_psum, l * NG)
                sp.dma_start(w_2_t[:].rearrange("p f d -> p (f d)"), a["w_2"][bass.ds(lo, P), :]
                             ).then_inc(s_w2, 16)
            sp.wait_ge(w2_psum, LAYERS * NG)
            sp.wait_ge(bias_added, LAYERS * 2)
            for e in range(E + 1):
                if e >= STAGE:
                    sp.wait_ge(wlo_sb, e - STAGE + 1)
                    sp.wait_ge(whi_sb, e - STAGE + 1)
                sp.dma_start(w_stage[:, e % STAGE, :], a["w_exp"][e * P:(e + 1) * P, :]
                             ).then_inc(s_expert[e % STAGE], 16)
            with sp.Fori(0, CHUNKS) as c:
                sp.wait_ge(final_sb, c + 2)
                sp.dma_start(out[bass.ds(c * CHUNK, CHUNK), :].rearrange("(t p) d -> p t d", p=P),
                             x_tok[:, bass.ds(c * CHUNK_TILES, CHUNK_TILES), :]).then_inc(s_out, 16)
            sp.wait_ge(s_out, 16 * CHUNKS)

        @block.gpsimd
        def _(pool):
            nc.gpsimd.memset(x_tok[:, TILES - 1, :], 0.0).then_inc(s_zero, 1)
            pool.wait_ge(s_idx, 32)
            pool.wait_ge(s_zero, 1)
            for t in range(TXT_TILES):
                rows = P if t < TXT_TILES - 1 else LAST_ROWS
                pool.indirect_dma_start(
                    out=x_tok[0:rows, IMG_TILES + t, :], out_offset=None, in_=a["item_emb"],
                    in_offset=bass.IndirectOffsetOnAxis(ap=idx[0:rows, t:t + 1], axis=0)
                ).then_inc(s_gather, 16)
            nc.gpsimd.memset(ctxT[:, T0 + TXT_TOKENS:COLS], 0.0).then_inc(s_zero, 1)
            nc.gpsimd.memset(eps_t[:], EPS).then_inc(s_zero, 1)
            nc.gpsimd.memset(half_t[:], -0.5).then_inc(s_zero, 1)
            nc.gpsimd.memset(v_joint[:], 1.0).then_inc(s_zero, 1)
            nc.gpsimd.memset(gateT[:].bitcast(F32), 0.0).then_inc(s_zero, 1)
            pool.wait_ge(s_zero, 6)
            pool.wait_ge(s_const, 16)
            with pool.Fori(0, LAYERS) as l:
                norm_pool(pool, TXT_GROUPS, lambda k: l * (2 * NG) + k)
                for b in range(B):
                    if b == 0:
                        pool.wait_ge(k_sb, l * NG + NG)
                    if b >= 2:
                        pool.wait_ge(scores_psum, l * B + (b - 1))
                    spread_keys(b % 2, S_TXT, [(T0 + b * S_TXT, S_TXT)])
                    if b == 3:
                        pool.wait_ge(xn_ready, l * (2 * NG) + NG)
                        pool.wait_ge(s_row, l * 16 + 16)
                        nc.gpsimd.tensor_tensor(x_tok[:, IMG_TILES:, :], x_tok[:, IMG_TILES:, :],
                                                row_of(row[:, R_BO:R_BO + D], TXT_TILES),
                                                ALU.add).then_inc(bias_added, 1)
                norm_pool(pool, TXT_GROUPS, lambda k: l * (2 * NG) + NG + k)
                pool.wait_ge(xn_ready, l * (2 * NG) + 2 * NG)
                nc.gpsimd.tensor_tensor(x_tok[:, IMG_TILES:, :], x_tok[:, IMG_TILES:, :],
                                        row_of(row[:, R_B2:R_B2 + D], TXT_TILES),
                                        ALU.add).then_inc(bias_added, 1)
            base = LAYERS * 2 * NG
            norm_pool(pool, TXT_GROUPS, lambda k: base + k)
            norm_pool(pool, ALL_GROUPS, lambda k: base + NG + k)
            for b in range(B):
                if b == 0:
                    pool.wait_ge(k_sb, LAYERS * NG + NA)
                if b >= 2:
                    pool.wait_ge(scores_psum, LAYERS * B + 2 * (b - 1))
                spread_keys(b % 2, K_JOINT, [(b * S_IMG, S_IMG), (T0 + b * S_TXT, K_JOINT - S_IMG)])
                if b == 3:
                    pool.wait_ge(xn_ready, base + NG + NA)
                    pool.wait_ge(s_joint, 48)
                    nc.gpsimd.tensor_tensor(x_tok[:], x_tok[:], row_of(jrow[:, JR_BO:JR_BO + D], TILES),
                                            ALU.add).then_inc(bias_added, 1)
                for e in range(max(b - 2, 0), b - 1 if b < B - 1 else E + 1):
                    pool.wait_ge(whi_sb, e + 1)
                    nc.gpsimd.tensor_tensor(w_lo[:, e, :], w_stage[:, e % STAGE, :], w_hi[:, e, :].bitcast(F32),
                                            ALU.subtract).then_inc(wlo_sb, 1)
            norm_pool(pool, ALL_GROUPS, lambda k: base + NG + NA + k)
            for g, (t0, nt) in enumerate(ALL_GROUPS):
                s = slice(t0 * P, (t0 + nt) * P)
                pool.wait_ge(hhi_sb, g + 1)
                nc.gpsimd.tensor_tensor(h_lo[:, s], hT[:, s], h_hi[:, s].bitcast(F32),
                                        ALU.subtract).then_inc(hlo_sb, 1)
            n = 2 * (E + 1)
            with pool.Fori(0, CHUNKS // 2) as c:
                for p in range(n):
                    pool.wait_ge(hghi_sb, c * n + (p + 1))
                    if p >= 2:
                        pool.wait_ge(d_psum, c * n + (p - 1))
                    nc.gpsimd.tensor_tensor(hg_lo[:, p % 2, :], hg_t[:, p % 2, :], hg_hi[:, p % 2, :].bitcast(F32),
                                            ALU.subtract).then_inc(hglo_sb, 1)

        @block.scalar
        def _(act):
            act.dma_start(jw[:], a["jw"]).then_inc(s_joint, 16)
            act.dma_start(jvec[:], a["jvec"]).then_inc(s_joint, 16)
            act.dma_start(w_gate[:], a["w_gate"]).then_inc(s_gate, 16)
            act.wait_ge(s_tokin, 16 * 7)
            nc.scalar.activation(noise_abs[:], noise[:], ACT.Abs).then_inc(s_act, 1)
            nc.scalar.activation(noise_sign[:], noise[:], ACT.Sign).then_inc(s_act, 1)
            act.wait_ge(s_act, 2)
            nc.scalar.activation(noise_root[:], noise_abs[:], ACT.Sqrt).then_inc(noise_ready, 1)
            for c in range(2):
                act.wait_ge(tok_min, c + 1)
                nc.scalar.activation(gelu_t[:, 0, 2 * c, :], gelu_t[:, 0, 2 * c + 1, :],
                                     ACT.Exp).then_inc(tok_exp, 1)

            def text_ctx(g):
                w = 4 * S_TXT
                nc.scalar.activation(ctxT[:, T0 + g * w:T0 + (g + 1) * w], ps[:, 7, 0:w],
                                     ACT.Copy).then_inc(ctxT_sb, 1)

            def joint_ctx(g):
                wi, wt = 2 * S_IMG, 2 * S_TXT
                nc.scalar.activation(ctxT[:, g * wi:(g + 1) * wi], ps[:, 7, 0:wi], ACT.Copy)
                nc.scalar.activation(ctxT[:, T0 + g * wt:T0 + (g + 1) * wt], ps[:, 7, wi:wi + wt],
                                     ACT.Copy).then_inc(ctxT_sb, 1)

            def norm_out(groups, at, banks, gain, shift):
                for k, (t0, nt) in enumerate(groups):
                    act.wait_ge(xT_psum, at(k + 1))
                    dst, src = hT[:, t0 * P:(t0 + nt) * P], ps[:, banks[k], 0:nt * P]
                    if gain is None:
                        ins = nc.scalar.activation(dst, src, ACT.Copy)
                    else:
                        ins = nc.scalar.activation(dst, src, ACT.Identity, bias=shift, scale=gain)
                    ins.then_inc(hT_sb, 1)

            with act.Fori(0, LAYERS) as l:
                act.wait_ge(s_vec, l * 16 + 16)
                norm_out(TXT_GROUPS, lambda k: l * (2 * NG) + k, (0, 1, 2),
                         vec[:, V_G1:V_G1 + 1], vec[:, V_B1:V_B1 + 1])
                for g, (t0, nt) in enumerate(TXT_GROUPS):
                    act.wait_ge(k_psum, l * NG + (g + 1))
                    nc.scalar.activation(kT[:, t0 * P:(t0 + nt) * P], ps[:, (6, 7, 0)[g], 0:nt * P],
                                         ACT.Identity, bias=vec[:, V_BK:V_BK + 1]).then_inc(k_sb, 1)
                attend_act(act, text_units(), lambda k: l * B + k, text_ctx)
                norm_out(TXT_GROUPS, lambda k: l * (2 * NG) + NG + k, (0, 1, 2),
                         vec[:, V_G2:V_G2 + 1], vec[:, V_B2:V_B2 + 1])
                for g, (t0, nt) in enumerate(TXT_GROUPS):
                    if g == 2:
                        act.wait_ge(w2_psum, l * NG + 1)
                    for f in range(FF):
                        j = g * FF + f
                        act.wait_ge(w1_psum, l * (NG * FF) + (j + 1))
                        nc.scalar.activation(gelu_t[:, g % 2, f, 0:nt * P], ps[:, (6, 7, 0, 1, 2)[j % 5], 0:nt * P],
                                             ACT.Gelu, bias=vec[:, V_BF + f:V_BF + f + 1]).then_inc(gelu_sb, 1)
            base = LAYERS * 2 * NG
            act.wait_ge(s_joint, 48)
            norm_out(ALL_GROUPS, lambda k: base + k, (0, 1, 2, 3, 4), None, None)
            for g, (t0, nt) in enumerate(ALL_GROUPS):
                act.wait_ge(k_psum, LAYERS * NG + g + 1)
                nc.scalar.activation(kT[:, t0 * P:(t0 + nt) * P], ps[:, 6, 0:nt * P], ACT.Identity,
                                     bias=jvec[:, JV_BK:JV_BK + 1]).then_inc(k_sb, 1)
                act.wait_ge(u_psum, g + 1)
                nc.scalar.activation(uT[:, t0 * P:(t0 + nt) * P], ps[:, 7, 0:nt * P], ACT.Identity,
                                     bias=jvec[:, JV_BU:JV_BU + 1]).then_inc(u_sb, 1)

            def split_weights(i):
                if i >= 2 and i % 2 == 0:
                    e = i // 2 - 1
                    act.wait_ge(s_expert[e % STAGE], 16 * (e // STAGE + 1))
                    nc.scalar.activation(w_hi[:, e, :], w_stage[:, e % STAGE, :], ACT.Copy).then_inc(whi_sb, 1)

            attend_act(act, joint_units(), lambda k: LAYERS * B + k, joint_ctx, split_weights)
            act.wait_ge(ctxT_sb, LAYERS * 4 + 8)
            for g, (t0, nt) in enumerate(ALL_GROUPS):
                nc.scalar.activation(hT[:, t0 * P:(t0 + nt) * P], ctxT[:, t0 * P:(t0 + nt) * P],
                                     ACT.Silu).then_inc(silu_ctx, 1)
            norm_out(ALL_GROUPS, lambda k: base + NA + k, (0, 1, 2, 3, 4), None, None)
            for g, (t0, nt) in enumerate(ALL_GROUPS):
                s = slice(t0 * P, (t0 + nt) * P)
                act.wait_ge(hT_sb, base + NA + g + 1)
                nc.scalar.activation(h_hi[:, s], hT[:, s], ACT.Copy).then_inc(hhi_sb, 1)
            act.wait_ge(lg_psum, 1)
            nc.scalar.activation(kT[:, 0:TILES * E], ps[:, 5, 0:TILES * E],
                                 ACT.Sigmoid).then_inc(aff_sb, 1)
            for g, (t0, nt) in enumerate(ALL_GROUPS):
                act.wait_ge(gT_psum, g + 1)
                nc.scalar.activation(gateT[0:2 * E, t0 * P:(t0 + nt) * P], ps[0:2 * E, (6, 7, 0, 1, 2)[g], 0:nt * P],
                                     ACT.Copy).then_inc(gT_sb, 1)
            n = 2 * (E + 1)
            with act.Fori(0, CHUNKS // 2) as c:
                for p in range(n + 4):
                    if p < n:
                        act.wait_ge(g_psum, c * n + (p + 1))
                        if p >= 2:
                            act.wait_ge(su_sb, c * n + (p - 1))
                        nc.scalar.activation(silu_t[:, p % 2, :], ps[:, p % 2, 0:CHUNK],
                                             ACT.Silu).then_inc(silu_sb, 1)
                    if 0 <= p - 1 < n:
                        j = p - 1
                        act.wait_ge(hg_sb, c * n + (j + 1))
                        if j >= 2:
                            act.wait_ge(d_psum, c * n + (j - 1))
                        nc.scalar.activation(hg_hi[:, j % 2, :], hg_t[:, j % 2, :], ACT.Copy).then_inc(hghi_sb, 1)
                    if p >= 3 and (p - 3) % (E + 1) == E:
                        k = (p - 3) // (E + 1)
                        act.wait_ge(d_psum, c * n + (k + 1) * (E + 1))
                        if k == 1:
                            act.wait_ge(oT_psum, c * 2 + 1)
                        nc.scalar.activation(oT_t[:], ps[:, 6 + k, 0:CHUNK], ACT.Copy).then_inc(oT_sb, 1)

        @block.tensor
        def _(pe):
            pe.wait_ge(tokw_ready, 1)
            pe.wait_ge(s_const, 16)
            for c in range(2):
                for m in range(2):
                    for h in range(2):
                        last = nc.tensor.matmul(ps[:, 2 * m + c, :], tok_w[:, m, h, :],
                                                patches[:, h, c * 512:(c + 1) * 512],
                                                start=(h == 0), stop=(h == 1))
                last.then_inc(tok_psum, 1)
            for c in range(2):
                pe.wait_ge(tok_mid, c + 1)
                project_tokens(tok_w3[:], gelu_t[:, 1, 0:2, :].rearrange("p a t -> p (a t)"), 4 * c, 4,
                               4 + c).then_inc(tok_out, 1)
            pe.wait_ge(img_ready, 2)
            pe.wait_ge(s_masks, 1)

            with pe.Fori(0, LAYERS) as l:
                norm_pe(pe, TXT_GROUPS, lambda k: l * (2 * NG) + k, (0, 1, 2))
                pe.wait_ge(s_wqkv, l * 16 + 16)
                for g, (t0, nt) in enumerate(TXT_GROUPS):
                    pe.wait_ge(hT_sb, l * (2 * NG) + (g + 1))
                    rhs = hT[:, t0 * P:(t0 + nt) * P]
                    nc.tensor.matmul(ps[:, 3 + g, 0:nt * P], w_qkv_t[:, 0:D], rhs,
                                     start=True, stop=True).then_inc(q_psum, 1)
                    nc.tensor.matmul(ps[:, (6, 7, 0)[g], 0:nt * P], w_qkv_t[:, D:2 * D], rhs,
                                     start=True, stop=True).then_inc(k_psum, 1)
                for j in range(4):
                    if j >= 2:
                        pe.wait_ge(q_sb, l * NG + (j - 1))
                    for b in range(4 * j, 4 * j + 4):
                        col = T0 + b * S_TXT
                        last = nc.tensor.matmul(ps[0:S_TXT, 1 + j, (b % 4) * D:(b % 4 + 1) * D],
                                                hT[:, col:col + S_TXT], w_qkv_t[:, 2 * D:3 * D],
                                                start=True, stop=True)
                    last.then_inc(v_psum, 1)
                pe.wait_ge(q_sb, l * NG + NG)
                pe.wait_ge(k_sb, l * NG + NG)
                pe.wait_ge(v_sb, l * 4 + 4)
                attend_pe(pe, text_units(), Passed(l), lambda k: l * B + k)
                pe.wait_ge(s_wo, l * 16 + 16)
                pe.wait_ge(ctxT_sb, l * 4 + 4)
                for g, (t0, nt) in enumerate(TXT_GROUPS):
                    project_tokens(w_o_t[:], ctxT, t0, nt, 3 + g).then_inc(wo_psum, 1)
                norm_pe(pe, TXT_GROUPS, lambda k: l * (2 * NG) + NG + k, (0, 1, 2))

                def hidden(g):
                    t0, nt = TXT_GROUPS[g]
                    pe.wait_ge(hT_sb, l * (2 * NG) + NG + (g + 1))
                    for f in range(FF):
                        j = g * FF + f
                        if j == 3:
                            pe.wait_ge(hT_sb, l * (2 * NG) + NG + 2)
                        if j == 4:
                            pe.wait_ge(hT_sb, l * (2 * NG) + NG + 3)
                        if j >= 5:
                            pe.wait_ge(gelu_sb, l * (NG * FF) + (j - 4))
                        nc.tensor.matmul(ps[:, (6, 7, 0, 1, 2)[j % 5], 0:nt * P], w_1_t[:, f * D:(f + 1) * D],
                                         hT[:, t0 * P:(t0 + nt) * P], start=True, stop=True
                                         ).then_inc(w1_psum, 1)

                def ffn_out(g):
                    t0, nt = TXT_GROUPS[g]
                    pe.wait_ge(gelu_sb, l * (NG * FF) + FF * (g + 1))
                    for t in range(nt):
                        for f in range(FF):
                            last = nc.tensor.matmul(ps[:, 3 + g, t * P:(t + 1) * P],
                                                    gelu_t[:, g % 2, f, t * P:(t + 1) * P], w_2_t[:, f, :],
                                                    start=(f == 0), stop=(f == FF - 1))
                    last.then_inc(w2_psum, 1)

                pe.wait_ge(s_w1, l * 16 + 16)
                hidden(0)
                hidden(1)
                pe.wait_ge(s_w2, l * 16 + 16)
                ffn_out(0)
                hidden(2)
                ffn_out(1)
                ffn_out(2)
            base = LAYERS * 2 * NG
            norm_pe(pe, ALL_GROUPS, lambda k: base + NG + k, (0, 1, 2, 3, 4))
            pe.wait_ge(s_joint, 48)
            for g, (t0, nt) in enumerate(ALL_GROUPS):
                pe.wait_ge(hT_sb, base + g + 1)
                rhs = hT[:, t0 * P:(t0 + nt) * P]
                for m, b, psum_sem, sb_sem in ((0, 5, q_psum, q_sb), (1, 6, k_psum, k_sb), (3, 7, u_psum, u_sb)):
                    if g >= 1:
                        before = 0 if m == 3 else LAYERS * NG
                        pe.wait_ge(sb_sem, before + g)
                    nc.tensor.matmul(ps[:, b, 0:nt * P], jw[:, m * D:(m + 1) * D], rhs,
                                     start=True, stop=True).then_inc(psum_sem, 1)
            for j in range(4):
                for b in range(4 * j, 4 * j + 4):
                    s = slice((b % 4) * D, (b % 4 + 1) * D)
                    nc.tensor.matmul(ps[0:S_IMG, 1 + j, s], hT[:, b * S_IMG:(b + 1) * S_IMG],
                                     jw[:, 2 * D:3 * D], start=True, stop=True)
                    col = T0 + b * S_TXT
                    last = nc.tensor.matmul(ps[S_IMG:K_JOINT, 1 + j, s], hT[:, col:col + K_JOINT - S_IMG],
                                            jw[:, 2 * D:3 * D], start=True, stop=True)
                last.then_inc(v_psum, 1)
            pe.wait_ge(q_sb, LAYERS * NG + NA)
            pe.wait_ge(k_sb, LAYERS * NG + NA)
            pe.wait_ge(u_sb, NA)
            pe.wait_ge(v_sb, LAYERS * 4 + 4)
            attend_pe(pe, joint_units(), Passed(LAYERS), lambda k: LAYERS * B + k)
            for g, (t0, nt) in enumerate(ALL_GROUPS):
                pe.wait_ge(gated_sb, g + 1)
                project_tokens(jw[:, 4 * D:5 * D], uT, t0, nt, 3 + g).then_inc(wo_psum, 1)
            norm_pe(pe, ALL_GROUPS, lambda k: base + NG + NA + k, (0, 1, 2, 3, 4))
            pe.wait_ge(s_gate, 16)
            pe.wait_ge(hT_sb, base + 2 * NA)
            for t in range(TILES):
                last = nc.tensor.matmul(ps[:, 5, t * E:(t + 1) * E], hT[:, t * P:(t + 1) * P], w_gate[:],
                                        start=True, stop=True)
            last.then_inc(lg_psum, 1)
            pe.wait_ge(gates_sb, 1)
            for g, (t0, nt) in enumerate(ALL_GROUPS):
                for t in range(t0, t0 + nt):
                    last = nc.tensor.transpose(ps[0:2 * E, (6, 7, 0, 1, 2)[g], (t - t0) * P:(t - t0 + 1) * P],
                                               gates[:, t, :].bitcast(F32), ident)
                last.then_inc(gT_psum, 1)
            pe.wait_ge(gT_sb, NA)
            pe.wait_ge(hlo_sb, NA)
            pe.wait_ge(wlo_sb, E + 1)
            n = 2 * (E + 1)

            def split_product(dst, w, e, x_hi, x_lo, start=True, stop=True):
                nc.tensor.matmul(dst, w_lo[:, e, w * D:(w + 1) * D], x_hi, start=start, stop=False)
                nc.tensor.matmul(dst, w_hi[:, e, w * D:(w + 1) * D], x_hi, start=False, stop=False)
                return nc.tensor.matmul(dst, w_hi[:, e, w * D:(w + 1) * D], x_lo, start=False, stop=stop)

            with pe.Fori(0, CHUNKS // 2) as c:
                for p in range(n + 4):
                    k, e = divmod(p, E + 1)
                    if p < n:
                        tok = bass.ds(c * (2 * CHUNK) + k * CHUNK, CHUNK)
                        if p >= 2:
                            pe.wait_ge(silu_sb, c * n + (p - 1))
                        split_product(ps[:, p % 2, 0:CHUNK], 0, e, h_hi[:, tok], h_lo[:, tok]
                                      ).then_inc(g_psum, 1)
                        if p >= 2:
                            pe.wait_ge(su_sb, c * n + (p - 1))
                        split_product(ps[:, 2 + p % 2, 0:CHUNK], 1, e, h_hi[:, tok], h_lo[:, tok]
                                      ).then_inc(up_psum, 1)
                        if e < E:
                            if p >= 2:
                                pe.wait_ge(hg_sb, c * n + (p - 1))
                            nc.tensor.matmul(ps[:, 4 + p % 2, 0:CHUNK], select[:, e, :], gateT[:, tok],
                                             start=True, stop=True).then_inc(gb_psum, 1)
                    if 0 <= p - 2 < n:
                        j = p - 2
                        kj, ej = divmod(j, E + 1)
                        pe.wait_ge(hglo_sb, c * n + (j + 1))
                        if ej == 0 and kj == 0:
                            pe.wait_ge(final_sb, c * 2 + 1)
                        split_product(ps[:, 6 + kj, 0:CHUNK], 2, ej, hg_hi[:, j % 2, :], hg_lo[:, j % 2, :],
                                      start=(ej == 0), stop=(ej == E)).then_inc(d_psum, 1)
                    if p >= 4 and (p - 4) % (E + 1) == E:
                        kj = (p - 4) // (E + 1)
                        pe.wait_ge(oT_sb, c * 2 + (kj + 1))
                        for t in range(CHUNK_TILES):
                            last = nc.tensor.transpose(ps[:, 6 + kj, t * P:(t + 1) * P],
                                                       oT_t[:, t * P:(t + 1) * P], ident)
                        last.then_inc(oT_psum, 1)

        @block.vector
        def _(dve):
            chain = [0]

            def link(ins):
                chain[0] += 1
                ins.then_inc(s_dve, 1)
                dve.wait_ge(s_dve, chain[0])

            dve.wait_ge(s_const, 16)
            dve.wait_ge(s_txtin, 32)
            nc.vector.tensor_copy(ident_bf[:], ident)
            nc.vector.tensor_copy(mask_l_bf[:], const[:, C_MASKL:C_MASKL + S_TXT])
            nc.vector.tensor_copy(joint_mask[:], const[:, C_JOINT:C_JOINT + K_JOINT])
            nc.vector.tensor_copy(txt_mask[0:PAD_ROW], row_of(const[:, C_CAUSAL:C_CAUSAL + S_TXT], B, PAD_ROW))
            r = slice(PAD_ROW, PAD_ROW + 1)
            nc.vector.tensor_scalar(txt_mask[r].rearrange("p b k -> p (b k)"), pad_in[r, :], 0.0, FAR,
                                    ALU.is_equal, ALU.mult)
            link(nc.vector.tensor_scalar(pad_col1[0:S_TXT, :], pad_col[0:S_TXT, :], 0.0, -1.0,
                                         ALU.is_equal, ALU.mult))
            nc.vector.tensor_scalar(
                v_txt[0:S_TXT, :, :, HD], pad_col1[0:S_TXT, :].unsqueeze(2).broadcast_to([S_TXT, B, NH]),
                1.0, None, ALU.add)
            link(nc.vector.tensor_tensor(gsum[:, 0:E], ident[:, 0:E], ident[:, E:2 * E], ALU.add))
            nc.vector.tensor_copy(select[:], gsum[:, 0:E].unsqueeze(2).broadcast_to([P, E, P])
                                  ).then_inc(s_masks, 1)
            dve.wait_ge(noise_ready, 1)
            dve.wait_ge(s_tokin, 16 * 7)
            link(nc.vector.tensor_tensor(noise[:], noise_root[:], noise_sign[:], ALU.mult))
            for m in range(2):
                for h in range(2):
                    nc.vector.scalar_tensor_tensor(
                        tok_sw[:, m, h, :], tok_sw[:, m, h, :], noise[:, 2 * m + h:2 * m + h + 1],
                        noise[:, 6 + m * D:6 + (m + 1) * D], ALU.mult, ALU.mult)
                last = nc.vector.scalar_tensor_tensor(tok_bn[:, m:m + 1], tok_b[:, 2 * m + 1:2 * m + 2],
                                                      noise[:, 4 + m:5 + m], tok_b[:, 2 * m:2 * m + 1],
                                                      ALU.mult, ALU.add)
            link(last)
            dve.wait_ge(s_joint, 48)
            nc.vector.tensor_tensor(tok_w[:], tok_w[:], tok_sw[:], ALU.add).then_inc(tokw_ready, 1)
            nc.vector.tensor_tensor(pos_b[:], const[:, C_POS:C_POS + D], jrow[:, JR_W3B:JR_W3B + D], ALU.add)
            dve.wait_ge(s_gather, 16 * TXT_TILES)
            dve.wait_ge(s_pos, 32)
            m = slice(IMG_TILES, TILES - 1)
            nc.vector.tensor_tensor(x_tok[:, m, :], x_tok[:, m, :], x_norm[:, m, :], ALU.add)
            nc.vector.tensor_tensor(x_tok[0:LAST_ROWS, TILES - 1, :], x_tok[0:LAST_ROWS, TILES - 1, :],
                                    x_norm[0:LAST_ROWS, TILES - 1, :], ALU.add).then_inc(x_upd, 1)
            for c in range(2):
                dve.wait_ge(tok_psum, c + 1)
                nc.vector.tensor_scalar(gelu_t[:, 0, 2 * c + 1, :], ps[:, c, :], tok_bn[:, 0:1], EXP_CAP,
                                        ALU.add, ALU.min).then_inc(tok_min, 1)
            for c in range(2):
                dve.wait_ge(tok_exp, c + 1)
                t = gelu_t[:, 0, 2 * c, :]
                w2 = gelu_t[:, 0, 2 * c + 1, :]
                w = gelu_t[:, 1, 2, :]
                link(nc.vector.scalar_tensor_tensor(w, t, 2.0, t, ALU.add, ALU.mult))
                link(nc.vector.tensor_scalar(w2, w, 2.0, None, ALU.add))
                link(nc.vector.reciprocal(t, w2))
                link(nc.vector.tensor_tensor(w2, w, t, ALU.mult))
                link(nc.vector.scalar_tensor_tensor(t, ps[:, c, :], tok_bn[:, 0:1], w2, ALU.add, ALU.mult))
                nc.vector.scalar_tensor_tensor(gelu_t[:, 1, c, :], ps[:, 2 + c, :], tok_bn[:, 1:2], t,
                                               ALU.add, ALU.mult).then_inc(tok_mid, 1)
            for c in range(2):
                dve.wait_ge(tok_out, c + 1)
                nc.vector.tensor_tensor(x_tok[:, 4 * c:4 * c + 4, :],
                                        ps[:, 4 + c, :].rearrange("p (t d) -> p t d", t=4),
                                        row_of(pos_b[:], 4), ALU.add).then_inc(img_ready, 1)

            def add_back(groups, signal, psum_at, psum_sem):
                for g, (t0, nt) in enumerate(groups):
                    dve.wait_ge(psum_sem, psum_at(g + 1))
                    nc.vector.tensor_tensor(x_tok[:, t0:t0 + nt, :], x_tok[:, t0:t0 + nt, :],
                                            ps[:, 3 + g, 0:nt * P].rearrange("p (t d) -> p t d", t=nt),
                                            ALU.add).then_inc(signal, 1)

            with dve.Fori(0, LAYERS) as l:
                dve.wait_ge(x_upd, l * (2 * NG) + 1)
                norm_dve(dve, TXT_GROUPS, Norms(l * (2 * NG), l * 2))
                dve.wait_ge(s_row, l * 16 + 16)
                dve.wait_ge(s_vec, l * 16 + 16)
                for g, (t0, nt) in enumerate(TXT_GROUPS):
                    dve.wait_ge(q_psum, l * NG + (g + 1))
                    nc.vector.tensor_scalar(qT[:, t0 * P:(t0 + nt) * P], ps[:, 3 + g, 0:nt * P],
                                            vec[:, V_BQ:V_BQ + 1], float(Q_SCALE), ALU.add, ALU.mult
                                            ).then_inc(q_sb, 1)
                for j in range(4):
                    dve.wait_ge(v_psum, l * 4 + (j + 1))
                    nc.vector.tensor_tensor(
                        v_txt[0:S_TXT, 4 * j:4 * j + 4, :, 0:HD],
                        ps[0:S_TXT, 1 + j, :].rearrange("p (b h w) -> p b h w", b=4, w=HD),
                        row[0:S_TXT, R_BV:R_BV + D].rearrange("p (h w) -> p h w", w=HD).unsqueeze(1)
                        .broadcast_to([S_TXT, 4, NH, HD]), ALU.add).then_inc(v_sb, 1)
                attend_dve(dve, text_units(), lambda k: l * B + k)
                dve.wait_ge(bias_added, l * 2 + 1)
                add_back(TXT_GROUPS, x_upd, lambda k: l * NG + k, wo_psum)
                dve.wait_ge(x_upd, l * (2 * NG) + (NG + 1))
                norm_dve(dve, TXT_GROUPS, Norms(l * (2 * NG) + NG, l * 2 + 1))
                dve.wait_ge(bias_added, l * 2 + 2)
                add_back(TXT_GROUPS, x_upd, lambda k: l * NG + k, w2_psum)
            base = LAYERS * 2 * NG
            dve.wait_ge(x_upd, base + 1)
            norm_dve(dve, TXT_GROUPS, Norms(base, 2 * LAYERS))
            dve.wait_ge(xn_ready, base + NG)
            m = slice(IMG_TILES, TILES)
            link(nc.vector.tensor_tensor(x_norm[:, m, :], x_norm[:, m, :],
                                         row_of(jrow[:, JR_FG:JR_FG + D], TXT_TILES), ALU.mult))
            link(nc.vector.tensor_tensor(x_tok[:, m, :], x_norm[:, m, :],
                                         row_of(jrow[:, JR_FB:JR_FB + D], TXT_TILES), ALU.add))
            dve.wait_ge(img_ready, 2)
            norm_dve(dve, ALL_GROUPS, Norms(base + NG, 2 * LAYERS + 1))
            for g, (t0, nt) in enumerate(ALL_GROUPS):
                dve.wait_ge(q_psum, LAYERS * NG + g + 1)
                nc.vector.tensor_scalar(qT[:, t0 * P:(t0 + nt) * P], ps[:, 5, 0:nt * P],
                                        jvec[:, JV_BQ:JV_BQ + 1], float(Q_SCALE), ALU.add, ALU.mult
                                        ).then_inc(q_sb, 1)
            for j in range(4):
                dve.wait_ge(v_psum, LAYERS * 4 + j + 1)
                nc.vector.tensor_tensor(
                    v_joint[0:K_JOINT, 4 * j:4 * j + 4, :, 0:HD],
                    ps[0:K_JOINT, 1 + j, :].rearrange("p (b h w) -> p b h w", b=4, w=HD),
                    jrow[0:K_JOINT, JR_BV:JR_BV + D].rearrange("p (h w) -> p h w", w=HD).unsqueeze(1)
                    .broadcast_to([K_JOINT, 4, NH, HD]), ALU.add).then_inc(v_sb, 1)
            attend_dve(dve, joint_units(), lambda k: LAYERS * B + k)
            for g, (t0, nt) in enumerate(ALL_GROUPS):
                s = slice(t0 * P, (t0 + nt) * P)
                dve.wait_ge(silu_ctx, g + 1)
                dve.wait_ge(u_sb, NA)
                nc.vector.tensor_tensor(uT[:, s], uT[:, s], hT[:, s], ALU.mult).then_inc(gated_sb, 1)
            dve.wait_ge(bias_added, 2 * LAYERS + 1)
            add_back(ALL_GROUPS, x_joint, lambda k: LAYERS * NG + k, wo_psum)
            dve.wait_ge(x_joint, NA)
            norm_dve(dve, ALL_GROUPS, Norms(base + NG + NA, 2 * LAYERS + 2))
            dve.wait_ge(aff_sb, 1)
            link(nc.vector.tensor_tensor(route[:], aff[:], row_of(jrow[:, JR_EB:JR_EB + E], TILES), ALU.add))
            for t in range(TILES):
                last = nc.vector.max(top8[:, t, :], route[:, t, :])
            link(last)
            for t in range(TILES):
                last = nc.vector.max_index(place[:, t, :], top8[:, t, :], route[:, t, :])
            link(last)
            for k in range(3):
                last = nc.vector.tensor_tensor(
                    (route, route2, route3)[k][:], row_of(const[:, C_IOTA:C_IOTA + E], TILES),
                    place[:, :, k:k + 1].broadcast_to([P, TILES, E]), ALU.is_equal)
            link(last)
            link(nc.vector.tensor_tensor(route[:], route[:], route2[:], ALU.add))
            link(nc.vector.tensor_tensor(route[:], route[:], route3[:], ALU.add))
            link(nc.vector.tensor_tensor(aff[:], aff[:], route[:], ALU.mult))
            link(nc.vector.tensor_reduce(gsum[:], aff[:], AX.X, ALU.add))
            link(nc.vector.tensor_scalar(gsum[:], gsum[:], 1e-9, None, ALU.add))
            link(nc.vector.reciprocal(veps[:], gsum[:]))
            link(nc.vector.tensor_tensor(aff[:], aff[:], veps[:].unsqueeze(2).broadcast_to([P, TILES, E]), ALU.mult))
            link(nc.vector.tensor_copy(gates[:, :, 0:E], aff[:]))
            nc.vector.tensor_tensor(gates[:, :, E:2 * E], aff[:], gates[:, :, 0:E].bitcast(F32),
                                    ALU.subtract).then_inc(gates_sb, 1)
            nc.vector.memset(wait_carrier[:], 0.0).then_inc(final_sb, 1)
            n = 2 * (E + 1)
            with dve.Fori(0, CHUNKS // 2) as c:
                for p in range(n + 4):
                    if p < n:
                        dve.wait_ge(up_psum, c * n + (p + 1))
                        dve.wait_ge(silu_sb, c * n + (p + 1))
                        shared = p % (E + 1) == E
                        if shared:
                            dve.wait_ge(hglo_sb, c * n + (p - 1))
                        ins = nc.vector.tensor_tensor((hg_t if shared else su_t)[:, p % 2, :], silu_t[:, p % 2, :],
                                                      ps[:, 2 + p % 2, 0:CHUNK], ALU.mult)
                        ins.then_inc(su_sb, 1)
                        if shared:
                            dve.wait_ge(su_sb, c * n + (p + 1))
                            nc.vector.memset(wait_carrier[:], 0.0).then_inc(hg_sb, 1)
                        else:
                            dve.wait_ge(gb_psum, c * (2 * E) + (p - p // (E + 1) + 1))
                            dve.wait_ge(su_sb, c * n + (p + 1))
                            if p >= 2:
                                dve.wait_ge(hglo_sb, c * n + (p - 1))
                            nc.vector.tensor_tensor(hg_t[:, p % 2, :], su_t[:, p % 2, :],
                                                    ps[:, 4 + p % 2, 0:CHUNK], ALU.mult).then_inc(hg_sb, 1)
                    if p >= 4 and (p - 4) % (E + 1) == E:
                        k = (p - 4) // (E + 1)
                        dve.wait_ge(oT_psum, c * 2 + (k + 1))
                        xs = x_tok[:, bass.ds(c * (2 * CHUNK_TILES) + k * CHUNK_TILES, CHUNK_TILES), :]
                        nc.vector.tensor_tensor(
                            xs, xs, ps[:, 6 + k, 0:CHUNK].rearrange("p (t d) -> p t d", t=CHUNK_TILES),
                            ALU.add).then_inc(final_sb, 1)


_NAMES = ["const", "tokens", "tokens_end", "noise_cols", "noise_rows", "tok_w", "tok_sw", "tok_w3", "tok_b", "patches",
          "pad_row", "pad_col", "pos", "item_emb", "w_qkv", "w_o", "w_1", "w_2", "vec", "row", "jw", "jvec",
          "jrow", "w_exp", "w_gate"]


def constants():
    c = np.zeros((P, C_ALL), np.float32)
    c[:, C_ID:C_ID + P] = np.eye(P)
    i, j = np.arange(S_TXT)[:, None], np.arange(S_TXT)[None, :]
    c[:S_TXT, C_CAUSAL:C_CAUSAL + S_TXT] = np.where(j > i, FAR, 0.0)
    i, j = S_IMG + np.arange(S_TXT)[:, None], np.arange(K_JOINT)[None, :]
    c[:S_TXT, C_JOINT:C_JOINT + K_JOINT] = np.where((j <= i) & (i + j <= S_ALL), 0.0, FAR)
    c[:S_TXT, C_MASKL:C_MASKL + S_TXT] = np.eye(S_TXT)
    c[PAD_ROW, C_MASKL:C_MASKL + S_TXT] = 1.0
    c[np.arange(P), C_HEAD + np.arange(P) // HD] = 1.0
    pos = np.arange(S_IMG, dtype=np.float32)[:, None]
    div = np.exp(np.arange(0, D, 2, dtype=np.float32) * np.float32(-np.log(10000.0) / D))
    ang = (pos * div).astype(np.float32)
    pe = np.stack([np.sin(ang), np.cos(ang)], axis=-1).reshape(S_IMG, D)
    c[:, C_IOTA:C_IOTA + E] = np.arange(E)
    c[:, C_POS:C_POS + D] = np.tile(pe, (P // S_IMG, 1))
    return c


def kernel(**inputs):
    import concourse.bacc as _bacc
    from concourse.bass_utils import run_bass_kernel_spmd as _run

    f = {k: np.asarray(v) for k, v in inputs.items()}

    def t(name):
        return f[name]

    def halves(w):
        return w.T.reshape(2, P, D).transpose(1, 0, 2)

    def col(name, n=1):
        return t(name).reshape(n, P).T

    x = t("x").reshape(B, 8, 16, 8, 16).transpose(2, 4, 0, 1, 3).reshape(2, P, T0).transpose(1, 0, 2)
    tokens = t("x_txt").reshape(TXT_TOKENS)
    layers = range(LAYERS)
    arrays = {
        "const": constants(),
        "tokens": tokens[:TXT_TOKENS - LAST_ROWS].reshape(TXT_TILES - 1, P).T,
        "tokens_end": tokens[TXT_TOKENS - LAST_ROWS:, None],
        "noise_cols": np.concatenate([col("L0_tok_eps_in1", 2), col("L0_tok_eps_in2", 2),
                                      col("L0_tok_eps_out1"), col("L0_tok_eps_out2")], axis=1),
        "noise_rows": np.concatenate([t("L0_tok_eps_out1"), t("L0_tok_eps_out2")])[None, :],
        "tok_w": np.stack([halves(t("L0_tok_W1_w")), halves(t("L0_tok_W2_w"))], axis=1).reshape(P, 4 * D),
        "tok_sw": np.stack([halves(t("L0_tok_W1_sw")), halves(t("L0_tok_W2_sw"))], axis=1).reshape(P, 4 * D),
        "tok_w3": t("L0_tok_W3_w").T,
        "tok_b": np.stack([t("L0_tok_W1_b"), t("L0_tok_W1_sb"), t("L0_tok_W2_b"), t("L0_tok_W2_sb")], axis=1),
        "patches": x.reshape(P, 2 * T0),
        "pad_row": t("mask_BS_f1_0").reshape(1, TXT_TOKENS),
        "pad_col": t("mask_BS_f1_0").T,
        "pos": np.concatenate([t("L0_txt_pos_emb")[:S_TXT]] * B, axis=0),
        "item_emb": t("L0_txt_item_emb"),
        "w_qkv": np.concatenate([t("L0_txt_Wq"), t("L0_txt_Wk"), t("L0_txt_Wv")], axis=2).reshape(LAYERS * P, 3 * D),
        "w_o": t("L0_txt_Wo").reshape(LAYERS * P, D),
        "w_1": t("L0_txt_W1").reshape(LAYERS * P, FF * D),
        "w_2": t("L0_txt_W2").reshape(LAYERS, FF, P, D).transpose(0, 2, 1, 3).reshape(LAYERS * P, FF * D),
        "vec": np.concatenate([
            np.concatenate([np.stack([t("L0_txt_" + n)[l] for n in ("ln1_g", "ln1_b", "bq", "bk", "ln2_g", "ln2_b")],
                                     axis=1), t("L0_txt_b1")[l].reshape(FF, P).T], axis=1) for l in layers], axis=0),
        "row": np.concatenate([t("L0_txt_bv"), t("L0_txt_bo"), t("L0_txt_b2")], axis=1),
        "jw": np.concatenate([t("L0_attn_w_qkv").T, t("L0_attn_w_u").T, t("L0_attn_w_out").T], axis=1),
        "jvec": np.stack([t("L0_attn_b_qkv")[0:D], t("L0_attn_b_qkv")[D:2 * D], t("L0_attn_b_u")], axis=1),
        "jrow": np.concatenate([t("L0_attn_b_qkv")[2 * D:], t("L0_attn_b_out"), t("L0_tok_W3_b"), t("L0_txt_lnf_g"),
                                t("L0_txt_lnf_b"), t("L0_ffn_expert_bias")])[None, :],
        "w_exp": np.concatenate([
            np.concatenate([t("L0_ffn_expert_gate_up").transpose(0, 2, 1), t("L0_ffn_expert_down").transpose(0, 2, 1)],
                           axis=2),
            np.concatenate([t("L0_ffn_shared_gate_up").T, t("L0_ffn_shared_down").T], axis=1)[None]],
            axis=0).reshape((E + 1) * P, EW),
        "w_gate": t("L0_ffn_gate_w").T,
    }
    nc = _bacc.Bacc("TRN2", target_bir_lowering=False, num_devices=1)
    given, aps = {}, {}
    for name in _NAMES:
        v = np.ascontiguousarray(arrays[name])
        given["in_" + name] = v
        aps[name] = nc.dram_tensor("in_" + name, v.shape, mybir.dt.from_np(v.dtype), kind="ExternalInput").ap()
    out = nc.dram_tensor("out_tokens", (COLS, D), F32, kind="ExternalOutput").ap()
    build(nc, aps, out)
    got = _run(nc, [given], core_ids=[0]).results[0]["out_tokens"]
    return np.concatenate([got[:T0].reshape(B, S_IMG, D), got[T0:T0 + TXT_TOKENS].reshape(B, S_TXT, D)], axis=1)
```

```python
from contextlib import ExitStack

import numpy as np

import concourse.bass as bass
from concourse import mybir

F32 = mybir.dt.float32
F32R = mybir.dt.float32r
BF16 = mybir.dt.bfloat16
I32 = mybir.dt.int32
U32 = mybir.dt.uint32
ALU = mybir.AluOpType
ACT = mybir.ActivationFunctionType
AX = mybir.AxisListType

P = 128
D = 128
B = 16
NH, HD = 8, 16
VW = HD + 1
LAYERS = 4
S_IMG, S_TXT = 64, 77
S_ALL = S_IMG + S_TXT
K_JOINT = S_ALL // 2 + 1
IMG_TILES = B * S_IMG // P
TXT_TOKENS = B * S_TXT
TXT_TILES = -(-TXT_TOKENS // P)
TILES = IMG_TILES + TXT_TILES
LAST_ROWS = TXT_TOKENS - (TXT_TILES - 1) * P
COLS = TILES * P
T0 = IMG_TILES * P
FF = 4
E = 16
CHUNK_TILES = 3
CHUNK = CHUNK_TILES * P
CHUNKS = TILES // CHUNK_TILES
EW = 3 * D
STAGE = 4
EPS = 1e-5
FAR = -1e30
Q_SCALE = 1.0 / np.sqrt(HD)
EXP_CAP = 30.0

IMG_GROUPS = [(0, 4), (4, 4)]
TXT_GROUPS = [(8, 4), (12, 3), (15, 3)]
ALL_GROUPS = IMG_GROUPS + TXT_GROUPS
NG = len(TXT_GROUPS)
NI = len(IMG_GROUPS)
NA = len(ALL_GROUPS)
OUT_GROUPS = [(0, 4), (8, 4), (4, 2), (12, 3), (6, 2), (15, 3)]
NO = len(OUT_GROUPS)
OUT_EARLY = 4
ROUTE_TILES = [t for t0, nt in OUT_GROUPS for t in range(t0, t0 + nt)]
ROUTE_PARTS = [(0, sum(nt for _, nt in OUT_GROUPS[:OUT_EARLY])), (sum(nt for _, nt in OUT_GROUPS[:OUT_EARLY]), TILES)]
LOGIT_BANKS, GATE_BANKS = (6, 4), (4, 5, 6, 7, 7, 7)
TXT_SPARE = {11: (8, 2, 2), 12: (10, 2, 2)}
ALL_SPARE = {22: (0, 2, 1), 23: (2, 2, 1), 24: (8, 2, 2), 25: (10, 2, 2), 30: (4, 2, 3), 31: (12, 2, 4), 32: (14, 1, 4)}
TOK_STEPS = {3: 0, 4: 1}
TOK_TILES = IMG_TILES // LAYERS
TXT_ADDS = len(TXT_SPARE) + 2
ADDS = TXT_ADDS + NG
SPARE_COL = NH * VW
QK_ORDER = [("T", 0), ("QK", 0), ("T", 1), ("V", 0), ("QK", 1), ("T", 2), ("V", 1), ("QK", 2), ("V", 2)]
FFN_ORDER = ([(0, 0), (0, 1), ("O", 2), ("T", 1), (0, 2), (0, 3), (1, 0), (1, 1), ("T", 2), (1, 2), (1, 3), ("W", 0),
              ("I", 0)]
             + [(2, f) for f in range(FF)] + [("W", 1), ("W", 2)])
JOINT_ORDER = [("T", 0), ("T", 1), ("QKU", 0), ("QKU", 1), ("T", 2), ("T", 3), ("QKU", 2), ("V", 0), ("T", 4), ("V", 1),
               ("QKU", 3), ("V", 2), ("QKU", 4), ("V", 3)]
Q_BANKS, K_BANKS, V_BANKS = (6, 4, 1), (7, 0, 2), (5, 4, 6, 7)
T1_BANKS, T2_BANKS = (2, 3, 2), (1, 0, 1)
OUT_BANKS = (0, 1, 2, 3, 5, 7)
HIDDEN_BANKS, W2_BANKS = (2, 3, 5, 6, 7), (4, 0, 1)
TOK_BANK = 5

C_ID, C_CAUSAL, C_JOINT, C_MASKL, C_HEAD, C_POS = 0, 128, 205, 276, 353, 361
C_IOTA = 489
C_ALL = 505
PAD_ROW = 96
V_G1, V_B1, V_BQ, V_BK, V_G2, V_B2, V_BF = 0, 1, 2, 3, 4, 5, 6
V_ALL = 10
R_BV, R_BO, R_B2 = 0, 128, 256
JV_BQ, JV_BK, JV_BU = 0, 1, 2
JR_BV, JR_BO, JR_W3B, JR_FG, JR_FB, JR_EB = 0, 128, 256, 384, 512, 640
JR_ALL = 656


class Unit:

    def __init__(self, nq, nk, qcol, kslot, vals, mask_l, mask_r, c_off, kexp_no):
        self.nq, self.nk, self.qcol, self.kslot, self.vals = nq, nk, qcol, kslot, vals
        self.mask_l, self.mask_r, self.c_off, self.kexp_no = mask_l, mask_r, c_off, kexp_no


ROUND = 2 * (E + 1)
ROUNDS = CHUNKS // 2
LAG = 4
HEAD = 13


def expert_steps(engine, step):
    for r in range(HEAD):
        step(0, r)
    with engine.Fori(0, ROUNDS - 1) as c:
        for r in range(HEAD, ROUND + HEAD):
            step(c, r)
    for r in range(HEAD, ROUND + LAG):
        step(ROUNDS - 1, r)


def taken(c, r):
    return r < ROUND or not isinstance(c, int)


def norm_no(l, k):
    return l * (2 * NG + 1) + k


class Passed:

    def __init__(self, l):
        self.l = l

    def __call__(self, k):
        return self.l * B + k

    def group(self, g):
        return self.l * (B // 4) + g

    def values(self):
        return self.l * 4 + 4


def build(nc, a, out):
    ctx = ExitStack()
    with ctx:
        def sb(name, shape, dt=F32):
            return ctx.enter_context(nc.sbuf_tensor(name, shape, dt))

        def sem(name):
            return ctx.enter_context(nc.semaphore(name))

        const = sb("const", [P, C_ALL])
        ident = const[:, C_ID:C_ID + P]
        ident_bf = sb("ident_bf", [P, P], BF16)
        mask_l_bf = sb("mask_l_bf", [P, S_TXT], BF16)
        txt_mask = sb("txt_mask", [P, B, S_TXT], BF16)
        joint_mask = sb("joint_mask", [P, K_JOINT], BF16)
        pad_col = sb("pad_col", [P, B])
        pad_col1 = sb("pad_col1", [P, B])
        head_mask = const[:, C_HEAD:C_HEAD + NH]
        eps_t = sb("eps_t", [P, TILES])
        half_t = sb("half_t", [P, TILES])
        x_tok = sb("x_tok", [P, TILES, D])
        x_norm = sb("x_norm", [P, TILES, D])
        hT = sb("hT", [P, COLS])
        qT = sb("qT", [P, COLS])
        kT = sb("kT", [P, COLS])
        uT = sb("uT", [P, COLS])
        ctxT = sb("ctxT", [P, COLS])
        stats = sb("stats", [P, TILES, 6])
        mv = sb("mv", [P, TILES, 2])
        wait_carrier = sb("wait_carrier", [1, 1])
        table_carrier = sb("table_carrier", [1, 1])
        veps = sb("veps", [P, TILES])
        rstd = sb("rstd", [P, TILES])
        k_exp = sb("k_exp", [P, 2, NH * S_TXT])
        v_joint = sb("v_joint", [P, B, NH, VW])
        probs = sb("probs", [P, 2, 2, 4 * S_TXT])
        probsT = sb("probsT", [P, 2, 2, 4 * S_TXT])
        pad_in = probsT[:].rearrange("p a b k -> p (a b k)")
        neg_max = sb("neg_max", [P, 2, NH])
        r_den = sb("r_den", [P, NH])
        ctx_sb_t = sb("ctx_sb_t", [P, 2, D])
        jw = sb("jw", [P, 5 * D])
        jvec = sb("jvec", [P, 3])
        jrow = sb("jrow", [P, JR_ALL])
        idx = sb("idx", [P, TXT_TILES], I32)
        w_gate = sb("w_gate", [P, E])
        select = sb("select", [P, E, P], F32R)
        gateT = sb("gateT", [P, COLS], F32R)
        top8 = sb("top8", [P, TILES, 8])
        place = sb("place", [P, TILES, 8], U32)
        gsum = sb("gsum", [P, TILES])
        oT_t = sb("oT_t", [P, CHUNK])
        slots = qT[:].rearrange("p (k s t) -> p k s t", k=3, s=2)
        silu_t, su_t, hg_t = slots[:, 0], slots[:, 1], slots[:, 2]

        def after_keys(k):
            n = TILES * E
            return kT[:, k * n:(k + 1) * n].rearrange("p (t e) -> p t e", t=TILES)

        aff, route, route2, route3 = (after_keys(k) for k in range(4))

        with ExitStack() as early:
            def sbe(name, shape, dt=F32):
                return early.enter_context(nc.sbuf_tensor(name, shape, dt))

            v_txt = sbe("v_txt", [P, B, NH, VW])
            gelu_t = sbe("gelu_t", [P, 2, FF, 512])
            w_qkv_t = sbe("w_qkv_t", [P, 3 * D])
            w_o_t = sbe("w_o_t", [P, D])
            w_1_t = sbe("w_1_t", [P, FF * D])
            w_2_t = sbe("w_2_t", [P, FF, D])
            vec = sbe("vec", [P, V_ALL])
            row = sbe("row", [P, 3 * D])
            patches = sbe("patches", [P, 2, T0])
            tok_w = sbe("tok_w", [P, 2, 2, D])
            tok_sw = sbe("tok_sw", [P, 2, 2, D])
            tok_w3 = sbe("tok_w3", [P, D])
            tok_b = sbe("tok_b", [P, 4])
            noise = sbe("noise", [P, 6 + 2 * D])
            noise_abs = sbe("noise_abs", [P, 6 + 2 * D])
            noise_root = sbe("noise_root", [P, 6 + 2 * D])
            noise_sign = sbe("noise_sign", [P, 6 + 2 * D])
            tok_bn = sbe("tok_bn", [P, 2])
            gate_t = sbe("gate_t", [P, TOK_TILES * P])
            inner_t = sbe("inner_t", [P, TOK_TILES * P])
            cap_t = sbe("cap_t", [P, TOK_TILES * P])
            exp_t = sbe("exp_t", [P, TOK_TILES * P])
            ratio_t = sbe("ratio_t", [P, TOK_TILES * P])
            mid_t = sbe("mid_t", [P, TOK_TILES * P])
            img_t = sbe("img_t", [P, TOK_TILES, D])
            img_stats = sbe("img_stats", [P, TOK_TILES, 6])
            img_mv = sbe("img_mv", [P, TOK_TILES, 2])
            img_veps = sbe("img_veps", [P, TOK_TILES])
            img_rstd = sbe("img_rstd", [P, TOK_TILES])
            pos_b = sbe("pos_b", [P, D])
        w_stage = sb("w_stage", [P, STAGE, EW])
        w_hi = sb("w_hi", [P, E + 1, EW], F32R)
        w_lo = sb("w_lo", [P, E + 1, EW], F32R)
        h_hi = sb("h_hi", [P, COLS], F32R)
        h_lo = sb("h_lo", [P, COLS], F32R)
        hg_hi = sb("hg_hi", [P, 2, CHUNK], F32R)
        hg_lo = sb("hg_lo", [P, 2, CHUNK], F32R)
        gates = sb("gates", [P, TILES, 2 * E], F32R)

        ps = ctx.enter_context(nc.psum_tensor("ps", [P, 8, 512], F32))

        s_const = sem("s_const")
        s_noise = sem("s_noise")
        s_tokin = sem("s_tokin")
        s_idx = sem("s_idx")
        s_txtin = sem("s_txtin")
        s_pos = sem("s_pos")
        s_gather = [sem(f"s_gather{g}") for g in range(NG)]
        s_joint = sem("s_joint")
        s_gate = sem("s_gate")
        s_expert = [sem(f"s_expert{k}") for k in range(STAGE)]
        whi_sb = sem("whi_sb")
        wlo_sb = sem("wlo_sb")
        hhi_sb = sem("hhi_sb")
        hlo_sb = sem("hlo_sb")
        hghi_sb = sem("hghi_sb")
        hglo_sb = sem("hglo_sb")
        s_wqkv, s_wo, s_w1, s_w2 = sem("s_wqkv"), sem("s_wo"), sem("s_w1"), sem("s_w2")
        s_vec, s_row = sem("s_vec"), sem("s_row")
        s_zero = sem("s_zero")
        s_masks = sem("s_masks")
        s_dve = sem("s_dve")
        s_act = sem("s_act")
        noise_ready = sem("noise_ready")
        tokw_ready = sem("tokw_ready")
        tok_psum = sem("tok_psum")
        tok_taken = sem("tok_taken")
        tok_cap = sem("tok_cap")
        tok_exp = sem("tok_exp")
        tok_num = sem("tok_num")
        tok_den = sem("tok_den")
        tok_rec = sem("tok_rec")
        tok_part = sem("tok_part")
        tok_mid = sem("tok_mid")
        embedded = sem("embedded")
        x_upd = sem("x_upd")
        ln_stats = sem("ln_stats")
        ln_mv = sem("ln_mv")
        ln_eps = sem("ln_eps")
        ln_rstd = sem("ln_rstd")
        xn_ready = sem("xn_ready")
        xT_psum = sem("xT_psum")
        hT_sb = sem("hT_sb")
        q_psum, k_psum, v_psum, u_psum = sem("q_psum"), sem("k_psum"), sem("v_psum"), sem("u_psum")
        q_sb, k_sb, v_sb, u_sb = sem("q_sb"), sem("k_sb"), sem("v_sb"), sem("u_sb")
        kexp_sb = sem("kexp_sb")
        bias_added = sem("bias_added")
        scores_psum = sem("scores_psum")
        max_sb = sem("max_sb")
        shifted_sb = sem("shifted_sb")
        probs_sb = sem("probs_sb")
        pT_psum = sem("pT_psum")
        pT_sb = sem("pT_sb")
        o_psum = sem("o_psum")
        rden_sb = sem("rden_sb")
        ctx_sb = sem("ctx_sb")
        c_psum = sem("c_psum")
        ctxT_sb = sem("ctxT_sb")
        wo_psum = sem("wo_psum")
        w1_psum = sem("w1_psum")
        gelu_sb = sem("gelu_sb")
        w2_psum = sem("w2_psum")
        tanh_ctx = sem("tanh_ctx")
        ctx_u = sem("ctx_u")
        gated_sb = sem("gated_sb")
        gained = sem("gained")
        txt_done = sem("txt_done")
        x_joint = sem("x_joint")
        lg_psum = sem("lg_psum")
        aff_sb = sem("aff_sb")
        gates_sb = sem("gates_sb")
        gT_psum = sem("gT_psum")
        gT_sb = sem("gT_sb")
        g_psum, up_psum, gb_psum = sem("g_psum"), sem("up_psum"), sem("gb_psum")
        silu_sb = sem("silu_sb")
        su_sb = sem("su_sb")
        hg_sb = sem("hg_sb")
        d_psum = sem("d_psum")
        oT_sb = sem("oT_sb")
        oT_psum = sem("oT_psum")
        final_sb = sem("final_sb")
        s_out = sem("s_out")

        def kview(slot, nk):
            return k_exp[:, slot, 0:NH * nk].rearrange("p (h k) -> p h k", h=NH)

        def text_units():
            return [Unit(S_TXT, S_TXT, T0 + b * S_TXT, kview(b % 2, S_TXT), v_txt[:, b],
                         mask_l_bf[0:PAD_ROW + 1, :], txt_mask[0:PAD_ROW + 1, b, :],
                         (b % 4) * S_TXT, b) for b in range(B)]

        def joint_units():
            units = []
            for b in range(B):
                keys = kview(b % 2, K_JOINT)
                units.append(Unit(S_IMG, S_IMG, b * S_IMG, keys, v_joint[:, b], ident_bf[0:S_IMG, :],
                                  txt_mask[0:S_IMG, 0, 0:S_IMG], (b % 2) * S_IMG, b))
                units.append(Unit(S_TXT, K_JOINT, T0 + b * S_TXT, keys, v_joint[:, b], ident_bf[0:S_TXT, :],
                                  joint_mask[0:S_TXT, :], 2 * S_IMG + (b % 2) * S_TXT, b))
            return units

        def scores_at(i, u):
            s = 2 * (i % 2)
            return ps[0:u.nq, s:s + 2, 0:4 * u.nk]


        def attend_pe(pe, units, at, kexp_at, spare, project, added, before=lambda i: None,
                      after=lambda i: None):
            n = len(units)
            for i in range(n + 3):
                if i < n:
                    u = units[i]
                    pe.wait_ge(kexp_sb, kexp_at(u.kexp_no + 1))
                    if i >= 2:
                        pe.wait_ge(shifted_sb, at(i - 1))
                    for half in range(2):
                        s = 2 * (i % 2) + half
                        dst = ps[0:u.nq, s, 0:4 * u.nk]
                        nc.tensor.matmul(dst, qT[:, u.qcol:u.qcol + u.nq],
                                         u.kslot[:, 4 * half:4 * half + 4, 0:u.nk],
                                         start=True, stop=False, skip_group_check=True)
                        last = nc.tensor.matmul(dst, u.mask_l[:, 0:u.nq],
                                                u.mask_r.unsqueeze(1).broadcast_to([u.mask_r.shape[0], 4, u.nk]),
                                                start=False, stop=True, skip_group_check=True)
                    last.then_inc(scores_psum, 1)
                before(i)
                if i == 1:
                    pe.wait_ge(v_sb, at.values() - 1)
                if i == 2:
                    pe.wait_ge(v_sb, at.values())
                if 0 <= i - 1 < n:
                    u, j = units[i - 1], i - 1
                    pe.wait_ge(probs_sb, at(j + 1))
                    if j >= 1:
                        pe.wait_ge(pT_sb, at(j))
                    for h in range(NH):
                        last = nc.tensor.transpose(
                            ps[0:u.nk, 4 + h // 4, (h % 4) * u.nq:(h % 4 + 1) * u.nq],
                            probs[0:u.nq, j % 2, h // 4, (h % 4) * u.nk:(h % 4 + 1) * u.nk],
                            ident[0:u.nq, 0:u.nq])
                    last.then_inc(pT_psum, 1)
                if 0 <= i - 2 < n:
                    u, j = units[i - 2], i - 2
                    if j >= 1:
                        pe.wait_ge(ctx_sb, at(j))
                    if i - 1 in spare:
                        added(i - 1)
                    if i in spare:
                        project(i)
                    pe.wait_ge(pT_sb, at(j + 1))
                    for h in range(NH):
                        last = nc.tensor.matmul(
                            ps[0:u.nq, 6, h * VW:(h + 1) * VW],
                            probsT[0:u.nk, j % 2, h // 4, (h % 4) * u.nq:(h % 4 + 1) * u.nq],
                            u.vals[0:u.nk, h, :], start=True, stop=True)
                    last.then_inc(o_psum, 1)
                after(i)
                if 0 <= i - 3 < n:
                    u, j = units[i - 3], i - 3
                    pe.wait_ge(ctx_sb, at(j + 1))
                    if j % 4 == 0 and j >= 4:
                        pe.wait_ge(ctxT_sb, at.group(j // 4))
                    nc.tensor.transpose(ps[:, 7, u.c_off:u.c_off + u.nq], ctx_sb_t[0:u.nq, j % 2, :],
                                        ident[0:u.nq, 0:u.nq]).then_inc(c_psum, 1)

        def attend_act(act, units, at, evict_ctx, beside=lambda i: None):
            n = len(units)
            for i in range(n + 3):
                if 0 <= i - 1 < n:
                    u, j = units[i - 1], i - 1
                    act.wait_ge(pT_psum, at(j + 1))
                    if j >= 2:
                        act.wait_ge(o_psum, at(j - 1))
                    nc.scalar.activation(probsT[0:u.nk, j % 2, :, 0:4 * u.nq], ps[0:u.nk, 4:6, 0:4 * u.nq],
                                         ACT.Copy).then_inc(pT_sb, 1)
                if i < n:
                    u = units[i]
                    act.wait_ge(shifted_sb, at(i + 1))
                    nc.scalar.activation(probs[0:u.nq, i % 2, :, 0:4 * u.nk], probs[0:u.nq, i % 2, :, 0:4 * u.nk],
                                         ACT.Exp).then_inc(probs_sb, 1)
                if 0 <= i - 3 < n and (i - 3) % 4 == 3:
                    act.wait_ge(c_psum, at(i - 2))
                    evict_ctx((i - 3) // 4)
                beside(i)

        def attend_dve(dve, units, at, beside):
            n = len(units)
            for i in range(n + 2):
                if i < n:
                    u = units[i]
                    dve.wait_ge(scores_psum, at(i + 1))
                    nc.vector.tensor_reduce(
                        neg_max[0:u.nq, i % 2, :].rearrange("p (a h) -> p a h", a=2),
                        scores_at(i, u).rearrange("p a (h k) -> p a h k", h=4),
                        AX.X, ALU.max, negate=True).then_inc(max_sb, 1)
                    dve.wait_ge(max_sb, at(i + 1))
                    if i >= 2:
                        dve.wait_ge(pT_psum, at(i - 1))
                    nc.vector.tensor_tensor(
                        probs[0:u.nq, i % 2, :, 0:4 * u.nk].rearrange("p a (h k) -> p a h k", h=4),
                        scores_at(i, u).rearrange("p a (h k) -> p a h k", h=4),
                        neg_max[0:u.nq, i % 2, :].rearrange("p (a h) -> p a h", a=2).unsqueeze(3)
                        .broadcast_to([u.nq, 2, 4, u.nk]), ALU.add).then_inc(shifted_sb, 1)
                if 0 <= i - 2 < n:
                    u, j = units[i - 2], i - 2
                    dve.wait_ge(o_psum, at(j + 1))
                    o = ps[0:u.nq, 6, 0:NH * VW].rearrange("p (h w) -> p h w", h=NH)
                    nc.vector.reciprocal(r_den[0:u.nq, :], o[:, :, HD]).then_inc(rden_sb, 1)
                    dve.wait_ge(rden_sb, at(j + 1))
                    if j >= 2:
                        dve.wait_ge(c_psum, at(j - 1))
                    nc.vector.tensor_tensor(
                        ctx_sb_t[0:u.nq, j % 2, :].rearrange("p (h w) -> p h w", h=NH), o[:, :, 0:HD],
                        r_den[0:u.nq, :].unsqueeze(2).broadcast_to([u.nq, NH, HD]),
                        ALU.mult).then_inc(ctx_sb, 1)
                beside(i)

        def spread_keys(slot, nk, parts):
            at, dst = 0, kview(slot, nk)
            for col, n in parts:
                last = nc.gpsimd.tensor_tensor(
                    dst[:, :, at:at + n], kT[:, col:col + n].unsqueeze(1).broadcast_to([P, NH, n]),
                    head_mask.unsqueeze(2).broadcast_to([P, NH, n]), ALU.mult)
                at += n
            last.then_inc(kexp_sb, 1)


        def tile_stats(t0, nt):
            for t in range(t0, t0 + nt):
                last = nc.vector.bn_stats(stats[:, t, :], x_tok[:, t, :])
            return last

        def norm_moments(dve, group, n):
            t0, nt = group
            dve.wait_ge(ln_stats, n)
            nc.vector.memset(wait_carrier[:], 0.0)
            for t in range(t0, t0 + nt):
                last = nc.vector.bn_aggr(mv[:, t, :], stats[:, t, :])
            last.then_inc(ln_mv, 1)

        def norm_apply(dve, group, n):
            t0, nt = group
            dve.wait_ge(ln_rstd, n)
            for t in range(t0, t0 + nt):
                last = nc.vector.tensor_scalar(x_norm[:, t, :], x_tok[:, t, :], mv[:, t, 0:1],
                                               rstd[:, t:t + 1], ALU.subtract, ALU.mult)
            last.then_inc(xn_ready, 1)

        def norm_root(pool, group, n):
            s = slice(group[0], group[0] + group[1])
            pool.wait_ge(ln_mv, n)
            nc.gpsimd.tensor_tensor(veps[:, s], mv[:, s, 1], eps_t[:, s], ALU.add).then_inc(ln_eps, 1)
            pool.wait_ge(ln_eps, n)
            nc.gpsimd.tensor_tensor(rstd[:, s], veps[:, s], half_t[:, s], ALU.pow).then_inc(ln_rstd, 1)

        def norm_transpose(pe, group, n, bank):
            t0, nt = group
            pe.wait_ge(xn_ready, n)
            for t in range(t0, t0 + nt):
                last = nc.tensor.transpose(ps[:, bank, (t - t0) * P:(t - t0 + 1) * P], x_norm[:, t, :], ident)
            last.then_inc(xT_psum, 1)

        def group_cols(group):
            return slice(group[0] * P, (group[0] + group[1]) * P)

        def bank_cols(bank, group, col=0):
            return ps[:, bank, col:col + group[1] * P].rearrange("p (t d) -> p t d", t=group[1])

        def project_tokens(weights, src, t0, nt, b, col=0):
            for t in range(t0, t0 + nt):
                last = nc.tensor.matmul(ps[:, b, col + (t - t0) * P:col + (t - t0 + 1) * P], src[:, t * P:(t + 1) * P],
                                        weights, start=True, stop=True)
            return last

        def row_of(r, n, rows=P):
            return r[0:rows].unsqueeze(1).broadcast_to([rows, n, r.shape[1]])

        block = ctx.enter_context(nc.Block())

        @block.sync
        def _(sp):
            sp.dma_start(idx[:, 0:TXT_TILES - 1],
                         a["tokens"]).then_inc(s_idx, 16)
            sp.dma_start(idx[0:LAST_ROWS, TXT_TILES - 1:TXT_TILES],
                         a["tokens_end"]).then_inc(s_idx, 16)
            sp.dma_start(const[:], a["const"]).then_inc(s_const, 16)
            sp.dma_start(pad_in[PAD_ROW:PAD_ROW + 1, :], a["pad_row"]).then_inc(s_txtin, 16)
            sp.dma_start(pad_col[0:S_TXT, :], a["pad_col"]).then_inc(s_txtin, 16)
            n9 = (TXT_TILES - 1) * P
            sp.dma_start(x_norm[:, IMG_TILES:TILES - 1, :],
                         a["pos"][0:n9, :].rearrange("(t p) d -> p t d", p=P)).then_inc(s_pos, 16)
            sp.dma_start(x_norm[0:LAST_ROWS, TILES - 1, :], a["pos"][n9:TXT_TOKENS, :]).then_inc(s_pos, 16)
            sp.dma_start(w_qkv_t[:], a["w_qkv"][0:P, :]).then_inc(s_wqkv, 16)
            sp.dma_start(vec[:], a["vec"][0:P, :]).then_inc(s_vec, 16)
            sp.dma_start(row[:], a["row"][0:1, :].broadcast_to([P, 3 * D])).then_inc(s_row, 16)
            sp.dma_start(patches[:].rearrange("p c t -> p (c t)"), a["patches"]).then_inc(s_tokin, 16)
            sp.dma_start(w_o_t[:], a["w_o"][0:P, :]).then_inc(s_wo, 16)
            sp.dma_start(w_1_t[:], a["w_1"][0:P, :]).then_inc(s_w1, 16)
            sp.dma_start(w_2_t[:].rearrange("p f d -> p (f d)"), a["w_2"][0:P, :]).then_inc(s_w2, 16)
            with sp.Fori(1, LAYERS) as l:
                lo = l * P
                sp.wait_ge(v_psum, l * 4)
                sp.dma_start(w_qkv_t[:], a["w_qkv"][bass.ds(lo, P), :]).then_inc(s_wqkv, 16)
                sp.wait_ge(wo_psum, l * TXT_ADDS)
                sp.dma_start(w_o_t[:], a["w_o"][bass.ds(lo, P), :]).then_inc(s_wo, 16)
                sp.wait_ge(w1_psum, l * (NG * FF))
                sp.dma_start(w_1_t[:], a["w_1"][bass.ds(lo, P), :]).then_inc(s_w1, 16)
                sp.wait_ge(gelu_sb, l * (NG * FF))
                sp.dma_start(vec[:], a["vec"][bass.ds(lo, P), :]).then_inc(s_vec, 16)
                sp.wait_ge(bias_added, l * (1 + NG))
                sp.dma_start(row[:], a["row"][bass.ds(l, 1), :].broadcast_to([P, 3 * D])).then_inc(s_row, 16)
                sp.wait_ge(w2_psum, l * NG)
                sp.dma_start(w_2_t[:].rearrange("p f d -> p (f d)"), a["w_2"][bass.ds(lo, P), :]
                             ).then_inc(s_w2, 16)
            sp.wait_ge(w2_psum, LAYERS * NG)
            sp.wait_ge(bias_added, LAYERS * (1 + NG))
            for e in range(E + 1):
                if e >= STAGE:
                    sp.wait_ge(wlo_sb, e - STAGE + 1)
                    sp.wait_ge(whi_sb, e - STAGE + 1)
                sp.dma_start(w_stage[:, e % STAGE, :], a["w_exp"][e * P:(e + 1) * P, :]
                             ).then_inc(s_expert[e % STAGE], 16)
            with sp.Fori(0, CHUNKS) as c:
                sp.wait_ge(final_sb, c + 2)
                sp.dma_start(out[bass.ds(c * CHUNK, CHUNK), :].rearrange("(t p) d -> p t d", p=P),
                             x_tok[:, bass.ds(c * CHUNK_TILES, CHUNK_TILES), :]).then_inc(s_out, 16)
            sp.wait_ge(s_out, 16 * CHUNKS)

        @block.gpsimd
        def _(pool):
            nc.gpsimd.memset(x_tok[:, TILES - 1, :], 0.0).then_inc(s_zero, 1)
            pool.wait_ge(s_idx, 32)
            pool.wait_ge(s_zero, 1)
            for t in range(TXT_TILES):
                rows = P if t < TXT_TILES - 1 else LAST_ROWS
                pool.indirect_dma_start(
                    out=x_tok[0:rows, IMG_TILES + t, :], out_offset=None, in_=a["item_emb"],
                    in_offset=bass.IndirectOffsetOnAxis(ap=idx[0:rows, t:t + 1], axis=0)
                ).then_inc(s_gather[0 if t < 4 else 1 if t < 7 else 2], 16)
            nc.gpsimd.memset(eps_t[:], EPS).then_inc(s_zero, 1)
            nc.gpsimd.memset(half_t[:], -0.5).then_inc(s_zero, 1)
            pool.wait_ge(s_zero, 3)
            for g, group in enumerate(TXT_GROUPS):
                norm_root(pool, group, g + 1)
            nc.gpsimd.memset(ctxT[:, T0 + TXT_TOKENS:COLS], 0.0).then_inc(s_zero, 1)
            nc.gpsimd.memset(v_joint[:], 1.0).then_inc(s_zero, 1)
            nc.gpsimd.memset(gateT[:].bitcast(F32), 0.0).then_inc(s_zero, 1)
            pool.wait_ge(s_zero, 6)
            pool.wait_ge(s_const, 16)
            with pool.Fori(0, LAYERS) as l:
                for b in range(B):
                    if b in (0, 7, 13):
                        pool.wait_ge(k_sb, l * NG + {0: 1, 7: 2, 13: NG}[b])
                    if b < 2:
                        if b == 1:
                            pool.wait_ge(k_sb, l * NG + NG)
                    else:
                        pool.wait_ge(scores_psum, l * B + (b - 1))
                    spread_keys(b % 2, S_TXT, [(T0 + b * S_TXT, S_TXT)])
                    if b == 3:
                        pool.wait_ge(xn_ready, norm_no(l, NG))
                        pool.wait_ge(s_row, l * 16 + 16)
                        nc.gpsimd.tensor_tensor(x_tok[:, IMG_TILES:, :], x_tok[:, IMG_TILES:, :],
                                                row_of(row[:, R_BO:R_BO + D], TXT_TILES),
                                                ALU.add).then_inc(bias_added, 1)
                for g, group in enumerate(TXT_GROUPS):
                    norm_root(pool, group, norm_no(l, NG + g + 1))
                pool.wait_ge(tok_den, l + 1)
                nc.gpsimd.tensor_tensor(ratio_t[:], ratio_t[:], gate_t[:], ALU.mult).then_inc(tok_part, 1)
                pool.wait_ge(tok_part, l * 2 + 1)
                nc.gpsimd.tensor_tensor(ratio_t[:], ratio_t[:], inner_t[:], ALU.mult).then_inc(tok_part, 1)
                for g, (t0, nt) in enumerate(TXT_GROUPS):
                    pool.wait_ge(xn_ready, norm_no(l, NG + g + 1))
                    nc.gpsimd.tensor_tensor(x_tok[:, t0:t0 + nt, :], x_tok[:, t0:t0 + nt, :],
                                            row_of(row[:, R_B2:R_B2 + D], nt), ALU.add).then_inc(bias_added, 1)
                n = norm_no(l, 2 * NG + 1)
                pool.wait_ge(ln_mv, n)
                nc.gpsimd.tensor_tensor(img_veps[:], img_mv[:, :, 1], eps_t[:, 0:TOK_TILES], ALU.add).then_inc(ln_eps, 1)
                pool.wait_ge(ln_eps, n)
                nc.gpsimd.tensor_tensor(img_rstd[:], img_veps[:], half_t[:, 0:TOK_TILES], ALU.pow).then_inc(ln_rstd, 1)
                for g, group in enumerate(TXT_GROUPS):
                    norm_root(pool, group, norm_no(l, 2 * NG + g + 2))
            base = norm_no(LAYERS, NG)
            for g, (t0, nt) in enumerate(TXT_GROUPS):
                if g == 0:
                    continue
                pool.wait_ge(xn_ready, base - NG + g + 1)
                nc.gpsimd.tensor_tensor(x_norm[:, t0:t0 + nt, :], x_norm[:, t0:t0 + nt, :],
                                        row_of(jrow[:, JR_FG:JR_FG + D], nt), ALU.mult).then_inc(gained, 1)
                pool.wait_ge(gained, g)
                nc.gpsimd.tensor_tensor(x_tok[:, t0:t0 + nt, :], x_norm[:, t0:t0 + nt, :],
                                        row_of(jrow[:, JR_FB:JR_FB + D], nt), ALU.add).then_inc(txt_done, 1)
            for g, group in enumerate(TXT_GROUPS):
                norm_root(pool, group, base + g + 1)
            for b in range(B):
                if b == 0:
                    pool.wait_ge(k_sb, LAYERS * NG + NA)
                if b >= 2:
                    pool.wait_ge(scores_psum, LAYERS * B + 2 * (b - 1))
                spread_keys(b % 2, K_JOINT, [(b * S_IMG, S_IMG), (T0 + b * S_TXT, K_JOINT - S_IMG)])
                if b == 3:
                    pool.wait_ge(xn_ready, base + NG)
                    pool.wait_ge(s_joint, 48)
                    nc.gpsimd.tensor_tensor(x_tok[:], x_tok[:], row_of(jrow[:, JR_BO:JR_BO + D], TILES),
                                            ALU.add).then_inc(bias_added, 1)
                if b in (10, 11, 14, 15):
                    g = (10, 11, 14, 15).index(b)
                    s = group_cols(OUT_GROUPS[g])
                    pool.wait_ge(ctxT_sb, LAYERS * 4 + (4 if g < 2 else 6))
                    nc.gpsimd.tensor_tensor(uT[:, s], uT[:, s], ctxT[:, s], ALU.mult).then_inc(ctx_u, 1)
                if b in (14, 15):
                    norm_root(pool, OUT_GROUPS[b - 14], base + NG + b - 13)
                for e in range(max(b - 2, 0), b - 1 if b < B - 1 else E + 1):
                    if e in (15, 16):
                        norm_root(pool, OUT_GROUPS[e - 13], base + NG + e - 12)
                    if e == E:
                        pool.wait_ge(ctxT_sb, LAYERS * 4 + 8)
                        for g in (4, 5):
                            s = group_cols(OUT_GROUPS[g])
                            nc.gpsimd.tensor_tensor(uT[:, s], uT[:, s], ctxT[:, s], ALU.mult).then_inc(ctx_u, 1)
                    pool.wait_ge(whi_sb, e + 1)
                    nc.gpsimd.tensor_tensor(w_lo[:, e, :], w_stage[:, e % STAGE, :], w_hi[:, e, :].bitcast(F32),
                                            ALU.subtract).then_inc(wlo_sb, 1)
            for g, group in enumerate(OUT_GROUPS):
                if g < 2:
                    norm_root(pool, OUT_GROUPS[OUT_EARLY + g], base + NG + OUT_EARLY + g + 1)
                s = group_cols(group)
                pool.wait_ge(hhi_sb, g + 1)
                nc.gpsimd.tensor_tensor(h_lo[:, s], hT[:, s], h_hi[:, s].bitcast(F32),
                                        ALU.subtract).then_inc(hlo_sb, 1)

            def low_part(c, r):
                if taken(c, r):
                    pool.wait_ge(hghi_sb, c * ROUND + (r + 1))
                    if r >= 2:
                        pool.wait_ge(d_psum, c * ROUND + (r - 1))
                    nc.gpsimd.tensor_tensor(hg_lo[:, r % 2, :], hg_t[:, r % 2, :], hg_hi[:, r % 2, :].bitcast(F32),
                                            ALU.subtract).then_inc(hglo_sb, 1)

            expert_steps(pool, low_part)

        @block.scalar
        def _(act):
            act.dma_start(noise[:, 0:6], a["noise_cols"]).then_inc(s_noise, 16)
            act.dma_start(noise[:, 6:6 + 2 * D], a["noise_rows"].broadcast_to([P, 2 * D])).then_inc(s_noise, 16)
            act.dma_start(tok_w[:].rearrange("p m c o -> p (m c o)"), a["tok_w"]).then_inc(s_tokin, 16)
            act.dma_start(tok_sw[:].rearrange("p m c o -> p (m c o)"), a["tok_sw"]).then_inc(s_tokin, 16)
            act.dma_start(tok_w3[:], a["tok_w3"]).then_inc(s_tokin, 16)
            act.dma_start(tok_b[:], a["tok_b"]).then_inc(s_tokin, 16)
            act.dma_start(jrow[:], a["jrow"].broadcast_to([P, JR_ALL])).then_inc(s_joint, 16)
            act.dma_start(jw[:], a["jw"]).then_inc(s_joint, 16)
            act.dma_start(jvec[:], a["jvec"]).then_inc(s_joint, 16)
            act.dma_start(w_gate[:], a["w_gate"]).then_inc(s_gate, 16)
            act.wait_ge(s_noise, 32)
            nc.scalar.activation(noise_abs[:], noise[:], ACT.Abs).then_inc(s_act, 1)
            nc.scalar.activation(noise_sign[:], noise[:], ACT.Sign).then_inc(s_act, 1)
            act.wait_ge(s_act, 2)
            nc.scalar.activation(noise_root[:], noise_abs[:], ACT.Sqrt).then_inc(noise_ready, 1)

            def text_ctx(g):
                w = 4 * S_TXT
                nc.scalar.activation(ctxT[:, T0 + g * w:T0 + (g + 1) * w], ps[:, 7, 0:w],
                                     ACT.Copy).then_inc(ctxT_sb, 1)

            def joint_ctx(g):
                wi, wt = 2 * S_IMG, 2 * S_TXT
                nc.scalar.activation(ctxT[:, g * wi:(g + 1) * wi], ps[:, 7, 0:wi], ACT.Copy)
                nc.scalar.activation(ctxT[:, T0 + g * wt:T0 + (g + 1) * wt], ps[:, 7, wi:wi + wt],
                                     ACT.Copy).then_inc(ctxT_sb, 1)

            def norm_out(group, n, bank, gain=None, shift=None):
                act.wait_ge(xT_psum, n)
                dst, src = hT[:, group_cols(group)], ps[:, bank, 0:group[1] * P]
                if gain is None:
                    ins = nc.scalar.activation(dst, src, ACT.Copy)
                else:
                    ins = nc.scalar.activation(dst, src, ACT.Identity, bias=shift, scale=gain)
                ins.then_inc(hT_sb, 1)

            with act.Fori(0, LAYERS) as l:
                act.wait_ge(s_vec, l * 16 + 16)
                for what, g in QK_ORDER:
                    if what == "T":
                        norm_out(TXT_GROUPS[g], l * (2 * NG) + (g + 1), T1_BANKS[g],
                                 vec[:, V_G1:V_G1 + 1], vec[:, V_B1:V_B1 + 1])
                    elif what == "QK":
                        act.wait_ge(k_psum, l * NG + (g + 1))
                        nc.scalar.activation(kT[:, group_cols(TXT_GROUPS[g])],
                                             ps[:, K_BANKS[g], 0:TXT_GROUPS[g][1] * P],
                                             ACT.Identity, bias=vec[:, V_BK:V_BK + 1]).then_inc(k_sb, 1)

                def text_beside(i):
                    if i == 16:
                        norm_out(TXT_GROUPS[0], l * (2 * NG) + (NG + 1), T2_BANKS[0],
                                 vec[:, V_G2:V_G2 + 1], vec[:, V_B2:V_B2 + 1])
                    if i == 5:
                        act.wait_ge(tok_cap, l + 1)
                        nc.scalar.activation(exp_t[:], cap_t[:], ACT.Exp).then_inc(tok_exp, 1)

                attend_act(act, text_units(), lambda k: l * B + k, text_ctx, text_beside)
                for what, f in FFN_ORDER:
                    if what in ("W", "I", "O"):
                        continue
                    if what == "T":
                        norm_out(TXT_GROUPS[f], l * (2 * NG) + (NG + f + 1), T2_BANKS[f],
                                 vec[:, V_G2:V_G2 + 1], vec[:, V_B2:V_B2 + 1])
                        continue
                    g, j = what, what * FF + f
                    if g == 2 and f == 0:
                        act.wait_ge(w2_psum, l * NG + 1)
                    act.wait_ge(w1_psum, l * (NG * FF) + (j + 1))
                    nt = TXT_GROUPS[g][1]
                    nc.scalar.activation(gelu_t[:, g % 2, f, 0:nt * P], ps[:, HIDDEN_BANKS[j % 5], 0:nt * P],
                                         ACT.Gelu, bias=vec[:, V_BF + f:V_BF + f + 1]).then_inc(gelu_sb, 1)
            base = LAYERS * 2 * NG
            act.wait_ge(s_joint, 48)
            for what, g in JOINT_ORDER:
                group = ALL_GROUPS[g]
                if what == "T":
                    norm_out(group, base + g + 2, g)
                if what != "QKU":
                    continue
                act.wait_ge(k_psum, LAYERS * NG + g + 1)
                nc.scalar.activation(kT[:, group_cols(group)], ps[:, 6, 0:group[1] * P], ACT.Identity,
                                     bias=jvec[:, JV_BK:JV_BK + 1]).then_inc(k_sb, 1)
                act.wait_ge(u_psum, g + 1)
                nc.scalar.activation(uT[:, group_cols(group)], ps[:, 7, 0:group[1] * P], ACT.Identity,
                                     bias=jvec[:, JV_BU:JV_BU + 1]).then_inc(u_sb, 1)

            def tanh_context(groups):
                for group in groups:
                    s = group_cols(group)
                    nc.scalar.activation(hT[:, s], ctxT[:, s], ACT.Tanh, scale=0.5).then_inc(tanh_ctx, 1)

            def joint_beside(i):
                if i in (19, 27):
                    act.wait_ge(ctxT_sb, LAYERS * 4 + (4 if i == 19 else 6))
                if i in (19, 20, 27, 28):
                    g = (19, 20, 27, 28).index(i)
                    tanh_context(OUT_GROUPS[g:g + 1])
                if i in (32, 33):
                    norm_out(OUT_GROUPS[i - 32], base + NA + i - 30, OUT_BANKS[i - 32])
                if i == 2 * B + 2:
                    act.wait_ge(ctxT_sb, LAYERS * 4 + 8)
                    tanh_context(OUT_GROUPS[4:6])
                if i >= 2 and i % 2 == 0:
                    e = i // 2 - 1
                    act.wait_ge(s_expert[e % STAGE], 16 * (e // STAGE + 1))
                    nc.scalar.activation(w_hi[:, e, :], w_stage[:, e % STAGE, :], ACT.Copy).then_inc(whi_sb, 1)

            attend_act(act, joint_units(), lambda k: LAYERS * B + k, joint_ctx, joint_beside)
            act.wait_ge(s_zero, 6)
            nc.scalar.activation(table_carrier[:], eps_t[0:1, 0:1], ACT.Sigmoid)
            def affinities(part):
                r0, r1 = ROUTE_PARTS[part]
                act.wait_ge(lg_psum, part + 1)
                nc.scalar.activation(kT[:, r0 * E:r1 * E], ps[:, LOGIT_BANKS[part], r0 * E:r1 * E],
                                     ACT.Sigmoid).then_inc(aff_sb, 1)

            def high_part(g):
                s = group_cols(OUT_GROUPS[g])
                act.wait_ge(hT_sb, base + NA + g + 1)
                nc.scalar.activation(h_hi[:, s], hT[:, s], ACT.Copy).then_inc(hhi_sb, 1)

            for g in range(2, OUT_EARLY):
                norm_out(OUT_GROUPS[g], base + NA + g + 2, OUT_BANKS[g])
            for g in range(OUT_EARLY):
                high_part(g)
            affinities(0)
            for g in range(OUT_EARLY, NO):
                norm_out(OUT_GROUPS[g], base + NA + g + 2, OUT_BANKS[g])
            affinities(1)
            for g in range(OUT_EARLY, NO):
                high_part(g)
            nc.scalar.activation(table_carrier[:], eps_t[0:1, 0:1], ACT.Silu)
            def take_gates(g):
                act.wait_ge(gT_psum, g + 1)
                nc.scalar.activation(gateT[0:2 * E, group_cols(OUT_GROUPS[g])],
                                     ps[0:2 * E, GATE_BANKS[g], 0:OUT_GROUPS[g][1] * P], ACT.Copy).then_inc(gT_sb, 1)

            def expert_act(c, r):
                if taken(c, r):
                    act.wait_ge(g_psum, c * ROUND + (r + 1))
                    if r >= 2:
                        act.wait_ge(su_sb, c * ROUND + (r - 1))
                    nc.scalar.activation(silu_t[:, r % 2, :], ps[:, r % 2, 0:CHUNK], ACT.Silu).then_inc(silu_sb, 1)
                    if r == 0:
                        for g in range(OUT_EARLY):
                            take_gates(g)
                if r >= 1 and taken(c, r - 1):
                    j = r - 1
                    act.wait_ge(hg_sb, c * ROUND + (j + 1))
                    if j >= 2:
                        act.wait_ge(d_psum, c * ROUND + (j - 1))
                    nc.scalar.activation(hg_hi[:, j % 2, :], hg_t[:, j % 2, :], ACT.Copy).then_inc(hghi_sb, 1)
                if isinstance(c, int) and c == 0 and r in (10, 12):
                    take_gates(OUT_EARLY + (r - 10) // 2)
                if r >= 3 and (r - 3) % (E + 1) == E:
                    k = (r - 3) // (E + 1)
                    act.wait_ge(d_psum, c * ROUND + (k + 1) * (E + 1))
                    nc.scalar.activation(oT_t[:], ps[:, 6 + k % 2, 0:CHUNK], ACT.Copy).then_inc(oT_sb, 1)

            expert_steps(act, expert_act)

        @block.tensor
        def _(pe):
            pe.wait_ge(s_const, 16)
            pe.wait_ge(s_masks, 1)

            norm_transpose(pe, TXT_GROUPS[0], 1, T1_BANKS[0])
            with pe.Fori(0, LAYERS) as l:
                pe.wait_ge(s_wqkv, l * 16 + 16)

                def values(j):
                    if j == 1:
                        pe.wait_ge(q_sb, l * NG + 2)
                        pe.wait_ge(hT_sb, l * (2 * NG) + 2)
                    for b in range(4 * j, 4 * j + 4):
                        col = T0 + b * S_TXT
                        last = nc.tensor.matmul(ps[0:S_TXT, V_BANKS[j], (b % 4) * D:(b % 4 + 1) * D],
                                                hT[:, col:col + S_TXT], w_qkv_t[:, 2 * D:3 * D],
                                                start=True, stop=True)
                    last.then_inc(v_psum, 1)

                for what, g in QK_ORDER:
                    if what == "V":
                        values(g)
                        continue
                    if what == "T":
                        if g >= 1:
                            norm_transpose(pe, TXT_GROUPS[g], norm_no(l, g + 1), T1_BANKS[g])
                        continue
                    t0, nt = TXT_GROUPS[g]
                    pe.wait_ge(hT_sb, l * (2 * NG) + (g + 1))
                    rhs = hT[:, t0 * P:(t0 + nt) * P]
                    nc.tensor.matmul(ps[:, Q_BANKS[g], 0:nt * P], w_qkv_t[:, 0:D], rhs,
                                     start=True, stop=True).then_inc(q_psum, 1)
                    nc.tensor.matmul(ps[:, K_BANKS[g], 0:nt * P], w_qkv_t[:, D:2 * D], rhs,
                                     start=True, stop=True).then_inc(k_psum, 1)
                pe.wait_ge(q_sb, l * NG + NG)
                pe.wait_ge(k_sb, l * NG + NG)

                def added(i):
                    if i in TOK_STEPS:
                        pe.wait_ge(tok_taken, l * 3 + (TOK_STEPS[i] + 1))
                    else:
                        pe.wait_ge(x_upd, l * ADDS + (1 + list(TXT_SPARE).index(i)))

                def project(i):
                    if i in TOK_STEPS:
                        k = TOK_STEPS[i]
                        if k == 0:
                            pe.wait_ge(tokw_ready, 1)
                            pe.wait_ge(s_tokin, 16 * 5)
                        tok = bass.ds(l * (TOK_TILES * P) + k * P, P)
                        for m in range(2):
                            at = SPARE_COL + m * P
                            for h in range(2):
                                last = nc.tensor.matmul(ps[:, 6, at:at + P], tok_w[:, m, h, :],
                                                        patches[:, h, tok], start=(h == 0), stop=(h == 1))
                        last.then_inc(tok_psum, 1)
                        return
                    t0, nt, ctx_groups = TXT_SPARE[i]
                    pe.wait_ge(s_wo, l * 16 + 16)
                    pe.wait_ge(ctxT_sb, l * 4 + ctx_groups)
                    project_tokens(w_o_t[:], ctxT, t0, nt, 6, SPARE_COL).then_inc(wo_psum, 1)

                def project_second(i):
                    if i == 1:
                        values(3)
                    if i == 16:
                        pe.wait_ge(ctxT_sb, l * 4 + 3)
                        project_tokens(w_o_t[:], ctxT, TXT_GROUPS[1][0], TXT_GROUPS[1][1], 0).then_inc(wo_psum, 1)

                def hidden(g, f):
                    (t0, nt), j = TXT_GROUPS[g], g * FF + f
                    pe.wait_ge(hT_sb, l * (2 * NG) + (NG + g + 1))
                    if j >= 5:
                        pe.wait_ge(gelu_sb, l * (NG * FF) + (j - 4))
                    nc.tensor.matmul(ps[:, HIDDEN_BANKS[j % 5], 0:nt * P], w_1_t[:, f * D:(f + 1) * D],
                                     hT[:, t0 * P:(t0 + nt) * P], start=True, stop=True).then_inc(w1_psum, 1)

                def hidden_first(i):
                    if i == 16:
                        norm_transpose(pe, TXT_GROUPS[0], norm_no(l, NG + 1), T2_BANKS[0])
                    if i == 17:
                        pe.wait_ge(s_w1, l * 16 + 16)
                        hidden(0, 0)

                attend_pe(pe, text_units(), Passed(l), lambda k: l * B + k, [*TXT_SPARE, *TOK_STEPS], project, added,
                          project_second, hidden_first)
                for what, f in FFN_ORDER[1:]:
                    if what == "O":
                        pe.wait_ge(ctxT_sb, l * 4 + 4)
                        project_tokens(w_o_t[:], ctxT, TXT_GROUPS[f][0], TXT_GROUPS[f][1], 4).then_inc(wo_psum, 1)
                    elif what == "I":
                        pe.wait_ge(tok_mid, l + 1)
                        pe.wait_ge(gelu_sb, l * (NG * FF) + 2 * FF)
                        project_tokens(tok_w3[:], mid_t, 0, TOK_TILES, TOK_BANK).then_inc(tok_psum, 1)
                    elif what == "T":
                        norm_transpose(pe, TXT_GROUPS[f], norm_no(l, NG + f + 1), T2_BANKS[f])
                    elif what == "W":
                        t0, nt = TXT_GROUPS[f]
                        if f == 0:
                            pe.wait_ge(s_w2, l * 16 + 16)
                        pe.wait_ge(gelu_sb, l * (NG * FF) + FF * (f + 1))
                        for t in range(nt):
                            if (f, t) == (2, nt - 1):
                                norm_transpose(pe, TXT_GROUPS[0], norm_no(l, 2 * NG + 2), T1_BANKS[0])
                            for k in range(FF):
                                last = nc.tensor.matmul(ps[:, W2_BANKS[f], t * P:(t + 1) * P],
                                                        gelu_t[:, f % 2, k, t * P:(t + 1) * P], w_2_t[:, k, :],
                                                        start=(k == 0), stop=(k == FF - 1))
                        last.then_inc(w2_psum, 1)
                    else:
                        hidden(what, f)
            base = norm_no(LAYERS, NG)
            hbase = LAYERS * 2 * NG
            pe.wait_ge(s_joint, 48)
            pe.wait_ge(x_upd, LAYERS * ADDS)
            def joint_values(j):
                pe.wait_ge(hT_sb, hbase + (3, 4, 4, 5)[j])
                for b in range(4 * j, 4 * j + 4):
                    s = slice((b % 4) * D, (b % 4 + 1) * D)
                    nc.tensor.matmul(ps[0:S_IMG, 1 + j, s], hT[:, b * S_IMG:(b + 1) * S_IMG],
                                     jw[:, 2 * D:3 * D], start=True, stop=True)
                    col = T0 + b * S_TXT
                    last = nc.tensor.matmul(ps[S_IMG:K_JOINT, 1 + j, s], hT[:, col:col + K_JOINT - S_IMG],
                                            jw[:, 2 * D:3 * D], start=True, stop=True)
                last.then_inc(v_psum, 1)

            for what, g in JOINT_ORDER:
                if what == "V":
                    joint_values(g)
                    continue
                t0, nt = ALL_GROUPS[g]
                if what == "T":
                    norm_transpose(pe, (t0, nt), base + g + 1 - NI if g >= NI else base - NG, g)
                    continue
                pe.wait_ge(hT_sb, hbase + g + 1)
                rhs = hT[:, t0 * P:(t0 + nt) * P]
                for m, b, psum_sem, sb_sem in ((0, 5, q_psum, q_sb), (1, 6, k_psum, k_sb), (3, 7, u_psum, u_sb)):
                    if g >= 1:
                        before = 0 if m == 3 else LAYERS * NG
                        pe.wait_ge(sb_sem, before + g)
                    nc.tensor.matmul(ps[:, b, 0:nt * P], jw[:, m * D:(m + 1) * D], rhs,
                                     start=True, stop=True).then_inc(psum_sem, 1)
            pe.wait_ge(q_sb, LAYERS * NG + NA)
            pe.wait_ge(k_sb, LAYERS * NG + NA)
            pe.wait_ge(u_sb, NA)
            pe.wait_ge(v_sb, LAYERS * 4 + 4)

            def added_joint(i):
                pe.wait_ge(x_joint, 1 + list(ALL_SPARE).index(i))

            def project_joint(i):
                t0, nt, gated_groups = ALL_SPARE[i]
                pe.wait_ge(gated_sb, gated_groups)
                project_tokens(jw[:, 4 * D:5 * D], uT, t0, nt, 6, SPARE_COL).then_inc(wo_psum, 1)

            def transpose_early(i):
                if i in (32, 33):
                    g = i - 32
                    norm_transpose(pe, OUT_GROUPS[g], base + NG + g + 1, OUT_BANKS[g])

            attend_pe(pe, joint_units(), Passed(LAYERS), lambda k: LAYERS * B + k, ALL_SPARE, project_joint,
                      added_joint, after=transpose_early)

            def logits(part):
                r0, r1 = ROUTE_PARTS[part]
                for r in range(r0, r1):
                    t = ROUTE_TILES[r]
                    last = nc.tensor.matmul(ps[:, LOGIT_BANKS[part], r * E:(r + 1) * E], hT[:, t * P:(t + 1) * P],
                                            w_gate[:], start=True, stop=True)
                last.then_inc(lg_psum, 1)

            for g in range(2, OUT_EARLY):
                norm_transpose(pe, OUT_GROUPS[g], base + NG + g + 1, OUT_BANKS[g])
            pe.wait_ge(gated_sb, NO)
            for g in (4, 5):
                t0, nt = OUT_GROUPS[g]
                project_tokens(jw[:, 4 * D:5 * D], uT, t0, nt, 4 if g == 4 else 5).then_inc(wo_psum, 1)
            pe.wait_ge(s_gate, 16)
            pe.wait_ge(hT_sb, hbase + NA + OUT_EARLY)
            logits(0)
            for g in (4, 5):
                norm_transpose(pe, OUT_GROUPS[g], base + NG + g + 1, OUT_BANKS[g])
            pe.wait_ge(hT_sb, hbase + NA + NO)
            logits(1)
            def transpose_gates(g):
                t0, nt = OUT_GROUPS[g]
                for k in range(nt):
                    r = ROUTE_TILES.index(t0 + k)
                    last = nc.tensor.transpose(ps[0:2 * E, GATE_BANKS[g], k * P:(k + 1) * P],
                                               gates[:, r, :].bitcast(F32), ident)
                last.then_inc(gT_psum, 1)

            pe.wait_ge(hlo_sb, OUT_EARLY)
            pe.wait_ge(wlo_sb, E + 1)
            def split_product(dst, w, e, x_hi, x_lo, start=True, stop=True):
                nc.tensor.matmul(dst, w_lo[:, e, w * D:(w + 1) * D], x_hi, start=start, stop=False)
                nc.tensor.matmul(dst, w_hi[:, e, w * D:(w + 1) * D], x_hi, start=False, stop=False)
                return nc.tensor.matmul(dst, w_hi[:, e, w * D:(w + 1) * D], x_lo, start=False, stop=stop)

            def expert_pe(c, r):
                k, e = divmod(r, E + 1)
                if r == ROUND:
                    pe.wait_ge(gT_sb, NO)
                    pe.wait_ge(hlo_sb, NO)
                if taken(c, r):
                    tok = slice((2 * c + k) * CHUNK, (2 * c + k + 1) * CHUNK) if isinstance(c, int) else \
                        bass.ds(c * (2 * CHUNK) + k * CHUNK, CHUNK)
                    if r >= 2:
                        pe.wait_ge(silu_sb, c * ROUND + (r - 1))
                    split_product(ps[:, r % 2, 0:CHUNK], 0, e, h_hi[:, tok], h_lo[:, tok]).then_inc(g_psum, 1)
                    if r >= 2:
                        pe.wait_ge(su_sb, c * ROUND + (r - 1))
                    split_product(ps[:, 2 + r % 2, 0:CHUNK], 1, e, h_hi[:, tok], h_lo[:, tok]).then_inc(up_psum, 1)
                    if r == 0:
                        pe.wait_ge(gates_sb, 1)
                        pe.wait_ge(aff_sb, 2)
                        for g in range(OUT_EARLY):
                            transpose_gates(g)
                        pe.wait_ge(gT_sb, OUT_EARLY)
                    if e < E:
                        if r >= 2:
                            pe.wait_ge(hg_sb, c * ROUND + (r - 1))
                        nc.tensor.matmul(ps[:, 4 + r % 2, 0:CHUNK], select[:, e, :], gateT[:, tok],
                                         start=True, stop=True).then_inc(gb_psum, 1)
                if r >= 2 and taken(c, r - 2):
                    j = r - 2
                    kj, ej = divmod(j, E + 1)
                    pe.wait_ge(hglo_sb, c * ROUND + (j + 1))
                    if ej == 0 and kj >= 1:
                        pe.wait_ge(final_sb, c * 2 + kj)
                    split_product(ps[:, 6 + kj % 2, 0:CHUNK], 2, ej, hg_hi[:, j % 2, :], hg_lo[:, j % 2, :],
                                  start=(ej == 0), stop=(ej == E)).then_inc(d_psum, 1)
                if isinstance(c, int) and c == 0 and r in (9, 11):
                    g = OUT_EARLY + (r - 9) // 2
                    pe.wait_ge(gates_sb, 2)
                    pe.wait_ge(gT_sb, g)
                    transpose_gates(g)
                if r >= 4 and (r - 4) % (E + 1) == E:
                    kj = (r - 4) // (E + 1)
                    pe.wait_ge(oT_sb, c * 2 + (kj + 1))
                    for t in range(CHUNK_TILES):
                        last = nc.tensor.transpose(ps[:, 6 + kj, t * P:(t + 1) * P],
                                                   oT_t[:, t * P:(t + 1) * P], ident)
                    last.then_inc(oT_psum, 1)

            expert_steps(pe, expert_pe)

        @block.vector
        def _(dve):
            chain = [0]

            def link(ins):
                chain[0] += 1
                ins.then_inc(s_dve, 1)
                dve.wait_ge(s_dve, chain[0])

            dve.wait_ge(s_const, 16)
            dve.wait_ge(s_txtin, 32)
            nc.vector.tensor_copy(ident_bf[:], ident)
            nc.vector.tensor_copy(mask_l_bf[:], const[:, C_MASKL:C_MASKL + S_TXT])
            nc.vector.tensor_copy(joint_mask[:], const[:, C_JOINT:C_JOINT + K_JOINT])
            nc.vector.tensor_copy(txt_mask[0:PAD_ROW], row_of(const[:, C_CAUSAL:C_CAUSAL + S_TXT], B, PAD_ROW))
            r = slice(PAD_ROW, PAD_ROW + 1)
            nc.vector.tensor_scalar(txt_mask[r].rearrange("p b k -> p (b k)"), pad_in[r, :], 0.0, FAR,
                                    ALU.is_equal, ALU.mult)
            link(nc.vector.tensor_scalar(pad_col1[0:S_TXT, :], pad_col[0:S_TXT, :], 0.0, -1.0,
                                         ALU.is_equal, ALU.mult))
            nc.vector.tensor_scalar(
                v_txt[0:S_TXT, :, :, HD], pad_col1[0:S_TXT, :].unsqueeze(2).broadcast_to([S_TXT, B, NH]),
                1.0, None, ALU.add)
            link(nc.vector.tensor_tensor(gsum[:, 0:E], ident[:, 0:E], ident[:, E:2 * E], ALU.add))
            nc.vector.tensor_copy(select[:], gsum[:, 0:E].unsqueeze(2).broadcast_to([P, E, P])
                                  ).then_inc(s_masks, 1)
            dve.wait_ge(s_pos, 32)
            for g, (t0, nt) in enumerate(TXT_GROUPS):
                dve.wait_ge(s_gather[g], 16 * nt)
                if g < NG - 1:
                    last = nc.vector.tensor_tensor(x_tok[:, t0:t0 + nt, :], x_tok[:, t0:t0 + nt, :],
                                                   x_norm[:, t0:t0 + nt, :], ALU.add)
                else:
                    m = slice(t0, TILES - 1)
                    nc.vector.tensor_tensor(x_tok[:, m, :], x_tok[:, m, :], x_norm[:, m, :], ALU.add)
                    last = nc.vector.tensor_tensor(x_tok[0:LAST_ROWS, TILES - 1, :], x_tok[0:LAST_ROWS, TILES - 1, :],
                                                   x_norm[0:LAST_ROWS, TILES - 1, :], ALU.add)
                last.then_inc(embedded, 1)
                dve.wait_ge(embedded, g + 1)
                tile_stats(t0, nt).then_inc(ln_stats, 1)
                norm_moments(dve, (t0, nt), g + 1)
                if g == 0:
                    norm_apply(dve, (t0, nt), g + 1)
            for g in (1, 2):
                norm_apply(dve, TXT_GROUPS[g], g + 1)
            dve.wait_ge(noise_ready, 1)
            dve.wait_ge(s_tokin, 16 * 5)
            link(nc.vector.tensor_tensor(noise[:], noise_root[:], noise_sign[:], ALU.mult))
            for m in range(2):
                for h in range(2):
                    nc.vector.scalar_tensor_tensor(
                        tok_sw[:, m, h, :], tok_sw[:, m, h, :], noise[:, 2 * m + h:2 * m + h + 1],
                        noise[:, 6 + m * D:6 + (m + 1) * D], ALU.mult, ALU.mult)
                last = nc.vector.scalar_tensor_tensor(tok_bn[:, m:m + 1], tok_b[:, 2 * m + 1:2 * m + 2],
                                                      noise[:, 4 + m:5 + m], tok_b[:, 2 * m:2 * m + 1],
                                                      ALU.mult, ALU.add)
            link(last)
            nc.vector.tensor_tensor(tok_w[:], tok_w[:], tok_sw[:], ALU.add).then_inc(tokw_ready, 1)
            dve.wait_ge(s_joint, 48)
            link(nc.vector.tensor_tensor(pos_b[:], const[:, C_POS:C_POS + D], jrow[:, JR_W3B:JR_W3B + D], ALU.add))

            def take_stats(tiles, n, group_done):
                dve.wait_ge(x_upd, n)
                last = tile_stats(*tiles)
                if group_done:
                    last.then_inc(ln_stats, 1)

            def tokenize(i, l):
                if i in (3, 4):
                    k = i - 3
                    dve.wait_ge(tok_psum, l * 3 + (k + 1))
                    for m, dst in enumerate((gate_t, inner_t)):
                        last = nc.vector.tensor_scalar(dst[:, k * P:(k + 1) * P],
                                                       ps[:, 6, SPARE_COL + m * P:SPARE_COL + (m + 1) * P],
                                                       tok_bn[:, m:m + 1], None, ALU.add)
                    last.then_inc(tok_taken, 1)
                if i == 4:
                    dve.wait_ge(tok_taken, l * 3 + 2)
                    nc.vector.tensor_scalar(cap_t[:], gate_t[:], EXP_CAP, None, ALU.min).then_inc(tok_cap, 1)

            def image_mid(l):
                dve.wait_ge(tok_exp, l + 1)
                nc.vector.scalar_tensor_tensor(ratio_t[:], exp_t[:], 2.0, exp_t[:], ALU.add, ALU.mult).then_inc(tok_num, 1)
                dve.wait_ge(tok_num, l + 1)
                nc.vector.tensor_scalar(exp_t[:], ratio_t[:], 2.0, None, ALU.add).then_inc(tok_den, 1)
                dve.wait_ge(tok_den, l + 1)
                nc.vector.reciprocal(cap_t[:], exp_t[:]).then_inc(tok_rec, 1)
                dve.wait_ge(tok_rec, l + 1)
                dve.wait_ge(tok_part, l * 2 + 2)
                nc.vector.tensor_tensor(mid_t[:], ratio_t[:], cap_t[:], ALU.mult).then_inc(tok_mid, 1)

            def image_out(l):
                dve.wait_ge(tok_psum, l * 3 + 3)
                out_ps = bank_cols(TOK_BANK, (0, TOK_TILES))
                nc.vector.tensor_tensor(x_tok[:, bass.ds(l * TOK_TILES, TOK_TILES), :], out_ps,
                                        row_of(pos_b[:], TOK_TILES), ALU.add)
                nc.vector.tensor_tensor(img_t[:], out_ps, row_of(pos_b[:], TOK_TILES), ALU.add
                                        ).then_inc(tok_taken, 1)
                dve.wait_ge(tok_taken, l * 3 + 3)
                nc.vector.memset(wait_carrier[:], 0.0)
                for t in range(TOK_TILES):
                    last = nc.vector.bn_stats(img_stats[:, t, :], img_t[:, t, :])
                last.then_inc(ln_stats, 1)
                dve.wait_ge(ln_stats, norm_no(l, 2 * NG + 1))
                nc.vector.memset(wait_carrier[:], 0.0)
                for t in range(TOK_TILES):
                    last = nc.vector.bn_aggr(img_mv[:, t, :], img_stats[:, t, :])
                last.then_inc(ln_mv, 1)

            def image_apply(l):
                dve.wait_ge(ln_rstd, norm_no(l, 2 * NG + 1))
                for t in range(TOK_TILES):
                    last = nc.vector.tensor_scalar(x_norm[:, bass.ds(l * TOK_TILES + t, 1), :],
                                                   img_t[:, t:t + 1, :], img_mv[:, t, 0:1],
                                                   img_rstd[:, t:t + 1], ALU.subtract, ALU.mult)
                last.then_inc(xn_ready, 1)

            with dve.Fori(0, LAYERS) as l:
                dve.wait_ge(s_row, l * 16 + 16)
                dve.wait_ge(s_vec, l * 16 + 16)

                def take_values(j):
                    dve.wait_ge(v_psum, l * 4 + (j + 1))
                    nc.vector.tensor_tensor(
                        v_txt[0:S_TXT, 4 * j:4 * j + 4, :, 0:HD],
                        ps[0:S_TXT, V_BANKS[j], :].rearrange("p (b h w) -> p b h w", b=4, w=HD),
                        row[0:S_TXT, R_BV:R_BV + D].rearrange("p (h w) -> p h w", w=HD).unsqueeze(1)
                        .broadcast_to([S_TXT, 4, NH, HD]), ALU.add).then_inc(v_sb, 1)

                for what, g in QK_ORDER:
                    if what == "QK":
                        dve.wait_ge(q_psum, l * NG + (g + 1))
                        nc.vector.tensor_scalar(qT[:, group_cols(TXT_GROUPS[g])],
                                                ps[:, Q_BANKS[g], 0:TXT_GROUPS[g][1] * P],
                                                vec[:, V_BQ:V_BQ + 1], float(Q_SCALE), ALU.add, ALU.mult
                                                ).then_inc(q_sb, 1)
                    elif what == "V":
                        take_values(g)

                def second_norm(k):
                    return norm_no(l, NG + k)

                def text_beside(i):
                    if i == 1:
                        take_values(3)
                    tokenize(i, l)
                    add_context(i)

                def add_context(i):
                    if i in TXT_SPARE:
                        k = list(TXT_SPARE).index(i)
                        t0, nt, _ = TXT_SPARE[i]
                        if k == 0:
                            dve.wait_ge(bias_added, l * (1 + NG) + 1)
                        dve.wait_ge(wo_psum, l * TXT_ADDS + (k + 1))
                        nc.vector.tensor_tensor(x_tok[:, t0:t0 + nt, :], x_tok[:, t0:t0 + nt, :],
                                                bank_cols(6, (t0, nt), SPARE_COL), ALU.add).then_inc(x_upd, 1)
                        take_stats((t0, nt), l * ADDS + (k + 1), i == 12)
                    if i == 13:
                        norm_moments(dve, TXT_GROUPS[0], second_norm(1))
                    if i == 15:
                        norm_apply(dve, TXT_GROUPS[0], second_norm(1))
                    if i == 16:
                        t0, nt = TXT_GROUPS[1]
                        dve.wait_ge(wo_psum, l * TXT_ADDS + 3)
                        nc.vector.tensor_tensor(x_tok[:, t0:t0 + nt, :], x_tok[:, t0:t0 + nt, :],
                                                bank_cols(0, (t0, nt)), ALU.add).then_inc(x_upd, 1)
                        take_stats((t0, nt), l * ADDS + 3, True)
                    if i == 17:
                        norm_moments(dve, TXT_GROUPS[1], second_norm(2))

                attend_dve(dve, text_units(), lambda k: l * B + k, text_beside)
                norm_apply(dve, TXT_GROUPS[1], second_norm(2))
                t0, nt = TXT_GROUPS[2]
                dve.wait_ge(wo_psum, l * TXT_ADDS + TXT_ADDS)
                nc.vector.tensor_tensor(x_tok[:, t0:t0 + nt, :], x_tok[:, t0:t0 + nt, :], bank_cols(4, (t0, nt)),
                                        ALU.add).then_inc(x_upd, 1)
                take_stats((t0, nt), l * ADDS + TXT_ADDS, True)
                norm_moments(dve, TXT_GROUPS[2], second_norm(3))
                norm_apply(dve, TXT_GROUPS[2], second_norm(3))
                image_mid(l)
                for g, (t0, nt) in enumerate(TXT_GROUPS):
                    if g == 0:
                        image_out(l)
                    dve.wait_ge(bias_added, l * (1 + NG) + (g + 2))
                    dve.wait_ge(w2_psum, l * NG + (g + 1))
                    nc.vector.tensor_tensor(x_tok[:, t0:t0 + nt, :], x_tok[:, t0:t0 + nt, :],
                                            bank_cols(W2_BANKS[g], (t0, nt)), ALU.add).then_inc(x_upd, 1)
                    take_stats((t0, nt), l * ADDS + (TXT_ADDS + g + 1), True)
                    norm_moments(dve, (t0, nt), second_norm(NG + g + 2))
                    if g == 0:
                        image_apply(l)
                        norm_apply(dve, TXT_GROUPS[0], second_norm(NG + 2))
                    if g == 2:
                        norm_apply(dve, TXT_GROUPS[1], second_norm(NG + 3))
                norm_apply(dve, TXT_GROUPS[NG - 1], second_norm(2 * NG + 1))
            def joint_q(g):
                group = ALL_GROUPS[g]
                dve.wait_ge(q_psum, LAYERS * NG + g + 1)
                nc.vector.tensor_scalar(qT[:, group_cols(group)], ps[:, 5, 0:group[1] * P],
                                        jvec[:, JV_BQ:JV_BQ + 1], float(Q_SCALE), ALU.add, ALU.mult
                                        ).then_inc(q_sb, 1)

            base = norm_no(LAYERS, NG)
            joint_q(0)
            t0, nt = TXT_GROUPS[0]
            dve.wait_ge(xn_ready, base)
            link(nc.vector.tensor_tensor(x_norm[:, t0:t0 + nt, :], x_norm[:, t0:t0 + nt, :],
                                         row_of(jrow[:, JR_FG:JR_FG + D], nt), ALU.mult))
            link(nc.vector.tensor_tensor(x_tok[:, t0:t0 + nt, :], x_norm[:, t0:t0 + nt, :],
                                         row_of(jrow[:, JR_FB:JR_FB + D], nt), ALU.add))

            def joint_moments(g):
                if g >= 1:
                    dve.wait_ge(txt_done, g)
                tile_stats(*TXT_GROUPS[g]).then_inc(ln_stats, 1)
                norm_moments(dve, TXT_GROUPS[g], base + g + 1)

            joint_moments(0)
            joint_moments(1)
            norm_apply(dve, TXT_GROUPS[0], base + 1)
            joint_q(1)
            joint_moments(2)
            norm_apply(dve, TXT_GROUPS[1], base + 2)
            norm_apply(dve, TXT_GROUPS[2], base + 3)
            for what, j in JOINT_ORDER:
                if what == "QKU" and j >= NI:
                    joint_q(j)
                if what != "V":
                    continue
                dve.wait_ge(v_psum, LAYERS * 4 + j + 1)
                nc.vector.tensor_tensor(
                    v_joint[0:K_JOINT, 4 * j:4 * j + 4, :, 0:HD],
                    ps[0:K_JOINT, 1 + j, :].rearrange("p (b h w) -> p b h w", b=4, w=HD),
                    jrow[0:K_JOINT, JR_BV:JR_BV + D].rearrange("p (h w) -> p h w", w=HD).unsqueeze(1)
                    .broadcast_to([K_JOINT, 4, NH, HD]), ALU.add).then_inc(v_sb, 1)

            out_base = base + NG

            def gate_context(g):
                s = group_cols(OUT_GROUPS[g])
                dve.wait_ge(tanh_ctx, g + 1)
                dve.wait_ge(ctx_u, g + 1)
                nc.vector.scalar_tensor_tensor(uT[:, s], hT[:, s], 1.0, uT[:, s], ALU.add, ALU.mult
                                               ).then_inc(gated_sb, 1)

            def join(t0, nt, src):
                return nc.vector.scalar_tensor_tensor(x_tok[:, t0:t0 + nt, :], src, 0.5, x_tok[:, t0:t0 + nt, :],
                                                      ALU.mult, ALU.add)

            def joint_beside(i):
                if i in ALL_SPARE:
                    k = list(ALL_SPARE).index(i)
                    t0, nt, _ = ALL_SPARE[i]
                    if k == 0:
                        dve.wait_ge(bias_added, LAYERS * (1 + NG) + 1)
                    dve.wait_ge(wo_psum, LAYERS * TXT_ADDS + k + 1)
                    join(t0, nt, bank_cols(6, (t0, nt), SPARE_COL)).then_inc(x_joint, 1)
                    dve.wait_ge(x_joint, k + 1)
                    last = tile_stats(t0, nt)
                    if i in (23, 25, 30, 32):
                        last.then_inc(ln_stats, 1)
                if i in (21, 23, 28, 29):
                    gate_context((21, 23, 28, 29).index(i))
                for k, step in enumerate((26, 27, 31, 32)):
                    if i == step:
                        norm_moments(dve, OUT_GROUPS[k], out_base + k + 1)
                for k, step in enumerate((29, 31, 33, 33)):
                    if i == step:
                        norm_apply(dve, OUT_GROUPS[k], out_base + k + 1)

            attend_dve(dve, joint_units(), lambda k: LAYERS * B + k, joint_beside)
            gate_context(4)
            gate_context(5)
            for g in (4, 5):
                group = t0, nt = OUT_GROUPS[g]
                k = len(ALL_SPARE) + g - 3
                dve.wait_ge(wo_psum, LAYERS * TXT_ADDS + k)
                join(t0, nt, bank_cols(g, group)).then_inc(x_joint, 1)
                dve.wait_ge(x_joint, k)
                tile_stats(t0, nt).then_inc(ln_stats, 1)
                norm_moments(dve, group, out_base + g + 1)
            for g in (4, 5):
                norm_apply(dve, OUT_GROUPS[g], out_base + g + 1)

            def routing(part, stage):
                r0, r1 = ROUTE_PARTS[part]
                m, nt = slice(r0, r1), r1 - r0
                if stage == 0:
                    dve.wait_ge(aff_sb, part + 1)
                    link(nc.vector.tensor_tensor(route[:, m], aff[:, m], row_of(jrow[:, JR_EB:JR_EB + E], nt), ALU.add))
                    for r in range(r0, r1):
                        last = nc.vector.max(top8[:, r, :], route[:, r, :])
                    link(last)
                if stage == 1:
                    for r in range(r0, r1):
                        last = nc.vector.max_index(place[:, r, :], top8[:, r, :], route[:, r, :])
                    link(last)
                if stage == 2:
                    for k in range(3):
                        last = nc.vector.tensor_tensor(
                            (route, route2, route3)[k][:, m], row_of(const[:, C_IOTA:C_IOTA + E], nt),
                            place[:, m, k:k + 1].broadcast_to([P, nt, E]), ALU.is_equal)
                    link(last)
                if stage == 3:
                    link(nc.vector.tensor_tensor(route[:, m], route[:, m], route2[:, m], ALU.add))
                    link(nc.vector.tensor_tensor(route[:, m], route[:, m], route3[:, m], ALU.add))
                if stage == 4:
                    link(nc.vector.tensor_tensor(aff[:, m], aff[:, m], route[:, m], ALU.mult))
                    link(nc.vector.tensor_reduce(gsum[:, m], aff[:, m], AX.X, ALU.add))
                if stage == 5:
                    link(nc.vector.tensor_scalar(gsum[:, m], gsum[:, m], 1e-9, None, ALU.add))
                    link(nc.vector.reciprocal(gsum[:, m], gsum[:, m]))
                if stage == 6:
                    link(nc.vector.tensor_tensor(aff[:, m], aff[:, m],
                                                 gsum[:, m].unsqueeze(2).broadcast_to([P, nt, E]), ALU.mult))
                if stage == 7:
                    link(nc.vector.tensor_copy(gates[:, m, 0:E], aff[:, m]))
                    nc.vector.tensor_tensor(gates[:, m, E:2 * E], aff[:, m], gates[:, m, 0:E].bitcast(F32),
                                            ALU.subtract).then_inc(gates_sb, 1)

            for stage in range(8):
                routing(0, stage)
            nc.vector.memset(wait_carrier[:], 0.0).then_inc(final_sb, 1)

            def expert_dve(c, r):
                if taken(c, r):
                    dve.wait_ge(up_psum, c * ROUND + (r + 1))
                    dve.wait_ge(silu_sb, c * ROUND + (r + 1))
                    shared = r % (E + 1) == E
                    if shared:
                        dve.wait_ge(hglo_sb, c * ROUND + (r - 1))
                    nc.vector.tensor_tensor((hg_t if shared else su_t)[:, r % 2, :], silu_t[:, r % 2, :],
                                            ps[:, 2 + r % 2, 0:CHUNK], ALU.mult).then_inc(su_sb, 1)
                    if shared:
                        dve.wait_ge(su_sb, c * ROUND + (r + 1))
                        nc.vector.memset(wait_carrier[:], 0.0).then_inc(hg_sb, 1)
                    else:
                        dve.wait_ge(gb_psum, c * (2 * E) + (r - r // (E + 1) + 1))
                        dve.wait_ge(su_sb, c * ROUND + (r + 1))
                        if r >= 2:
                            dve.wait_ge(hglo_sb, c * ROUND + (r - 1))
                        nc.vector.tensor_tensor(hg_t[:, r % 2, :], su_t[:, r % 2, :],
                                                ps[:, 4 + r % 2, 0:CHUNK], ALU.mult).then_inc(hg_sb, 1)
                if isinstance(c, int) and c == 0 and 1 <= r <= 8:
                    routing(1, r - 1)
                if r >= 4 and (r - 4) % (E + 1) == E:
                    k = (r - 4) // (E + 1)
                    dve.wait_ge(oT_psum, c * 2 + (k + 1))
                    t0 = c * (2 * CHUNK_TILES) + k * CHUNK_TILES
                    xs = x_tok[:, slice(t0, t0 + CHUNK_TILES) if isinstance(c, int) else bass.ds(t0, CHUNK_TILES), :]
                    nc.vector.tensor_tensor(
                        xs, xs, ps[:, 6 + k, 0:CHUNK].rearrange("p (t d) -> p t d", t=CHUNK_TILES),
                        ALU.add).then_inc(final_sb, 1)

            expert_steps(dve, expert_dve)


_NAMES = ["const", "tokens", "tokens_end", "noise_cols", "noise_rows", "tok_w", "tok_sw", "tok_w3", "tok_b", "patches",
          "pad_row", "pad_col", "pos", "item_emb", "w_qkv", "w_o", "w_1", "w_2", "vec", "row", "jw", "jvec",
          "jrow", "w_exp", "w_gate"]


def constants():
    c = np.zeros((P, C_ALL), np.float32)
    c[:, C_ID:C_ID + P] = np.eye(P)
    i, j = np.arange(S_TXT)[:, None], np.arange(S_TXT)[None, :]
    c[:S_TXT, C_CAUSAL:C_CAUSAL + S_TXT] = np.where(j > i, FAR, 0.0)
    i, j = S_IMG + np.arange(S_TXT)[:, None], np.arange(K_JOINT)[None, :]
    c[:S_TXT, C_JOINT:C_JOINT + K_JOINT] = np.where((j <= i) & (i + j <= S_ALL), 0.0, FAR)
    c[:S_TXT, C_MASKL:C_MASKL + S_TXT] = np.eye(S_TXT)
    c[PAD_ROW, C_MASKL:C_MASKL + S_TXT] = 1.0
    c[np.arange(P), C_HEAD + np.arange(P) // HD] = 1.0
    pos = np.arange(S_IMG, dtype=np.float32)[:, None]
    div = np.exp(np.arange(0, D, 2, dtype=np.float32) * np.float32(-np.log(10000.0) / D))
    ang = (pos * div).astype(np.float32)
    pe = np.stack([np.sin(ang), np.cos(ang)], axis=-1).reshape(S_IMG, D)
    c[:, C_IOTA:C_IOTA + E] = np.arange(E)
    c[:, C_POS:C_POS + D] = np.tile(pe, (P // S_IMG, 1))
    return c


def kernel(**inputs):
    import concourse.bacc as _bacc
    from concourse.bass_utils import run_bass_kernel_spmd as _run

    f = {k: np.asarray(v) for k, v in inputs.items()}

    def t(name):
        return f[name]

    def halves(w):
        return w.T.reshape(2, P, D).transpose(1, 0, 2)

    def col(name, n=1):
        return t(name).reshape(n, P).T

    x = t("x").reshape(B, 8, 16, 8, 16).transpose(2, 4, 0, 1, 3).reshape(2, P, T0).transpose(1, 0, 2)
    tokens = t("x_txt").reshape(TXT_TOKENS)
    layers = range(LAYERS)
    arrays = {
        "const": constants(),
        "tokens": tokens[:TXT_TOKENS - LAST_ROWS].reshape(TXT_TILES - 1, P).T,
        "tokens_end": tokens[TXT_TOKENS - LAST_ROWS:, None],
        "noise_cols": np.concatenate([col("L0_tok_eps_in1", 2), col("L0_tok_eps_in2", 2),
                                      col("L0_tok_eps_out1"), col("L0_tok_eps_out2")], axis=1),
        "noise_rows": np.concatenate([t("L0_tok_eps_out1"), t("L0_tok_eps_out2")])[None, :],
        "tok_w": np.stack([halves(t("L0_tok_W1_w")), halves(t("L0_tok_W2_w"))], axis=1).reshape(P, 4 * D),
        "tok_sw": np.stack([halves(t("L0_tok_W1_sw")), halves(t("L0_tok_W2_sw"))], axis=1).reshape(P, 4 * D),
        "tok_w3": t("L0_tok_W3_w").T,
        "tok_b": np.stack([t("L0_tok_W1_b"), t("L0_tok_W1_sb"), t("L0_tok_W2_b"), t("L0_tok_W2_sb")], axis=1),
        "patches": x.reshape(P, 2 * T0),
        "pad_row": t("mask_BS_f1_0").reshape(1, TXT_TOKENS),
        "pad_col": t("mask_BS_f1_0").T,
        "pos": np.concatenate([t("L0_txt_pos_emb")[:S_TXT]] * B, axis=0),
        "item_emb": t("L0_txt_item_emb"),
        "w_qkv": np.concatenate([t("L0_txt_Wq"), t("L0_txt_Wk"), t("L0_txt_Wv")], axis=2).reshape(LAYERS * P, 3 * D),
        "w_o": t("L0_txt_Wo").reshape(LAYERS * P, D),
        "w_1": t("L0_txt_W1").reshape(LAYERS * P, FF * D),
        "w_2": t("L0_txt_W2").reshape(LAYERS, FF, P, D).transpose(0, 2, 1, 3).reshape(LAYERS * P, FF * D),
        "vec": np.concatenate([
            np.concatenate([np.stack([t("L0_txt_" + n)[l] for n in ("ln1_g", "ln1_b", "bq", "bk", "ln2_g", "ln2_b")],
                                     axis=1), t("L0_txt_b1")[l].reshape(FF, P).T], axis=1) for l in layers], axis=0),
        "row": np.concatenate([t("L0_txt_bv"), t("L0_txt_bo"), t("L0_txt_b2")], axis=1),
        "jw": np.concatenate([t("L0_attn_w_qkv").T, t("L0_attn_w_u").T, t("L0_attn_w_out").T], axis=1),
        "jvec": np.stack([t("L0_attn_b_qkv")[0:D], t("L0_attn_b_qkv")[D:2 * D], t("L0_attn_b_u")], axis=1),
        "jrow": np.concatenate([t("L0_attn_b_qkv")[2 * D:], t("L0_attn_b_out"), t("L0_tok_W3_b"), t("L0_txt_lnf_g"),
                                t("L0_txt_lnf_b"), t("L0_ffn_expert_bias")])[None, :],
        "w_exp": np.concatenate([
            np.concatenate([t("L0_ffn_expert_gate_up").transpose(0, 2, 1), t("L0_ffn_expert_down").transpose(0, 2, 1)],
                           axis=2),
            np.concatenate([t("L0_ffn_shared_gate_up").T, t("L0_ffn_shared_down").T], axis=1)[None]],
            axis=0).reshape((E + 1) * P, EW),
        "w_gate": t("L0_ffn_gate_w").T,
    }
    nc = _bacc.Bacc("TRN2", target_bir_lowering=False, num_devices=1)
    given, aps = {}, {}
    for name in _NAMES:
        v = np.ascontiguousarray(arrays[name])
        given["in_" + name] = v
        aps[name] = nc.dram_tensor("in_" + name, v.shape, mybir.dt.from_np(v.dtype), kind="ExternalInput").ap()
    out = nc.dram_tensor("out_tokens", (COLS, D), F32, kind="ExternalOutput").ap()
    build(nc, aps, out)
    got = _run(nc, [given], core_ids=[0]).results[0]["out_tokens"]
    return np.concatenate([got[:T0].reshape(B, S_IMG, D), got[T0:T0 + TXT_TOKENS].reshape(B, S_TXT, D)], axis=1)
```
